# Optimizing a Trainium2 kernel written in Bass

```python
import numpy as np
import jax
import jax.numpy as jnp

def _softmax(x, axis=-1):
    return jax.nn.softmax(x, axis=axis)

def _gelu(x):
    return jax.nn.gelu(x, approximate=True)

def _silu(x):
    return jax.nn.silu(x)

def _sigmoid(x):
    return jax.nn.sigmoid(x)

def _layernorm(x, axis=-1, eps=1e-05):
    m = jnp.mean(x, axis=axis, keepdims=True)
    v = jnp.var(x, axis=axis, keepdims=True)
    return (x - m) / jnp.sqrt(v + eps)

def _scatter_add(tgt, idx, src, axis=0):
    return tgt.at[idx].add(src)

def _segment_sum(src, seg, n):
    return jax.ops.segment_sum(src, seg, n)
kernel_name = 'mk_gnn_preln_d2_gnn_r64_a4eb6a'

def setup_inputs(seed: int=0):
    np.random.seed(seed)
    _w = jnp.asarray

    def _rec_inputs():
        import jax
        import jax.numpy as jnp
        _gk = jax.random.key(seed)
        x = -0.0005121 + 1.001 * jax.random.normal(jax.random.fold_in(_gk, 1), (100000, 64), jnp.float32)
        src = jax.random.randint(jax.random.fold_in(_gk, 2), (25000,), 0, 100000, jnp.int32)
        dst = jax.random.randint(jax.random.fold_in(_gk, 3), (25000,), 0, 100000, jnp.int32)
        _o = jnp.argsort(dst, stable=True)
        src = src[_o]
        dst = dst[_o]
        edge_attr_32 = 0.000216709 + 1.00012 * jax.random.normal(jax.random.fold_in(_gk, 12), (25000, 32), jnp.float32)
        edge_attr_64 = -9.77346e-05 + 0.999888 * jax.random.normal(jax.random.fold_in(_gk, 13), (25000, 64), jnp.float32)
        edge_weight = jax.random.uniform(jax.random.fold_in(_gk, 15), (25000,), jnp.float32, 0.0, 1.1)
        node_vec = jax.random.uniform(jax.random.fold_in(_gk, 16), (100000,), jnp.float32, 0.0, 1.09988)
        return (x, src, dst, edge_attr_32, edge_attr_64, edge_weight, node_vec)
    x, src, dst, edge_attr_32, edge_attr_64, edge_weight, node_vec = _rec_inputs()

    def _L0_gnn_setup():
        import jax, jax.numpy as jnp
        import numpy as np
        N_NODES = 50000
        N_EDGES = 12500
        D_NODE = 64
        D_EDGE = 32
        D_HID = 128

        def _mlp(x, W1, b1, W2, b2):
            return jax.nn.relu(x @ W1 + b1) @ W2 + b2
        key = jax.random.key(seed)
        ks = jax.random.split(key, 12)
        inp = {'nodes': jax.random.normal(ks[0], (N_NODES, D_NODE), dtype=jnp.float32), 'row': jax.random.randint(ks[1], (N_EDGES,), 0, N_NODES, dtype=jnp.int32), 'col': jax.random.randint(ks[2], (N_EDGES,), 0, N_NODES, dtype=jnp.int32), 'edge_features': jax.random.normal(ks[3], (N_EDGES, D_EDGE), dtype=jnp.float32)}
        d_in_msg = 2 * D_NODE + D_EDGE
        inp['mW1'] = jax.random.normal(ks[4], (d_in_msg, D_HID), dtype=jnp.float32) / np.sqrt(d_in_msg)
        inp['mb1'] = jnp.zeros((D_HID,), dtype=jnp.float32)
        inp['mW2'] = jax.random.normal(ks[5], (D_HID, D_NODE), dtype=jnp.float32) / np.sqrt(D_HID)
        inp['mb2'] = jnp.zeros((D_NODE,), dtype=jnp.float32)
        d_in_upd = 2 * D_NODE
        inp['uW1'] = jax.random.normal(ks[6], (d_in_upd, D_HID), dtype=jnp.float32) / np.sqrt(d_in_upd)
        inp['ub1'] = jnp.zeros((D_HID,), dtype=jnp.float32)
        inp['uW2'] = jax.random.normal(ks[7], (D_HID, D_NODE), dtype=jnp.float32) / np.sqrt(D_HID)
        inp['ub2'] = jnp.zeros((D_NODE,), dtype=jnp.float32)
        return inp
    _L0_gnn_all = _L0_gnn_setup()
    _L0_gnn_in = {k: v for k, v in _L0_gnn_all.items() if k in ('mW1', 'mb1', 'mW2', 'mb2', 'uW1', 'ub1', 'uW2', 'ub2')}
    del _L0_gnn_all

    def _L1_gnn_setup():
        import jax, jax.numpy as jnp
        import numpy as np
        EPS = 1e-05

        def weighted_bn(x, w, gamma, beta):
            wn = w / jnp.sum(w)
            mean = jnp.einsum('r,rd->d', wn, x)
            var = jnp.einsum('r,rd->d', wn, (x - mean) ** 2)
            return gamma * (x - mean) * jax.lax.rsqrt(var + EPS) + beta
        key = jax.random.key(seed)
        ks = jax.random.split(key, 8)
        N_ATOMS, N_EDGES = (50000, 12500)
        AF, BF = (64, 64)
        D_IN, D_OUT = (2 * AF + BF, 2 * AF)
        atom_in_fea = jax.random.normal(ks[0], (N_ATOMS, AF), jnp.float32)
        nbr_fea = jax.random.normal(ks[1], (N_EDGES, BF), jnp.float32)
        nbr_fea_idx = jax.random.randint(ks[2], (N_EDGES, 2), 0, N_ATOMS, jnp.int64)
        weights = jax.random.uniform(ks[3], (N_ATOMS,), jnp.float32) + 0.1
        edge_weights = jax.random.uniform(ks[4], (N_EDGES,), jnp.float32) + 0.1
        W = jax.random.normal(ks[5], (D_IN, D_OUT), jnp.float32) * (1.0 / np.sqrt(D_IN))
        b = jnp.zeros((D_OUT,), jnp.float32)
        g1 = jnp.ones((D_OUT,), jnp.float32)
        b1 = jnp.zeros((D_OUT,), jnp.float32)
        g2 = jnp.ones((AF,), jnp.float32)
        b2 = jnp.zeros((AF,), jnp.float32)
        return {'atom_in_fea': atom_in_fea, 'nbr_fea': nbr_fea, 'nbr_fea_idx': nbr_fea_idx, 'weights': weights, 'edge_weights': edge_weights, 'W': W, 'b': b, 'g1': g1, 'b1': b1, 'g2': g2, 'b2': b2}
    _L1_gnn_all = _L1_gnn_setup()
    _L1_gnn_in = {k: v for k, v in _L1_gnn_all.items() if k in ('W', 'b', 'g1', 'b1', 'g2', 'b2')}
    del _L1_gnn_all
    return {'x': x, 'src': src, 'dst': dst, 'edge_attr_32': edge_attr_32, 'edge_attr_64': edge_attr_64, 'edge_weight': edge_weight, 'node_vec': node_vec, 'L0_gnn_mW1': _L0_gnn_in['mW1'], 'L0_gnn_mb1': _L0_gnn_in['mb1'], 'L0_gnn_mW2': _L0_gnn_in['mW2'], 'L0_gnn_mb2': _L0_gnn_in['mb2'], 'L0_gnn_uW1': _L0_gnn_in['uW1'], 'L0_gnn_ub1': _L0_gnn_in['ub1'], 'L0_gnn_uW2': _L0_gnn_in['uW2'], 'L0_gnn_ub2': _L0_gnn_in['ub2'], 'L1_gnn_W': _L1_gnn_in['W'], 'L1_gnn_b': _L1_gnn_in['b'], 'L1_gnn_g1': _L1_gnn_in['g1'], 'L1_gnn_b1': _L1_gnn_in['b1'], 'L1_gnn_g2': _L1_gnn_in['g2'], 'L1_gnn_b2': _L1_gnn_in['b2']}

def reference(x, src, dst, edge_attr_32, edge_attr_64, edge_weight, node_vec, L0_gnn_mW1, L0_gnn_mb1, L0_gnn_mW2, L0_gnn_mb2, L0_gnn_uW1, L0_gnn_ub1, L0_gnn_uW2, L0_gnn_ub2, L1_gnn_W, L1_gnn_b, L1_gnn_g1, L1_gnn_b1, L1_gnn_g2, L1_gnn_b2):
    import jax
    import jax.numpy as jnp

    def _L0_gnn_ref(nodes, row, col, edge_features, mW1, mb1, mW2, mb2, uW1, ub1, uW2, ub2):
        import jax, jax.numpy as jnp
        import numpy as np
        N_NODES = 50000
        N_EDGES = 12500
        D_NODE = 64
        D_EDGE = 32
        D_HID = 128

        def _mlp(x, W1, b1, W2, b2):
            return jax.nn.relu(x @ W1 + b1) @ W2 + b2
        msg_in = jnp.concatenate([nodes[row], nodes[col], edge_features], axis=-1)
        messages = _mlp(msg_in, mW1, mb1, mW2, mb2)
        aggregated = jax.ops.segment_sum(messages, col, num_segments=nodes.shape[0])
        upd_in = jnp.concatenate([nodes, aggregated], axis=-1)
        return _mlp(upd_in, uW1, ub1, uW2, ub2)

    def _L1_gnn_ref(atom_in_fea, nbr_fea, nbr_fea_idx, weights, edge_weights, W, b, g1, b1, g2, b2):
        import jax, jax.numpy as jnp
        import numpy as np
        EPS = 1e-05

        def weighted_bn(x, w, gamma, beta):
            wn = w / jnp.sum(w)
            mean = jnp.einsum('r,rd->d', wn, x)
            var = jnp.einsum('r,rd->d', wn, (x - mean) ** 2)
            return gamma * (x - mean) * jax.lax.rsqrt(var + EPS) + beta
        N_atoms, AF = atom_in_fea.shape
        E = nbr_fea_idx.shape[0]
        atom_nbr_fea = atom_in_fea[nbr_fea_idx, :].reshape(E, 2 * AF)
        total = jnp.concatenate([atom_nbr_fea, nbr_fea], axis=-1)
        gated = weighted_bn(total @ W + b, edge_weights, g1, b1)
        nbr_filter, nbr_core = jnp.split(gated, 2, axis=-1)
        msg = jax.nn.sigmoid(nbr_filter) * jax.nn.softplus(nbr_core)
        nbr_sumed = jnp.zeros((N_atoms, AF), atom_in_fea.dtype).at[nbr_fea_idx[:, 0]].add(msg)
        nbr_sumed = weighted_bn(nbr_sumed, weights, g2, b2)
        return jax.nn.softplus(atom_in_fea + nbr_sumed)
    edge_index_t = jnp.stack([src, dst], axis=1)
    h = jnp.maximum(_layernorm(x, axis=-1), 0.0)
    x = x + _L0_gnn_ref(h, src, dst, edge_attr_32, L0_gnn_mW1, L0_gnn_mb1, L0_gnn_mW2, L0_gnn_mb2, L0_gnn_uW1, L0_gnn_ub1, L0_gnn_uW2, L0_gnn_ub2)
    h = jnp.maximum(_layernorm(x, axis=-1), 0.0)
    x = x + _L1_gnn_ref(h, edge_attr_64, edge_index_t, node_vec, edge_weight, L1_gnn_W, L1_gnn_b, L1_gnn_g1, L1_gnn_b1, L1_gnn_g2, L1_gnn_b2)
    return x

_drawn_inputs = setup_inputs


def setup_inputs(seed=0):
    import zlib

    import numpy as np

    out = dict(_drawn_inputs(seed))
    spreads = {'L0_gnn_mb1': (0.0, 0.585),
     'L0_gnn_mb2': (0.0, 0.375),
     'L0_gnn_ub1': (0.0, 0.1),
     'L0_gnn_ub2': (0.0, 0.1),
     'L1_gnn_b': (0.0, 0.8),
     'L1_gnn_g1': (1.0, 0.2),
     'L1_gnn_b1': (0.0, 0.8),
     'L1_gnn_g2': (1.0, 0.2),
     'L1_gnn_b2': (0.0, 0.1)}
    factors = {'edge_weight': 8.0, 'node_vec': 8.0}
    for name, (base, spread) in spreads.items():
        noise = np.random.default_rng([zlib.crc32(name.encode()), seed]).standard_normal(out[name].shape)
        drawn = base * np.exp(spread * noise) if base else spread * noise
        out[name] = jnp.asarray(drawn.astype(out[name].dtype))
    for name, factor in factors.items():
        out[name] = (out[name] * factor).astype(out[name].dtype)
    return out
```

```python
from contextlib import ExitStack

import concourse.bass as bass
from concourse import mybir

F32 = mybir.dt.float32
I32 = mybir.dt.int32
ALU = mybir.AluOpType
ACT = mybir.ActivationFunctionType
X = mybir.AxisListType.X

P = 128
D = 64
H = 128
N = 100000
E = 25000
J = 16
CHUNK = P * J
CHUNKS = -(-N // CHUNK)
NP = CHUNKS * CHUNK
GT = 4
GROUP = GT * P
GROUPS = -(-E // GROUP)
EP = GROUPS * GROUP
TILES = GROUPS * GT
DUMP = NP
ROWS = NP + GROUP + (EP - E)
EPS = 1e-5
assert GROUPS % 2 == 1 and CHUNKS % 2 == 1


def build(nc, x, gat, key_cols, key_src, key_dst, ea32_t, ea64_t, edge_w, edge_w_cols, node_w, weights, out):
    agg = nc.dram_tensor("agg_table", [ROWS, D], F32, kind="Internal").ap()
    ctab = nc.dram_tensor("centred_table", [NP, D], F32, kind="Internal").ap()
    nsum = nc.dram_tensor("nsum_table", [ROWS, D], F32, kind="Internal").ap()
    chunk_rows = lambda t, g: t[bass.ds(g * CHUNK, CHUNK), :].rearrange("(p j) d -> p j d", j=J)

    ctx = ExitStack()
    with ctx:
        def sb(name, shape, dt=F32):
            return ctx.enter_context(nc.sbuf_tensor(name, shape, dt))

        def sem(name):
            return ctx.enter_context(nc.semaphore(name))

        bank = [ctx.enter_context(nc.psum_tensor(f"bank{i}", [P, 512], F32)) for i in range(8)]

        ident = sb("ident", [P, P])
        ones = sb("ones", [P, P])
        before = sb("before", [P, GROUP])
        dump_rows = sb("dump_rows", [P, GT], I32)
        dump_f = sb("dump_f", [P, GT])
        eps_col = sb("eps_col", [P, 1])
        zero_col = sb("zero_col", [P, 1])
        w_msg1 = sb("w_msg1", [P, H])
        w_msg1e = sb("w_msg1e", [32, H])
        b_msg1 = sb("b_msg1", [P, 1])
        w_msg2 = sb("w_msg2", [P, D])
        b_msg2 = sb("b_msg2", [P, D])
        w_upd1 = sb("w_upd1", [P, H])
        b_upd1 = sb("b_upd1", [P, 1])
        w_upd2 = sb("w_upd2", [P, D + 1])
        b_upd2 = sb("b_upd2", [P, D + 1])
        w_gate = sb("w_gate", [P, H])
        w_gatee = sb("w_gatee", [D, H])
        b_gate = sb("b_gate", [P, 1])
        g1c = sb("g1c", [P, 1])
        b1c = sb("b1c", [P, 1])
        g2r = sb("g2r", [P, D])
        b2r = sb("b2r", [P, D])
        ew = sb("ew", [P, TILES])
        nw = sb("nw", [P, CHUNKS * J])
        wsum = sb("wsum", [P, 2])
        wsum_inv = sb("wsum_inv", [P, 2])
        m1 = sb("m1", [P, CHUNKS * J])
        r1 = sb("r1", [P, CHUNKS * J])
        s1 = sb("s1", [P, 2])
        s2 = sb("s2", [P, 2])
        tbuf = sb("tbuf", [P, 2, GROUP])
        tmp = sb("tmp", [P, 8])
        A1 = sb("A1", [P, 1])
        B1 = sb("B1", [P, 1])
        A2 = sb("A2", [P, D])
        B2 = sb("B2", [P, D])
        row_tmp = sb("row_tmp", [P, 4, D])
        kcols = sb("kcols", [P, 2, TILES], I32)
        kcolf = sb("kcolf", [P, 2, TILES])
        gidx = sb("gidx", [P, 2, 2 * GT], I32)
        krow = sb("krow", [P, 2, GROUP], I32)
        eat = sb("eat", [D, 2, GROUP])
        ewr = sb("ewr", [P, 2, GROUP])
        gx = sb("gx", [P, 2, 2 * GT, D])
        gc = sb("gc", [P, 2 * GT, D])
        gsq = sb("gsq", [P, 2 * GT, D])
        gh = sb("gh", [P, 2 * GT, D])
        gst = sb("gst", [P, 4, 2 * GT])
        ght = sb("ght", [P, GROUP])
        ghid = sb("ghid", [P, GROUP])
        gmsg = sb("gmsg", [P, GT, D])
        gtot = sb("gtot", [P, 2, GT, D])
        same = sb("same", [P, GT, GROUP])
        same_out = sb("same_out", [P, GROUP])
        cnt = sb("cnt", [P, 2, GT])
        sidx = sb("sidx", [P, 2, GT], I32)
        big = sb("big", [P, EP])

        def area(i, shape=(J, D)):
            n = shape[0] * shape[1]
            return big[:, i * J * D:i * J * D + n].rearrange("p (a b) -> p a b", b=shape[1])

        zeros = big[:, 0:4 * J * D]

        chain = [sem("dve_chain"), 0]

        s_const = sem("s_const")
        s_cpool = sem("s_cpool")
        s_zero = sem("s_zero")
        s_zeroed = sem("s_zeroed")
        s_wdve = sem("s_wdve")
        s_wpe = sem("s_wpe")
        NLOADS = 18
        with nc.Block() as block:
            @block.sync
            def _(sp):
                W = weights
                loads = [
                    (w_msg1[:, :], W["mW1"][0:P, :]), (w_msg1e[:, :], W["mW1"][P:P + 32, :]),
                    (b_msg1[:, :], W["mb1"].rearrange("(p a) -> p a", a=1)), (w_msg2[:, :], W["mW2"]),
                    (b_msg2[:, :], W["mb2"].partition_broadcast(P)), (w_upd1[:, :], W["uW1"]),
                    (b_upd1[:, :], W["ub1"].rearrange("(p a) -> p a", a=1)), (w_upd2[:, 0:D], W["uW2"]),
                    (b_upd2[:, 0:D], W["ub2"].partition_broadcast(P)), (w_gate[:, :], W["W"][0:P, :]),
                    (w_gatee[:, :], W["W"][P:P + D, :]), (b_gate[:, :], W["b"].rearrange("(p a) -> p a", a=1)),
                    (g1c[:, :], W["g1"].rearrange("(p a) -> p a", a=1)),
                    (b1c[:, :], W["b1"].rearrange("(p a) -> p a", a=1)),
                    (g2r[:, :], W["g2"].partition_broadcast(P)), (b2r[:, :], W["b2"].partition_broadcast(P)),
                    (ew[:, :], edge_w_cols), (nw[:, :], node_w),
                ]
                assert len(loads) == NLOADS
                for dst, src in loads:
                    sp.dma_start(dst, src).then_inc(s_const, 16)
                sp.dma_start(kcols[:, :, :], key_cols).then_inc(s_const, 16)
                sp.wait_ge(s_zero, 1)
                for table in (agg, nsum):
                    flat = table.rearrange("r d -> (r d)")
                    step = P * 4 * J * D
                    at = 0
                    while at < ROWS * D:
                        n = min(step, ROWS * D - at)
                        sp.dma_start(flat[at:at + n].rearrange("(p f) -> p f", p=P),
                                     zeros[:, 0:n // P]).then_inc(s_zeroed, 16)
                        at += n
                sp.wait_ge(s_zeroed, 16 * 2 * -(-ROWS * D // step))

            @block.gpsimd
            def _(pool):
                nc.gpsimd.memset(ident[:, :], 0.0).then_inc(s_cpool, 1)
                nc.gpsimd.memset(before[:, :], 1.0).then_inc(s_cpool, 1)
                nc.gpsimd.memset(ones[:, :], 1.0).then_inc(s_cpool, 1)
                pool.wait_ge(s_cpool, 3)
                nc.gpsimd.affine_select(out=ident[:, :], in_=ident[:, :], compare_op=ALU.not_equal, fill=1.0,
                                        base=0, pattern=[[-1, P]], channel_multiplier=1).then_inc(s_cpool, 1)
                nc.gpsimd.affine_select(out=before[:, :], in_=before[:, :], compare_op=ALU.is_gt, fill=0.0,
                                        base=GROUP - P, pattern=[[-1, GROUP]],
                                        channel_multiplier=1).then_inc(s_cpool, 1)
                nc.gpsimd.iota(dump_rows[:, :], pattern=[[P, GT]], base=DUMP,
                               channel_multiplier=1).then_inc(s_cpool, 1)

            @block.vector
            def _(dve):
                def link(ins):
                    chain[1] += 1
                    ins.then_inc(chain[0], 1)
                    dve.wait_ge(chain[0], chain[1])

                nc.vector.memset(zeros, 0.0).then_inc(s_zero, 1)
                nc.vector.memset(eps_col[:, :], EPS)
                nc.vector.memset(zero_col[:, :], 0.0)
                nc.vector.memset(s1[:, :], 0.0)
                nc.vector.memset(s2[:, :], 0.0)
                dve.wait_ge(s_cpool, 6)
                nc.vector.tensor_copy(dump_f[:, :], dump_rows[:, :])
                dve.wait_ge(s_const, 16 * (NLOADS + 1))
                nc.vector.tensor_copy(kcolf[:, :, :], kcols[:, :, :])
                for w in (w_upd2, b_upd2):
                    link(nc.vector.reduce_sum(tmp[:, 0:1], w[:, 0:D], X))
                    link(nc.vector.tensor_scalar(w[:, D:D + 1], tmp[:, 0:1], 1.0 / D, None, ALU.mult))
                    link(nc.vector.tensor_scalar(w[:, 0:D], w[:, 0:D], w[:, D:D + 1], None, ALU.subtract))
                nc.vector.reduce_sum(tmp[:, 1:2], ew[:, :], X).then_inc(s_wdve, 1)
                nc.vector.reduce_sum(tmp[:, 2:3], nw[:, :], X).then_inc(s_wdve, 1)
                dve.wait_ge(s_wpe, 1)
                link(nc.vector.tensor_copy(wsum[:, :], bank[0][:, 0:2]))
                link(nc.vector.reciprocal(wsum_inv[:, :], wsum[:, :]))

            @block.tensor
            def _(pe):
                pe.wait_ge(s_cpool, 6)
                pe.wait_ge(s_wdve, 2)
                nc.tensor.matmul(bank[0][:, 0:2], ones[:, :], tmp[:, 1:3], start=True, stop=True).then_inc(s_wpe, 1)

        s_step = sem("s_step")
        s_gi = [sem(f"s_gi{b}") for b in range(2)]
        s_gx = [sem(f"s_gx{b}") for b in range(2)]
        s_used = sem("s_used")
        s_idxused = sem("s_idxused")
        s_sq = sem("s_sq")
        s_c = sem("s_c")
        s_ss = sem("s_ss")
        s_std = sem("s_std")
        s_h = sem("s_h")
        s_tp = sem("s_tp")
        s_ht = sem("s_ht")
        s_m1 = sem("s_m1")
        s_hid = sem("s_hid")
        s_m2 = sem("s_m2")
        s_msg = sem("s_msg")
        s_same = sem("s_same")
        s_sidx = sem("s_sidx")
        s_m3 = sem("s_m3")
        s_tot = sem("s_tot")
        s_sc = sem("s_sc")
        with nc.Block() as block:
            @block.sync
            def _(sp):
                def load(u, b, g):
                    if not isinstance(g, int) or g >= 2:
                        sp.wait_ge(s_gx[b], 128 * u)
                        sp.wait_ge(s_same, g - 1)
                        sp.wait_ge(s_m1, g - 1)
                    sp.dma_start(gidx[:, b, :], gat[bass.ds(g, 1), :, :].rearrange("g p c -> (g p) c")).then_inc(s_gi[b], 16)
                    sp.dma_start(krow[:, b, :], key_dst[bass.ds(g * GROUP, GROUP)].partition_broadcast(P)).then_inc(s_gi[b], 16)
                    sp.dma_start(eat[0:32, b, :], ea32_t[:, bass.ds(g * GROUP, GROUP)]).then_inc(s_gi[b], 16)

                load(0, 0, 0)
                load(0, 1, 1)
                with sp.Fori(1, GROUPS // 2) as u:
                    for b in range(2):
                        load(u, b, u * 2 + b)
                load(GROUPS // 2, 0, GROUPS - 1)

            @block.gpsimd
            def _(pool):
                def gather(u, b, g):
                    pool.wait_ge(s_gi[b], 48 * (u + 1))
                    if not isinstance(g, int) or g >= 2:
                        pool.wait_ge(s_c, g - 1)
                    pool.sem_inc(s_step, 1)
                    for k in range(2 * GT):
                        pool.indirect_dma_start(gx[:, b, k, :], None, x,
                                                bass.IndirectOffsetOnAxis(gidx[:, b, k:k + 1], 0)).then_inc(s_gx[b], 16)

                def scatter(b, g):
                    pool.wait_ge(s_tot, g + 1)
                    pool.wait_ge(s_sidx, g + 1)
                    if not isinstance(g, int) or g > 0:
                        pool.wait_ge(s_sc, 64 * g)
                    pool.sem_inc(s_step, 1)
                    for k in range(GT):
                        pool.indirect_dma_start(agg, bass.IndirectOffsetOnAxis(sidx[:, b, k:k + 1], 0),
                                                gtot[:, b, k, :], None, compute_op=ALU.add).then_inc(s_sc, 16)

                gather(0, 0, 0)
                gather(0, 1, 1)
                for b in range(2):
                    gather(1, b, b + 2)
                    scatter(b, b)
                with pool.Fori(1, GROUPS // 2 - 1) as u:
                    for b in range(2):
                        gather(u + 1, b, u * 2 + b + 2)
                        scatter(b, u * 2 + b)
                gather(GROUPS // 2, 0, GROUPS - 1)
                for b in range(3):
                    scatter(b % 2, GROUPS - 3 + b)
                pool.wait_ge(s_sc, 64 * GROUPS)

            @block.vector
            def _(dve):
                ch = sem("p1_chain")
                PER = 9

                def group(u, b, g):
                    k = [0]

                    def link(ins):
                        k[0] += 1
                        ins.then_inc(ch, 1)
                        dve.wait_ge(ch, g * PER + k[0])

                    rows = gx[:, b, :, :]
                    bc = lambda i: gst[:, i, :].rearrange("p (a o) -> p a o", o=1).to_broadcast([P, 2 * GT, D])
                    dve.wait_ge(s_gx[b], 128 * (u + 1))
                    link(nc.vector.reduce_sum(gst[:, 0, :], rows, X))
                    link(nc.vector.tensor_scalar(gst[:, 1, :], gst[:, 0, :], 1.0 / D, None, ALU.mult))
                    nc.vector.tensor_tensor(gc[:, :, :], rows, bc(1), ALU.subtract).then_inc(s_c, 1)
                    dve.wait_ge(s_gi[b], 48 * (u + 1))
                    dve.wait_ge(s_m3, g)
                    for j in range(GT):
                        ins = nc.vector.tensor_scalar(same[:, j, :], krow[:, b, :], kcolf[:, 0, bass.ds(g * GT + j, 1)],
                                                      None, ALU.is_equal)
                        if j == GT - 1:
                            ins.then_inc(s_same, 1)
                    dve.wait_ge(s_same, g + 1)
                    dve.wait_ge(s_sq, g + 1)
                    nc.vector.reduce_sum(gst[:, 2, :], gsq[:, :, :], X).then_inc(s_ss, 1)
                    for j in range(GT):
                        n = P * (j + 1)
                        link(nc.vector.tensor_tensor_reduce(
                            out=same_out[:, 0:n], in0=same[:, j, 0:n], in1=before[:, GROUP - n:GROUP], scale=1.0,
                            scalar=0.0, op0=ALU.mult, op1=ALU.add, accum_out=cnt[:, 0, j:j + 1]))
                    dve.wait_ge(s_std, g + 1)
                    link(nc.vector.reciprocal(gst[:, 0, :], gst[:, 3, :]))
                    nc.vector.scalar_tensor_tensor(out=gh[:, :, :], in0=gc[:, :, :], scalar=0.0, in1=bc(0),
                                                   op0=ALU.max, op1=ALU.mult).then_inc(s_h, 1)
                    link(nc.vector.scalar_tensor_tensor(out=cnt[:, 1, :], in0=cnt[:, 0, :], scalar=1.0,
                                                        in1=dump_f[:, :], op0=ALU.min, op1=ALU.mult))
                    if not isinstance(g, int) or g >= 2:
                        dve.wait_ge(s_sc, 64 * (g - 1))
                    nc.vector.tensor_tensor(sidx[:, b, :], cnt[:, 1, :],
                                            kcolf[:, 0, bass.ds(g * GT, GT)], ALU.max).then_inc(s_sidx, 1)
                    dve.wait_ge(s_m2, g + 1)
                    nc.vector.tensor_tensor(
                        gmsg[:, :, :], bank[2][:, 0:GT * D].rearrange("p (j d) -> p j d", d=D),
                        b_msg2[:, :].rearrange("p (a d) -> p a d", a=1).to_broadcast([P, GT, D]), ALU.add).then_inc(s_msg, 1)
                    link(nc.vector.tensor_copy(tmp[:, 3:4], zero_col[:, :]))
                    assert k[0] == PER

                group(0, 0, 0)
                group(0, 1, 1)
                with dve.Fori(1, GROUPS // 2) as u:
                    for b in range(2):
                        group(u, b, u * 2 + b)
                group(GROUPS // 2, 0, GROUPS - 1)

            @block.scalar
            def _(act):
                def group(u, b, g):
                    act.wait_ge(s_c, g + 1)
                    nc.scalar.activation(gsq[:, :, :], gc[:, :, :], ACT.Square).then_inc(s_sq, 1)
                    act.wait_ge(s_ss, g + 1)
                    nc.scalar.activation(gst[:, 3, :], gst[:, 2, :], ACT.Sqrt, bias=eps_col[:, :],
                                         scale=1.0 / D).then_inc(s_std, 1)
                    act.wait_ge(s_tp, g + 1)
                    nc.scalar.copy(ght[:, :], bank[0][:, :]).then_inc(s_ht, 1)
                    act.wait_ge(s_m1, g + 1)
                    nc.scalar.activation(ghid[:, :], bank[1][:, :], ACT.Relu, bias=b_msg1[:, :]).then_inc(s_hid, 1)
                    act.wait_ge(s_m3, g + 1)
                    if not isinstance(g, int) or g >= 2:
                        act.wait_ge(s_sc, 64 * (g - 1))
                    nc.scalar.copy(gtot[:, b, :, :], bank[3][:, 0:GT * D].rearrange("p (j d) -> p j d", d=D)).then_inc(s_tot, 1)

                group(0, 0, 0)
                group(0, 1, 1)
                with act.Fori(1, GROUPS // 2) as u:
                    for b in range(2):
                        group(u, b, u * 2 + b)
                group(GROUPS // 2, 0, GROUPS - 1)

            @block.tensor
            def _(pe):
                def group(u, b, g):
                    pe.wait_ge(s_h, g + 1)
                    for j in range(GT):
                        ins = nc.tensor.transpose(bank[0][:, P * j:P * j + P],
                                                  gh[:, 2 * j:2 * j + 2, :].rearrange("p a d -> p (a d)"), ident[:, :])
                    ins.then_inc(s_tp, 1)
                    pe.wait_ge(s_ht, g + 1)
                    nc.tensor.matmul(bank[1][:, :], w_msg1[:, :], ght[:, :], start=True, stop=False)
                    nc.tensor.matmul(bank[1][:, :], w_msg1e[:, :], eat[0:32, b, :], start=False, stop=True).then_inc(s_m1, 1)
                    pe.wait_ge(s_hid, g + 1)
                    for j in range(GT):
                        ins = nc.tensor.matmul(bank[2][:, D * j:D * j + D], ghid[:, P * j:P * j + P], w_msg2[:, :],
                                               start=True, stop=True)
                    ins.then_inc(s_m2, 1)
                    pe.wait_ge(s_msg, g + 1)
                    pe.wait_ge(s_same, g + 1)
                    pe.wait_ge(s_tot, g)
                    for i in range(GT):
                        for j in range(GT):
                            ins = nc.tensor.matmul(bank[3][:, D * i:D * i + D], same[:, j, P * i:P * i + P],
                                                   gmsg[:, j, :], start=(j == 0), stop=(j == GT - 1))
                    ins.then_inc(s_m3, 1)

                group(0, 0, 0)
                group(0, 1, 1)
                with pe.Fori(1, GROUPS // 2) as u:
                    for b in range(2):
                        group(u, b, u * 2 + b)
                group(GROUPS // 2, 0, GROUPS - 1)

        s_nx = [sem(f"s_nx{b}") for b in range(2)]
        s_nc = sem("s_nc")
        s_nsq = sem("s_nsq")
        s_nss = sem("s_nss")
        s_nstd = sem("s_nstd")
        s_nh = sem("s_nh")
        s_npool = sem("s_npool")
        s_ncb = sem("s_ncb")
        s_ntp = sem("s_ntp")
        s_nht = sem("s_nht")
        s_nm1 = sem("s_nm1")
        s_nhid = sem("s_nhid")
        s_nm2 = sem("s_nm2")
        s_nc1 = sem("s_nc1")
        s_nsq1 = sem("s_nsq1")
        s_nss1 = sem("s_nss1")
        s_nstd1 = sem("s_nstd1")
        s_nst = [sem(f"s_nst{b}") for b in range(2)]
        xin = [area(0), area(1)]
        ain = [area(2), area(3)]
        c0 = area(4)
        sq0 = area(5)
        c0b = [area(6), area(7)]
        c1 = [area(8), area(9)]
        sq1 = area(10)
        ha = area(11, (J, 2 * D))
        hts = [area(13, (4, P)), area(14, (4, P))]
        hids = [area(15, (4, P)), area(16, (4, P))]
        nst = big[:, 17 * J * D:17 * J * D + 16 * J].rearrange("p (a j) -> p a j", j=J)
        Q = J // 4
        with nc.Block() as block:
            @block.sync
            def _(sp):
                def load(u, b, g):
                    if not isinstance(g, int) or g >= 2:
                        sp.wait_ge(s_nc, g - 1)
                        sp.wait_ge(s_npool, g - 1)
                    sp.dma_start(xin[b], chunk_rows(x, g)).then_inc(s_nx[b], 16)
                    sp.dma_start(ain[b], chunk_rows(agg, g)).then_inc(s_nx[b], 16)

                def store(u, b, g):
                    sp.wait_ge(s_nc1, Q * (g + 1))
                    sp.dma_start(chunk_rows(ctab, g), c1[b]).then_inc(s_nst[b], 16)

                load(0, 0, 0)
                load(0, 1, 1)
                with sp.Fori(0, CHUNKS // 2 - 1) as u:
                    for b in range(2):
                        load(u + 1, b, u * 2 + b + 2)
                        store(u, b, u * 2 + b)
                load(CHUNKS // 2, 0, CHUNKS - 1)
                for b in range(3):
                    store(0, b % 2, CHUNKS - 3 + b)
                sp.wait_ge(s_nst[0], 16 * (CHUNKS // 2 + 1))
                sp.wait_ge(s_nst[1], 16 * (CHUNKS // 2))

            bcj = lambda ap: ap.rearrange("p (a o) -> p a o", o=1).to_broadcast([P, J, D])

            @block.gpsimd
            def _(pool):
                def chunk(u, b, g):
                    pool.wait_ge(s_nx[b], 32 * (u + 1))
                    if not isinstance(g, int) or g >= 1:
                        pool.wait_ge(s_ntp, Q * g)
                    pool.sem_inc(s_step, 1)
                    nc.gpsimd.tensor_copy(ha[:, :, D:2 * D], ain[b]).then_inc(s_npool, 1)
                    pool.wait_ge(s_nc, g + 1)
                    if not isinstance(g, int) or g >= 2:
                        pool.wait_ge(s_nc1, Q * (g - 1))
                    nc.gpsimd.tensor_tensor(c0b[b], c0, b_upd2[:, 0:D].rearrange("p (a d) -> p a d", a=1).to_broadcast([P, J, D]),
                                            ALU.add).then_inc(s_ncb, 1)

                chunk(0, 0, 0)
                chunk(0, 1, 1)
                with pool.Fori(1, CHUNKS // 2) as u:
                    for b in range(2):
                        chunk(u, b, u * 2 + b)
                chunk(CHUNKS // 2, 0, CHUNKS - 1)

            @block.vector
            def _(dve):
                cha = sem("p2_chain_a")
                chb = sem("p2_chain_b")
                PA, PB = 4, 3

                def linker(s, base):
                    k = [0]

                    def link(ins):
                        k[0] += 1
                        ins.then_inc(s, 1)
                        dve.wait_ge(s, base + k[0])
                    return link

                def front(u, b, g):
                    link = linker(cha, g * PA)
                    dve.wait_ge(s_nx[b], 32 * (u + 1))
                    link(nc.vector.reduce_sum(nst[:, 0, :], xin[b], X))
                    link(nc.vector.tensor_scalar(nst[:, 1 + b, :], nst[:, 0, :], 1.0 / D, None, ALU.mult))
                    if not isinstance(g, int) or g >= 1:
                        dve.wait_ge(s_ncb, g)
                    nc.vector.tensor_tensor(c0, xin[b], bcj(nst[:, 1 + b, :]), ALU.subtract).then_inc(s_nc, 1)

                def front_sum(u, b, g):
                    dve.wait_ge(s_nsq, g + 1)
                    nc.vector.reduce_sum(nst[:, 3, :], sq0, X).then_inc(s_nss, 1)

                def front_end(u, b, g):
                    link = linker(cha, g * PA + 2)
                    dve.wait_ge(s_nstd, g + 1)
                    link(nc.vector.reciprocal(nst[:, 5, :], nst[:, 4, :]))
                    if not isinstance(g, int) or g >= 1:
                        dve.wait_ge(s_ntp, Q * g)
                    nc.vector.scalar_tensor_tensor(out=ha[:, :, 0:D], in0=c0, scalar=0.0, in1=bcj(nst[:, 5, :]),
                                                   op0=ALU.max, op1=ALU.mult).then_inc(s_nh, 1)
                    link(nc.vector.tensor_copy(tmp[:, 3:4], zero_col[:, :]))

                def back(u, b, g):
                    link = linker(chb, g * PB)
                    dve.wait_ge(s_ncb, g + 1)
                    if not isinstance(g, int) or g >= 2:
                        dve.wait_ge(s_nst[b], 16 * u)
                    link(nc.vector.tensor_scalar(nst[:, 6, :], nst[:, 1 + b, :], b_upd2[:, D:D + 1], None, ALU.add))
                    for q in range(4):
                        dve.wait_ge(s_nm2, 4 * g + q + 1)
                        o = bank[4 + q][:, 0:Q * (D + 1)].rearrange("p (j e) -> p j e", e=D + 1)
                        nc.vector.tensor_tensor(m1[:, bass.ds(g * J + Q * q, Q)], nst[:, 6, Q * q:Q * q + Q],
                                                o[:, :, D:D + 1].rearrange("p j o -> p (j o)"), ALU.add)
                        nc.vector.tensor_tensor(c1[b][:, Q * q:Q * q + Q, :], c0b[b][:, Q * q:Q * q + Q, :],
                                                o[:, :, 0:D], ALU.add).then_inc(s_nc1, 1)

                def back_end(u, b, g):
                    link = linker(chb, g * PB + 1)
                    dve.wait_ge(s_nsq1, g + 1)
                    nc.vector.reduce_sum(nst[:, 7, :], sq1, X).then_inc(s_nss1, 1)
                    dve.wait_ge(s_nstd1, g + 1)
                    link(nc.vector.reciprocal(r1[:, bass.ds(g * J, J)], nst[:, 8, :]))
                    link(nc.vector.tensor_copy(tmp[:, 4:5], zero_col[:, :]))

                def both(un, bn, gn, u, b, g):
                    front(un, bn, gn)
                    back(u, b, g)
                    front_sum(un, bn, gn)
                    front_end(un, bn, gn)
                    back_end(u, b, g)

                front(0, 0, 0)
                front_sum(0, 0, 0)
                front_end(0, 0, 0)
                both(0, 1, 1, 0, 0, 0)
                both(1, 0, 2, 0, 1, 1)
                with dve.Fori(1, CHUNKS // 2) as u:
                    both(u, 1, u * 2 + 1, u, 0, u * 2)
                    both(u + 1, 0, u * 2 + 2, u, 1, u * 2 + 1)
                back(CHUNKS // 2, 0, CHUNKS - 1)
                back_end(CHUNKS // 2, 0, CHUNKS - 1)

            @block.scalar
            def _(act):
                def front(u, b, g):
                    act.wait_ge(s_nc, g + 1)
                    nc.scalar.activation(sq0, c0, ACT.Square).then_inc(s_nsq, 1)
                    act.wait_ge(s_nss, g + 1)
                    nc.scalar.activation(nst[:, 4, :], nst[:, 3, :], ACT.Sqrt, bias=eps_col[:, :], scale=1.0 / D).then_inc(s_nstd, 1)

                def mid(u, b, g):
                    for q in range(4):
                        act.wait_ge(s_ntp, 4 * g + q + 1)
                        nc.scalar.copy(hts[q % 2], bank[q % 2][:, :].rearrange("p (a b) -> p a b", b=P)).then_inc(s_nht, 1)
                        act.wait_ge(s_nm1, 4 * g + q + 1)
                        nc.scalar.activation(hids[q % 2], bank[2 + q % 2][:, :].rearrange("p (a b) -> p a b", b=P), ACT.Relu,
                                             bias=b_upd1[:, :]).then_inc(s_nhid, 1)

                def back(u, b, g):
                    act.wait_ge(s_nc1, Q * (g + 1))
                    nc.scalar.activation(sq1, c1[b], ACT.Square).then_inc(s_nsq1, 1)

                def back_end(u, b, g):
                    act.wait_ge(s_nss1, g + 1)
                    nc.scalar.activation(nst[:, 8, :], nst[:, 7, :], ACT.Sqrt, bias=eps_col[:, :], scale=1.0 / D).then_inc(s_nstd1, 1)

                def both(un, bn, gn, u, b, g):
                    mid(u, b, g)
                    front(un, bn, gn)
                    back(u, b, g)
                    back_end(u, b, g)

                front(0, 0, 0)
                both(0, 1, 1, 0, 0, 0)
                both(1, 0, 2, 0, 1, 1)
                with act.Fori(1, CHUNKS // 2) as u:
                    both(u, 1, u * 2 + 1, u, 0, u * 2)
                    both(u + 1, 0, u * 2 + 2, u, 1, u * 2 + 1)
                mid(CHUNKS // 2, 0, CHUNKS - 1)
                back(CHUNKS // 2, 0, CHUNKS - 1)
                back_end(CHUNKS // 2, 0, CHUNKS - 1)

            @block.tensor
            def _(pe):
                def chunk(u, b, g):
                    pe.wait_ge(s_nh, g + 1)
                    pe.wait_ge(s_npool, g + 1)

                    def tp(q):
                        if q >= 2:
                            pe.wait_ge(s_nht, 4 * g + q - 1)
                        elif not isinstance(g, int) or g >= 1:
                            pe.wait_ge(s_nht, 4 * g + q - 1)
                        for j in range(4):
                            ins = nc.tensor.transpose(bank[q % 2][:, P * j:P * j + P], ha[:, 4 * q + j, :], ident[:, :])
                        ins.then_inc(s_ntp, 1)

                    def mm1(q):
                        pe.wait_ge(s_nht, 4 * g + q + 1)
                        if q >= 2 or not isinstance(g, int) or g >= 1:
                            pe.wait_ge(s_nhid, 4 * g + q - 1)
                        nc.tensor.matmul(bank[2 + q % 2][:, :], w_upd1[:, :], hts[q % 2].rearrange("p a b -> p (a b)"),
                                         start=True, stop=True).then_inc(s_nm1, 1)

                    def mm2(q):
                        pe.wait_ge(s_nhid, 4 * g + q + 1)
                        if not isinstance(g, int) or g >= 1:
                            pe.wait_ge(s_nc1, 4 * (g - 1) + q + 1)
                        for j in range(4):
                            ins = nc.tensor.matmul(bank[4 + q][:, (D + 1) * j:(D + 1) * (j + 1)], hids[q % 2][:, j, :],
                                                   w_upd2[:, :], start=True, stop=True)
                        ins.then_inc(s_nm2, 1)

                    tp(0)
                    tp(1)
                    mm1(0)
                    for q in range(4):
                        if q + 2 < 4:
                            tp(q + 2)
                        if q + 1 < 4:
                            mm1(q + 1)
                        mm2(q)

                chunk(0, 0, 0)
                chunk(0, 1, 1)
                with pe.Fori(1, CHUNKS // 2) as u:
                    for b in range(2):
                        chunk(u, b, u * 2 + b)
                chunk(CHUNKS // 2, 0, CHUNKS - 1)

        s_ei = [sem(f"s_ei{b}") for b in range(2)]
        s_ex = [sem(f"s_ex{b}") for b in range(2)]
        s_esq = sem("s_esq")
        s_ess = sem("s_ess")
        s_estd = sem("s_estd")
        s_eh = sem("s_eh")
        s_etp = sem("s_etp")
        s_eht = sem("s_eht")
        s_em = sem("s_em")
        s_et = sem("s_et")
        s_es = sem("s_es")
        with nc.Block() as block:
            @block.sync
            def _(sp):
                def load(u, b, g):
                    if not isinstance(g, int) or g >= 2:
                        sp.wait_ge(s_ex[b], 128 * u)
                        sp.wait_ge(s_em, g - 1)
                        sp.wait_ge(s_es, g - 1)
                    sp.dma_start(gidx[:, b, :], gat[bass.ds(g, 1), :, :].rearrange("g p c -> (g p) c")).then_inc(s_ei[b], 16)
                    sp.dma_start(eat[:, b, :], ea64_t[:, bass.ds(g * GROUP, GROUP)]).then_inc(s_ei[b], 16)
                    sp.dma_start(ewr[:, b, :], edge_w[bass.ds(g * GROUP, GROUP)].partition_broadcast(P)).then_inc(s_ei[b], 16)

                load(0, 0, 0)
                load(0, 1, 1)
                with sp.Fori(1, GROUPS // 2) as u:
                    for b in range(2):
                        load(u, b, u * 2 + b)
                load(GROUPS // 2, 0, GROUPS - 1)

            @block.gpsimd
            def _(pool):
                def gather(u, b, g):
                    pool.wait_ge(s_ei[b], 48 * (u + 1))
                    if not isinstance(g, int) or g >= 2:
                        pool.wait_ge(s_eh, g - 1)
                    pool.sem_inc(s_step, 1)
                    for k in range(2 * GT):
                        pool.indirect_dma_start(gx[:, b, k, :], None, ctab,
                                                bass.IndirectOffsetOnAxis(gidx[:, b, k:k + 1], 0)).then_inc(s_ex[b], 16)

                gather(0, 0, 0)
                gather(0, 1, 1)
                with pool.Fori(1, GROUPS // 2) as u:
                    for b in range(2):
                        gather(u, b, u * 2 + b)
                gather(GROUPS // 2, 0, GROUPS - 1)

            @block.vector
            def _(dve):
                ch = sem("p3_chain")
                PER = 3

                def group(u, b, g):
                    k = [0]

                    def link(ins):
                        k[0] += 1
                        ins.then_inc(ch, 1)
                        dve.wait_ge(ch, g * PER + k[0])

                    dve.wait_ge(s_esq, g + 1)
                    nc.vector.reduce_sum(gst[:, 2, :], gsq[:, :, :], X).then_inc(s_ess, 1)
                    dve.wait_ge(s_estd, g + 1)
                    link(nc.vector.reciprocal(gst[:, 0, :], gst[:, 3, :]))
                    nc.vector.scalar_tensor_tensor(
                        out=gh[:, :, :], in0=gx[:, b, :, :], scalar=0.0,
                        in1=gst[:, 0, :].rearrange("p (a o) -> p a o", o=1).to_broadcast([P, 2 * GT, D]),
                        op0=ALU.max, op1=ALU.mult).then_inc(s_eh, 1)
                    dve.wait_ge(s_et, g + 1)
                    t = tbuf[:, b, :]
                    link(nc.vector.tensor_tensor_reduce(out=same_out[:, :], in0=t, in1=ewr[:, b, :], scale=1.0,
                                                        scalar=s1[:, 1 - b:2 - b],
                                                        op0=ALU.mult, op1=ALU.add, accum_out=s1[:, b:b + 1]))
                    link(nc.vector.tensor_tensor_reduce(out=same[:, 0, :], in0=same_out[:, :], in1=t, scale=1.0,
                                                        scalar=s2[:, 1 - b:2 - b], op0=ALU.mult, op1=ALU.add,
                                                        accum_out=s2[:, b:b + 1]))
                    nc.vector.tensor_copy(big[:, bass.ds(g * GROUP, GROUP)], t).then_inc(s_es, 1)

                group(0, 0, 0)
                group(0, 1, 1)
                with dve.Fori(1, GROUPS // 2) as u:
                    for b in range(2):
                        group(u, b, u * 2 + b)
                group(GROUPS // 2, 0, GROUPS - 1)

            @block.scalar
            def _(act):
                def group(u, b, g):
                    act.wait_ge(s_ex[b], 128 * (u + 1))
                    nc.scalar.activation(gsq[:, :, :], gx[:, b, :, :], ACT.Square).then_inc(s_esq, 1)
                    act.wait_ge(s_ess, g + 1)
                    nc.scalar.activation(gst[:, 3, :], gst[:, 2, :], ACT.Sqrt, bias=eps_col[:, :], scale=1.0 / D).then_inc(s_estd, 1)
                    act.wait_ge(s_etp, g + 1)
                    nc.scalar.copy(ght[:, :], bank[0][:, :]).then_inc(s_eht, 1)
                    act.wait_ge(s_em, g + 1)
                    if not isinstance(g, int) or g >= 2:
                        act.wait_ge(s_es, g - 1)
                    nc.scalar.activation(tbuf[:, b, :], bank[1][:, :], ACT.Identity, bias=b_gate[:, :]).then_inc(s_et, 1)

                group(0, 0, 0)
                group(0, 1, 1)
                with act.Fori(1, GROUPS // 2) as u:
                    for b in range(2):
                        group(u, b, u * 2 + b)
                group(GROUPS // 2, 0, GROUPS - 1)

            @block.tensor
            def _(pe):
                def group(u, b, g):
                    pe.wait_ge(s_eh, g + 1)
                    for j in range(GT):
                        ins = nc.tensor.transpose(bank[0][:, P * j:P * j + P],
                                                  gh[:, 2 * j:2 * j + 2, :].rearrange("p a d -> p (a d)"), ident[:, :])
                    ins.then_inc(s_etp, 1)
                    pe.wait_ge(s_eht, g + 1)
                    pe.wait_ge(s_ei[b], 48 * (u + 1))
                    nc.tensor.matmul(bank[1][:, :], w_gate[:, :], ght[:, :], start=True, stop=False)
                    nc.tensor.matmul(bank[1][:, :], w_gatee[:, :], eat[:, b, :], start=False, stop=True).then_inc(s_em, 1)

                group(0, 0, 0)
                group(0, 1, 1)
                with pe.Fori(1, GROUPS // 2) as u:
                    for b in range(2):
                        group(u, b, u * 2 + b)
                group(GROUPS // 2, 0, GROUPS - 1)

        s_var = sem("s_var")
        s_sd = sem("s_sd")
        with nc.Block() as block:
            @block.vector
            def _(dve):
                ch = sem("p3b_chain")
                k = [0]

                def link(ins):
                    k[0] += 1
                    ins.then_inc(ch, 1)
                    dve.wait_ge(ch, k[0])

                link(nc.vector.tensor_copy(tmp[:, 0:1], s1[:, 0:1]))
                link(nc.vector.tensor_copy(tmp[:, 1:2], s2[:, 0:1]))
                link(nc.vector.tensor_scalar(tmp[:, 2:4], tmp[:, 0:2], wsum_inv[:, 0:1], None, ALU.mult))
                link(nc.vector.tensor_tensor(tmp[:, 4:5], tmp[:, 2:3], tmp[:, 2:3], ALU.mult))
                link(nc.vector.tensor_tensor(tmp[:, 5:6], tmp[:, 3:4], tmp[:, 4:5], ALU.subtract))
                nc.vector.tensor_scalar(tmp[:, 5:6], tmp[:, 5:6], 0.0, None, ALU.max).then_inc(s_var, 1)
                dve.wait_ge(s_sd, 1)
                link(nc.vector.reciprocal(tmp[:, 7:8], tmp[:, 6:7]))
                link(nc.vector.tensor_tensor(A1[:, :], g1c[:, :], tmp[:, 7:8], ALU.mult))
                link(nc.vector.tensor_tensor(tmp[:, 0:1], A1[:, :], tmp[:, 2:3], ALU.mult))
                link(nc.vector.tensor_tensor(B1[:, :], b1c[:, :], tmp[:, 0:1], ALU.subtract))

            @block.scalar
            def _(act):
                act.wait_ge(s_var, 1)
                nc.scalar.activation(tmp[:, 6:7], tmp[:, 5:6], ACT.Sqrt, bias=eps_col[:, :]).then_inc(s_sd, 1)

        s_fi = [sem(f"s_fi{b}") for b in range(2)]
        s_fg = sem("s_fg")
        s_ftp = sem("s_ftp")
        s_fe = sem("s_fe")
        s_fl = sem("s_fl")
        s_fmsg = sem("s_fmsg")
        s_fsame = sem("s_fsame")
        s_fsidx = sem("s_fsidx")
        s_fm = sem("s_fm")
        s_ftot = sem("s_ftot")
        s_fsc = sem("s_fsc")
        gq = gsq
        with nc.Block() as block:
            @block.sync
            def _(sp):
                def load(u, b, g):
                    if not isinstance(g, int) or g >= 2:
                        sp.wait_ge(s_fsame, g - 1)
                    sp.dma_start(krow[:, b, :], key_src[bass.ds(g * GROUP, GROUP)].partition_broadcast(P)).then_inc(s_fi[b], 16)

                load(0, 0, 0)
                load(0, 1, 1)
                with sp.Fori(1, GROUPS // 2) as u:
                    for b in range(2):
                        load(u, b, u * 2 + b)
                load(GROUPS // 2, 0, GROUPS - 1)

            @block.gpsimd
            def _(pool):
                def scatter(b, g):
                    pool.wait_ge(s_ftot, g + 1)
                    pool.wait_ge(s_fsidx, g + 1)
                    if not isinstance(g, int) or g > 0:
                        pool.wait_ge(s_fsc, 64 * g)
                    pool.sem_inc(s_step, 1)
                    for k in range(GT):
                        pool.indirect_dma_start(nsum, bass.IndirectOffsetOnAxis(sidx[:, b, k:k + 1], 0),
                                                gtot[:, b, k, :], None, compute_op=ALU.add).then_inc(s_fsc, 16)

                scatter(0, 0)
                scatter(1, 1)
                with pool.Fori(1, GROUPS // 2) as u:
                    for b in range(2):
                        scatter(b, u * 2 + b)
                scatter(0, GROUPS - 1)
                pool.wait_ge(s_fsc, 64 * GROUPS)

            @block.vector
            def _(dve):
                ch = sem("p4_chain")
                PER = 8

                def group(u, b, g):
                    k = [0]

                    def link(ins):
                        k[0] += 1
                        ins.then_inc(ch, 1)
                        dve.wait_ge(ch, g * PER + k[0])

                    dve.wait_ge(s_fi[b], 16 * (u + 1))
                    dve.wait_ge(s_fm, g)
                    for j in range(GT):
                        ins = nc.vector.tensor_scalar(same[:, j, :], krow[:, b, :], kcolf[:, 1, bass.ds(g * GT + j, 1)],
                                                      None, ALU.is_equal)
                    ins.then_inc(s_fsame, 1)
                    dve.wait_ge(s_fsame, g + 1)
                    for j in range(GT):
                        n = P * (j + 1)
                        link(nc.vector.tensor_tensor_reduce(
                            out=same_out[:, 0:n], in0=same[:, j, 0:n], in1=before[:, GROUP - n:GROUP], scale=1.0,
                            scalar=0.0, op0=ALU.mult, op1=ALU.add, accum_out=cnt[:, 0, j:j + 1]))
                    link(nc.vector.scalar_tensor_tensor(out=cnt[:, 1, :], in0=cnt[:, 0, :], scalar=1.0,
                                                        in1=dump_f[:, :], op0=ALU.min, op1=ALU.mult))
                    if not isinstance(g, int) or g >= 2:
                        dve.wait_ge(s_fsc, 64 * (g - 1))
                    nc.vector.tensor_tensor(sidx[:, b, :], cnt[:, 1, :],
                                            kcolf[:, 1, bass.ds(g * GT, GT)], ALU.max).then_inc(s_fsidx, 1)
                    dve.wait_ge(s_fe, g + 1)
                    link(nc.vector.tensor_scalar(gh[:, 0:GT, :], gq[:, 0:GT, :], 1.0, None, ALU.add))
                    link(nc.vector.reciprocal(gh[:, GT:2 * GT, :], gh[:, 0:GT, :]))
                    dve.wait_ge(s_fl, g + 1)
                    link(nc.vector.scalar_tensor_tensor(
                        out=gc[:, 0:GT, :], in0=bank[g_bank][:, :].rearrange("p (j e) -> p j e", e=P)[:, :, D:P], scalar=0.0,
                        in1=gc[:, GT:2 * GT, :], op0=ALU.max, op1=ALU.add))
                    nc.vector.tensor_tensor(gmsg[:, :, :], gc[:, 0:GT, :], gh[:, GT:2 * GT, :], ALU.mult).then_inc(s_fmsg, 1)
                    assert k[0] == PER

                g_bank = 0
                group(0, 0, 0)
                group(0, 1, 1)
                with dve.Fori(1, GROUPS // 2) as u:
                    for b in range(2):
                        group(u, b, u * 2 + b)
                group(GROUPS // 2, 0, GROUPS - 1)

            @block.scalar
            def _(act):
                cha = sem("act_chain")

                def group(u, b, g):
                    act.wait_ge(s_ftp, g)
                    nc.scalar.activation(ght[:, :], big[:, bass.ds(g * GROUP, GROUP)], ACT.Identity, bias=B1[:, :],
                                         scale=A1[:, :]).then_inc(s_fg, 1)
                    act.wait_ge(s_ftp, g + 1)
                    act.wait_ge(s_fmsg, g)
                    tb = bank[0][:, :].rearrange("p (j e) -> p j e", e=P)
                    nc.scalar.activation(gq[:, 0:GT, :], tb[:, :, 0:D], ACT.Exp, scale=-1.0).then_inc(s_fe, 1)
                    nc.scalar.activation(gq[:, GT:2 * GT, :], tb[:, :, D:P], ACT.Abs).then_inc(cha, 1)
                    act.wait_ge(cha, 2 * g + 1)
                    nc.scalar.activation(gx[:, 0, 0:GT, :], gq[:, GT:2 * GT, :], ACT.Exp, scale=-1.0).then_inc(cha, 1)
                    act.wait_ge(cha, 2 * g + 2)
                    nc.scalar.activation(gc[:, GT:2 * GT, :], gx[:, 0, 0:GT, :], ACT.Ln, bias=1.0).then_inc(s_fl, 1)
                    act.wait_ge(s_fm, g + 1)
                    if not isinstance(g, int) or g >= 2:
                        act.wait_ge(s_fsc, 64 * (g - 1))
                    nc.scalar.copy(gtot[:, b, :, :], bank[3][:, 0:GT * D].rearrange("p (j d) -> p j d", d=D)).then_inc(s_ftot, 1)

                group(0, 0, 0)
                group(0, 1, 1)
                with act.Fori(1, GROUPS // 2) as u:
                    for b in range(2):
                        group(u, b, u * 2 + b)
                group(GROUPS // 2, 0, GROUPS - 1)

            @block.tensor
            def _(pe):
                def group(u, b, g):
                    pe.wait_ge(s_fg, g + 1)
                    pe.wait_ge(s_fmsg, g)
                    for j in range(GT):
                        ins = nc.tensor.transpose(bank[0][:, P * j:P * j + P], ght[:, P * j:P * j + P], ident[:, :])
                    ins.then_inc(s_ftp, 1)
                    pe.wait_ge(s_fmsg, g + 1)
                    pe.wait_ge(s_fsame, g + 1)
                    pe.wait_ge(s_ftot, g)
                    for i in range(GT):
                        for j in range(GT):
                            ins = nc.tensor.matmul(bank[3][:, D * i:D * i + D], same[:, j, P * i:P * i + P],
                                                   gmsg[:, j, :], start=(j == 0), stop=(j == GT - 1))
                    ins.then_inc(s_fm, 1)

                group(0, 0, 0)
                group(0, 1, 1)
                with pe.Fori(1, GROUPS // 2) as u:
                    for b in range(2):
                        group(u, b, u * 2 + b)
                group(GROUPS // 2, 0, GROUPS - 1)

        s_vx = [sem(f"s_vx{b}") for b in range(2)]
        s_vcp = sem("s_vcp")
        s_vsq = sem("s_vsq")
        s_vm = sem("s_vm")
        s_vend = sem("s_vend")
        s_vd = sem("s_vd")
        s_vbc = sem("s_vbc")
        s_vvar = sem("s_vvar")
        s_vsd = sem("s_vsd")
        vin = [area(0), area(1)]
        vw = [nst[:, 0, :], nst[:, 1, :]]
        pair = [area(3, (J, 2 * D)), area(5, (J, 2 * D))]
        with nc.Block() as block:
            @block.sync
            def _(sp):
                def load(u, b, g):
                    if not isinstance(g, int) or g >= 2:
                        sp.wait_ge(s_vcp, g - 1)
                        sp.wait_ge(s_vsq, g - 1)
                        sp.wait_ge(s_vm, g - 1)
                    sp.dma_start(vin[b], chunk_rows(nsum, g)).then_inc(s_vx[b], 16)
                    sp.dma_start(vw[b], node_w[:, bass.ds(g * J, J)]).then_inc(s_vx[b], 16)

                load(0, 0, 0)
                load(0, 1, 1)
                with sp.Fori(1, CHUNKS // 2) as u:
                    for b in range(2):
                        load(u, b, u * 2 + b)
                load(CHUNKS // 2, 0, CHUNKS - 1)

            @block.scalar
            def _(act):
                def chunk(u, b, g):
                    act.wait_ge(s_vx[b], 32 * (u + 1))
                    if not isinstance(g, int) or g >= 2:
                        act.wait_ge(s_vm, g - 1)
                    nc.scalar.activation(pair[b][:, :, D:2 * D], vin[b], ACT.Square).then_inc(s_vsq, 1)

                chunk(0, 0, 0)
                chunk(0, 1, 1)
                with act.Fori(1, CHUNKS // 2) as u:
                    for b in range(2):
                        chunk(u, b, u * 2 + b)
                chunk(CHUNKS // 2, 0, CHUNKS - 1)
                act.wait_ge(s_vvar, 1)
                nc.scalar.activation(row_tmp[:, 2, :], row_tmp[:, 1, :], ACT.Sqrt, bias=eps_col[:, :]).then_inc(s_vsd, 1)

            @block.vector
            def _(dve):
                def chunk(u, b, g):
                    dve.wait_ge(s_vx[b], 32 * (u + 1))
                    if not isinstance(g, int) or g >= 2:
                        dve.wait_ge(s_vm, g - 1)
                    nc.vector.tensor_copy(pair[b][:, :, 0:D], vin[b]).then_inc(s_vcp, 1)

                chunk(0, 0, 0)
                chunk(0, 1, 1)
                with dve.Fori(1, CHUNKS // 2) as u:
                    for b in range(2):
                        chunk(u, b, u * 2 + b)
                chunk(CHUNKS // 2, 0, CHUNKS - 1)
                ch = sem("p5_chain")
                k = [0]

                def link(ins):
                    k[0] += 1
                    ins.then_inc(ch, 1)
                    dve.wait_ge(ch, k[0])

                dve.wait_ge(s_vend, 1)
                link(nc.vector.tensor_scalar(tmp[:, 0:1], bank[0][:, 0:1], wsum_inv[:, 1:2], None, ALU.mult))
                nc.vector.tensor_scalar(same_out[:, 0:P], ident[:, :], tmp[:, 0:1], None, ALU.mult).then_inc(s_vd, 1)
                dve.wait_ge(s_vbc, 1)
                link(nc.vector.tensor_copy(row_tmp[:, 0, :], bank[1][:, 0:D]))
                link(nc.vector.tensor_tensor(row_tmp[:, 3, :], row_tmp[:, 0, :], row_tmp[:, 0, :], ALU.mult))
                link(nc.vector.tensor_tensor(row_tmp[:, 1, :], bank[1][:, D:2 * D], row_tmp[:, 3, :], ALU.subtract))
                nc.vector.tensor_scalar(row_tmp[:, 1, :], row_tmp[:, 1, :], 0.0, None, ALU.max).then_inc(s_vvar, 1)
                dve.wait_ge(s_vsd, 1)
                link(nc.vector.reciprocal(row_tmp[:, 3, :], row_tmp[:, 2, :]))
                link(nc.vector.tensor_tensor(A2[:, :], g2r[:, :], row_tmp[:, 3, :], ALU.mult))
                link(nc.vector.tensor_tensor(row_tmp[:, 1, :], A2[:, :], row_tmp[:, 0, :], ALU.mult))
                link(nc.vector.tensor_tensor(B2[:, :], b2r[:, :], row_tmp[:, 1, :], ALU.subtract))

            @block.tensor
            def _(pe):
                def chunk(u, b, g):
                    pe.wait_ge(s_vcp, g + 1)
                    pe.wait_ge(s_vsq, g + 1)
                    pe.wait_ge(s_vx[b], 32 * (u + 1))
                    for j in range(J):
                        first = isinstance(g, int) and g == 0 and j == 0
                        last = isinstance(g, int) and g == CHUNKS - 1 and j == J - 1
                        ins = nc.tensor.matmul(bank[0][:, 0:1], pair[b][:, j, :], vw[b][:, j:j + 1], start=first,
                                               stop=last)
                    ins.then_inc(s_vm, 1)
                    return ins

                chunk(0, 0, 0)
                chunk(0, 1, 1)
                with pe.Fori(1, CHUNKS // 2) as u:
                    for b in range(2):
                        chunk(u, b, u * 2 + b)
                chunk(CHUNKS // 2, 0, CHUNKS - 1)
                pe.wait_ge(s_vm, CHUNKS)
                pe.nop().then_inc(s_vend, 1)
                pe.wait_ge(s_vd, 1)
                nc.tensor.matmul(bank[1][:, 0:P], ones[:, :], same_out[:, 0:P], start=True, stop=True).then_inc(s_vbc, 1)

        s_ox = [sem(f"s_oxin{b}") for b in range(2)]
        s_oh = sem("s_oh")
        s_ou = sem("s_ou")
        s_oub = sem("s_oub")
        s_oz = sem("s_oz")
        s_osp = sem("s_osp")
        s_oabs = sem("s_oabs")
        s_oexp = sem("s_oexp")
        s_ol = sem("s_ol")
        s_ox1 = sem("s_ox1")
        s_oo = sem("s_oo")
        s_ost = [sem(f"s_ost{b}") for b in range(2)]
        cin = [area(0), area(1)]
        sin = [area(2), area(3)]
        oh = area(4)
        ou = area(5)
        oub = [area(6), area(7)]
        oz = [area(8), area(9)]
        oabs = area(10)
        oexp = area(11)
        ol = [area(12), area(13)]
        ox1 = [area(14), area(15)]
        osp = area(16)
        oo = [area(18), area(19)]
        with nc.Block() as block:
            bcj = lambda ap: ap.rearrange("p (a o) -> p a o", o=1).to_broadcast([P, J, D])
            bcd = lambda ap: ap.rearrange("p (a d) -> p a d", a=1).to_broadcast([P, J, D])

            @block.sync
            def _(sp):
                def load(u, b, g):
                    if not isinstance(g, int) or g >= 2:
                        sp.wait_ge(s_ox1, g - 1)
                        sp.wait_ge(s_ou, g - 1)
                        sp.wait_ge(s_oh, g - 1)
                    sp.dma_start(cin[b], chunk_rows(ctab, g)).then_inc(s_ox[b], 16)
                    sp.dma_start(sin[b], chunk_rows(nsum, g)).then_inc(s_ox[b], 16)

                def store(b, g):
                    sp.wait_ge(s_oo, g + 1)
                    sp.dma_start(chunk_rows(out, g), oo[b]).then_inc(s_ost[b], 16)

                load(0, 0, 0)
                load(0, 1, 1)
                with sp.Fori(0, CHUNKS // 2 - 1) as u:
                    for b in range(2):
                        load(u + 1, b, u * 2 + b + 2)
                        store(b, u * 2 + b)
                load(CHUNKS // 2, 0, CHUNKS - 1)
                for b in range(3):
                    store(b % 2, CHUNKS - 3 + b)
                sp.wait_ge(s_ost[0], 16 * (CHUNKS // 2 + 1))
                sp.wait_ge(s_ost[1], 16 * (CHUNKS // 2))

            @block.gpsimd
            def _(pool):
                def chunk(u, b, g):
                    pool.wait_ge(s_ox[b], 32 * (u + 1))
                    nc.gpsimd.tensor_tensor(ou, sin[b], bcd(A2[:, :]), ALU.mult).then_inc(s_ou, 1)
                    pool.wait_ge(s_ou, g + 1)
                    if not isinstance(g, int) or g >= 2:
                        pool.wait_ge(s_oz, g - 1)
                    nc.gpsimd.tensor_tensor(oub[b], ou, bcd(B2[:, :]), ALU.add).then_inc(s_oub, 1)
                    pool.wait_ge(s_oub, g + 1)

                chunk(0, 0, 0)
                chunk(0, 1, 1)
                with pool.Fori(1, CHUNKS // 2) as u:
                    for b in range(2):
                        chunk(u, b, u * 2 + b)
                chunk(CHUNKS // 2, 0, CHUNKS - 1)

            @block.vector
            def _(dve):
                def front(u, b, g):
                    dve.wait_ge(s_ox[b], 32 * (u + 1))
                    dve.wait_ge(s_oz, g)
                    nc.vector.scalar_tensor_tensor(out=oh, in0=cin[b], scalar=0.0, in1=bcj(r1[:, bass.ds(g * J, J)]),
                                                   op0=ALU.max, op1=ALU.mult).then_inc(s_oh, 1)
                    if not isinstance(g, int) or g >= 2:
                        dve.wait_ge(s_oo, g - 1)
                    nc.vector.tensor_tensor(ox1[b], cin[b], bcj(m1[:, bass.ds(g * J, J)]), ALU.add).then_inc(s_ox1, 1)
                    dve.wait_ge(s_oub, g + 1)
                    dve.wait_ge(s_oh, g + 1)
                    if not isinstance(g, int) or g >= 2:
                        dve.wait_ge(s_oabs, g - 1)
                        dve.wait_ge(s_osp, g - 1)
                    nc.vector.tensor_tensor(oz[b], oub[b], oh, ALU.add).then_inc(s_oz, 1)

                def back(u, b, g):
                    dve.wait_ge(s_ol, g + 1)
                    dve.wait_ge(s_oo, g)
                    nc.vector.scalar_tensor_tensor(out=osp, in0=oz[b], scalar=0.0, in1=ol[b], op0=ALU.max,
                                                   op1=ALU.add).then_inc(s_osp, 1)
                    dve.wait_ge(s_osp, g + 1)
                    if not isinstance(g, int) or g >= 2:
                        dve.wait_ge(s_ost[b], 16 * u)
                    nc.vector.tensor_tensor(oo[b], osp, ox1[b], ALU.add).then_inc(s_oo, 1)

                front(0, 0, 0)
                front(0, 1, 1)
                back(0, 0, 0)
                front(1, 0, 2)
                back(0, 1, 1)
                with dve.Fori(1, CHUNKS // 2) as u:
                    front(u, 1, u * 2 + 1)
                    back(u, 0, u * 2)
                    front(u + 1, 0, u * 2 + 2)
                    back(u, 1, u * 2 + 1)
                back(CHUNKS // 2, 0, CHUNKS - 1)

            @block.scalar
            def _(act):
                def chunk(u, b, g):
                    act.wait_ge(s_oz, g + 1)
                    act.wait_ge(s_oexp, g)
                    nc.scalar.activation(oabs, oz[b], ACT.Abs).then_inc(s_oabs, 1)
                    act.wait_ge(s_oabs, g + 1)
                    act.wait_ge(s_ol, g)
                    nc.scalar.activation(oexp, oabs, ACT.Exp, scale=-1.0).then_inc(s_oexp, 1)
                    act.wait_ge(s_oexp, g + 1)
                    if not isinstance(g, int) or g >= 2:
                        act.wait_ge(s_osp, g - 1)
                    nc.scalar.activation(ol[b], oexp, ACT.Ln, bias=1.0).then_inc(s_ol, 1)

                chunk(0, 0, 0)
                chunk(0, 1, 1)
                with act.Fori(1, CHUNKS // 2) as u:
                    for b in range(2):
                        chunk(u, b, u * 2 + b)
                chunk(CHUNKS // 2, 0, CHUNKS - 1)


_WEIGHTS = {"mW1": "L0_gnn_mW1", "mb1": "L0_gnn_mb1", "mW2": "L0_gnn_mW2", "mb2": "L0_gnn_mb2",
            "uW1": "L0_gnn_uW1", "ub1": "L0_gnn_ub1", "uW2": "L0_gnn_uW2", "ub2": "L0_gnn_ub2",
            "W": "L1_gnn_W", "b": "L1_gnn_b", "g1": "L1_gnn_g1", "b1": "L1_gnn_b1", "g2": "L1_gnn_g2",
            "b2": "L1_gnn_b2"}


def kernel(**inputs):
    import numpy as np
    import concourse.bacc as bacc
    from concourse.bass_utils import run_bass_kernel_spmd

    a = {k: np.asarray(v) for k, v in inputs.items()}

    def padded(v, rows, fill=None):
        more = np.zeros((rows - v.shape[0],) + v.shape[1:], v.dtype)
        if fill is not None:
            more[:] = fill
        return np.concatenate([v, more])

    x = padded(a["x"], NP)
    pad_rows = np.arange(NP + GROUP, ROWS)
    key_src, key_dst = padded(a["src"], EP, pad_rows), padded(a["dst"], EP, pad_rows)
    cols = lambda v: np.ascontiguousarray(v.reshape(TILES, P).T)
    ends = [padded(a[k], EP).reshape(GROUPS, GT, P) for k in ("src", "dst")]
    arrays = {
        "x": x,
        "gat": np.ascontiguousarray(np.stack(ends, axis=-1).transpose(0, 2, 1, 3).reshape(GROUPS, P, 2 * GT)),
        "key_cols": np.ascontiguousarray(np.stack([cols(key_dst), cols(key_src)], axis=1)),
        "key_src": key_src,
        "key_dst": key_dst,
        "ea32_t": np.ascontiguousarray(padded(a["edge_attr_32"], EP).T),
        "ea64_t": np.ascontiguousarray(padded(a["edge_attr_64"], EP).T),
        "edge_w": padded(a["edge_weight"], EP),
        "edge_w_cols": cols(padded(a["edge_weight"], EP)),
        "node_w": np.ascontiguousarray(
            padded(a["node_vec"], NP).reshape(CHUNKS, P, J).transpose(1, 0, 2).reshape(P, CHUNKS * J)),
    }
    nc = bacc.Bacc("TRN2", target_bir_lowering=False, num_devices=1)

    def given(name, v):
        return nc.dram_tensor(name, v.shape, mybir.dt.from_np(v.dtype), kind="ExternalInput").ap()

    aps = {k: given(k, v) for k, v in arrays.items()}
    weights = {}
    for short, name in _WEIGHTS.items():
        arrays[f"w_{short}"] = np.ascontiguousarray(a[name])
        weights[short] = given(f"w_{short}", arrays[f"w_{short}"])
    out = nc.dram_tensor("out", [NP, D], F32, kind="ExternalOutput").ap()
    build(nc, **aps, weights=weights, out=out)
    r = run_bass_kernel_spmd(nc, [arrays], core_ids=[0])
    return r.results[0]["out"][:N]
```

```python
from contextlib import ExitStack

import concourse.bass as bass
from concourse import mybir

F32 = mybir.dt.float32
I32 = mybir.dt.int32
BF16 = mybir.dt.bfloat16
ALU = mybir.AluOpType
ACT = mybir.ActivationFunctionType
X = mybir.AxisListType.X

P = 128
D = 64
H = 128
N = 100000
E = 25000
J = 16
CHUNK = P * J
CHUNKS = -(-N // CHUNK)
NP = CHUNKS * CHUNK
GT = 4
GROUP = GT * P
GROUPS = -(-E // GROUP)
EP = GROUPS * GROUP
TILES = GROUPS * GT
DUMP = NP
ROWS = NP + GROUP + (EP - E)
EPS = 1e-5
assert GROUPS % 2 == 1 and CHUNKS % 2 == 1


def known(n):
    return isinstance(n, int)


def await_(eng, s, n):
    if not known(n) or n > 0:
        eng.wait_ge(s, n)


def build(nc, x, gat, key_cols, key_src, key_dst, ea32_t, ea64_t, edge_w, edge_w_cols, node_w, weights, out):
    agg = nc.dram_tensor("agg_table", [ROWS, D], F32, kind="Internal").ap()
    ctab = nc.dram_tensor("centred_table", [NP, D], F32, kind="Internal").ap()
    nsum = nc.dram_tensor("nsum_table", [ROWS, D], F32, kind="Internal").ap()
    chunk_rows = lambda t, g: t[bass.ds(g * CHUNK, CHUNK), :].rearrange("(p j) d -> p j d", j=J)

    ctx = ExitStack()
    with ctx:
        def sb(name, shape, dt=F32):
            return ctx.enter_context(nc.sbuf_tensor(name, shape, dt))

        def sem(name):
            return ctx.enter_context(nc.semaphore(name))

        bank = [ctx.enter_context(nc.psum_tensor(f"bank{i}", [P, 512], F32)) for i in range(8)]

        ident = sb("ident", [P, P])
        ones = sb("ones", [P, P])
        before = sb("before", [P, GROUP])
        dump_rows = sb("dump_rows", [P, GT], I32)
        dump_f = sb("dump_f", [P, GT])
        eps_col = sb("eps_col", [P, 1])
        zero_col = sb("zero_col", [P, 1])
        w_msg1 = sb("w_msg1", [P, H])
        w_msg1e = sb("w_msg1e", [32, H])
        b_msg1 = sb("b_msg1", [P, 1])
        w_msg2 = sb("w_msg2", [P, D])
        b_msg2 = sb("b_msg2", [P, D])
        w_upd1 = sb("w_upd1", [P, H])
        b_upd1 = sb("b_upd1", [P, 1])
        w_upd2 = sb("w_upd2", [P, D + 1])
        b_upd2 = sb("b_upd2", [P, D + 1])
        w_gate = sb("w_gate", [P, H])
        w_gatee = sb("w_gatee", [D, H])
        b_gate = sb("b_gate", [P, 1])
        g1c = sb("g1c", [P, 1])
        b1c = sb("b1c", [P, 1])
        g2r = sb("g2r", [P, D])
        b2r = sb("b2r", [P, D])
        ew = sb("ew", [P, TILES])
        nw = sb("nw", [P, CHUNKS * J])
        wsum = sb("wsum", [P, 2])
        wsum_inv = sb("wsum_inv", [P, 2])
        m1 = sb("m1", [P, CHUNKS * J])
        r1 = sb("r1", [P, CHUNKS * J])
        s1 = sb("s1", [P, 2])
        s2 = sb("s2", [P, 2])
        tbuf = sb("tbuf", [P, 2, GROUP])
        tmp = sb("tmp", [P, 8])
        A1 = sb("A1", [P, 1])
        B1 = sb("B1", [P, 1])
        A2 = sb("A2", [P, D])
        B2 = sb("B2", [P, D])
        row_tmp = sb("row_tmp", [P, 4, D])
        kcols = sb("kcols", [P, 2, TILES], I32)
        kcolf = sb("kcolf", [P, 2, TILES])
        gidx = sb("gidx", [P, 2, 2 * GT], I32)
        krow = sb("krow", [P, 2, GROUP], I32)
        eat = sb("eat", [D, 2, GROUP])
        ewr = sb("ewr", [P, 2, GROUP])
        gx = sb("gx", [P, 2, 2 * GT, D])
        gc = sb("gc", [P, 2 * GT, D])
        gsq = sb("gsq", [P, 2 * GT, D])
        gh = sb("gh", [P, 2 * GT, D])
        gst = sb("gst", [P, 4, 2 * GT])
        ght = sb("ght", [P, GROUP])
        ghid = sb("ghid", [P, GROUP])
        gmsg = sb("gmsg", [P, GT, D])
        gtot = sb("gtot", [P, 2, GT, D])
        same = sb("same", [P, 2, GT, GROUP], BF16)
        same_out = sb("same_out", [P, GROUP])
        gparts = sb("gparts", [P, 3, GT, D], BF16)
        grest = sb("grest", [P, GT, D])
        sidx_src = sb("sidx_src", [P, TILES], I32)
        cnt = sb("cnt", [P, 2, GT])
        dumped = sb("dumped", [P, 2, GT])
        sidx = sb("sidx", [P, 2, GT], I32)
        big = sb("big", [P, EP])

        def area(i, shape=(J, D)):
            n = shape[0] * shape[1]
            return big[:, i * J * D:i * J * D + n].rearrange("p (a b) -> p a b", b=shape[1])

        zeros = big[:, 0:4 * J * D]

        chain = [sem("dve_chain"), 0]

        s_const = sem("s_const")
        s_cpool = sem("s_cpool")
        s_zero = sem("s_zero")
        s_zagg = sem("s_zagg")
        s_znsum = sem("s_znsum")
        ZSTEP = P * 4 * J * D
        ZEROED = 16 * -(-ROWS * D // ZSTEP)
        s_wdve = sem("s_wdve")
        s_wpe = sem("s_wpe")
        NLOADS = 18
        with nc.Block() as block:
            @block.sync
            def _(sp):
                W = weights
                loads = [
                    (w_msg1[:, :], W["mW1"][0:P, :]), (w_msg1e[:, :], W["mW1"][P:P + 32, :]),
                    (b_msg1[:, :], W["mb1"].rearrange("(p a) -> p a", a=1)), (w_msg2[:, :], W["mW2"]),
                    (b_msg2[:, :], W["mb2"].partition_broadcast(P)), (w_upd1[:, :], W["uW1"]),
                    (b_upd1[:, :], W["ub1"].rearrange("(p a) -> p a", a=1)), (w_upd2[:, 0:D], W["uW2"]),
                    (b_upd2[:, 0:D], W["ub2"].partition_broadcast(P)), (w_gate[:, :], W["W"][0:P, :]),
                    (w_gatee[:, :], W["W"][P:P + D, :]), (b_gate[:, :], W["b"].rearrange("(p a) -> p a", a=1)),
                    (g1c[:, :], W["g1"].rearrange("(p a) -> p a", a=1)),
                    (b1c[:, :], W["b1"].rearrange("(p a) -> p a", a=1)),
                    (g2r[:, :], W["g2"].partition_broadcast(P)), (b2r[:, :], W["b2"].partition_broadcast(P)),
                    (ew[:, :], edge_w_cols), (nw[:, :], node_w),
                ]
                assert len(loads) == NLOADS
                for dst, src in loads:
                    sp.dma_start(dst, src).then_inc(s_const, 16)
                sp.dma_start(kcols[:, :, :], key_cols).then_inc(s_const, 16)
                sp.wait_ge(s_zero, 1)
                for table, zeroed in ((agg, s_zagg), (nsum, s_znsum)):
                    flat = table.rearrange("r d -> (r d)")
                    at = 0
                    while at < ROWS * D:
                        n = min(ZSTEP, ROWS * D - at)
                        sp.dma_start(flat[at:at + n].rearrange("(p f) -> p f", p=P),
                                     zeros[:, 0:n // P]).then_inc(zeroed, 16)
                        at += n

            @block.gpsimd
            def _(pool):
                nc.gpsimd.memset(ident[:, :], 0.0).then_inc(s_cpool, 1)
                nc.gpsimd.memset(before[:, :], 1.0).then_inc(s_cpool, 1)
                nc.gpsimd.memset(ones[:, :], 1.0).then_inc(s_cpool, 1)
                pool.wait_ge(s_cpool, 3)
                nc.gpsimd.affine_select(out=ident[:, :], in_=ident[:, :], compare_op=ALU.not_equal, fill=1.0,
                                        base=0, pattern=[[-1, P]], channel_multiplier=1).then_inc(s_cpool, 1)
                nc.gpsimd.affine_select(out=before[:, :], in_=before[:, :], compare_op=ALU.is_gt, fill=0.0,
                                        base=GROUP - P, pattern=[[-1, GROUP]],
                                        channel_multiplier=1).then_inc(s_cpool, 1)
                nc.gpsimd.iota(dump_rows[:, :], pattern=[[P, GT]], base=DUMP,
                               channel_multiplier=1).then_inc(s_cpool, 1)

            @block.vector
            def _(dve):
                def link(ins):
                    chain[1] += 1
                    ins.then_inc(chain[0], 1)
                    dve.wait_ge(chain[0], chain[1])

                nc.vector.memset(zeros, 0.0).then_inc(s_zero, 1)
                nc.vector.memset(eps_col[:, :], EPS)
                nc.vector.memset(zero_col[:, :], 0.0)
                nc.vector.memset(s1[:, :], 0.0)
                nc.vector.memset(s2[:, :], 0.0)
                dve.wait_ge(s_cpool, 6)
                nc.vector.tensor_copy(dump_f[:, :], dump_rows[:, :])
                dve.wait_ge(s_const, 16 * (NLOADS + 1))
                nc.vector.tensor_copy(kcolf[:, :, :], kcols[:, :, :])
                for w in (w_upd2, b_upd2):
                    link(nc.vector.reduce_sum(tmp[:, 0:1], w[:, 0:D], X))
                    link(nc.vector.tensor_scalar(w[:, D:D + 1], tmp[:, 0:1], 1.0 / D, None, ALU.mult))
                    link(nc.vector.tensor_scalar(w[:, 0:D], w[:, 0:D], w[:, D:D + 1], None, ALU.subtract))
                nc.vector.reduce_sum(tmp[:, 1:2], ew[:, :], X).then_inc(s_wdve, 1)
                nc.vector.reduce_sum(tmp[:, 2:3], nw[:, :], X).then_inc(s_wdve, 1)
                dve.wait_ge(s_wpe, 1)
                link(nc.vector.tensor_copy(wsum[:, :], bank[0][:, 0:2]))
                link(nc.vector.reciprocal(wsum_inv[:, :], wsum[:, :]))

            @block.tensor
            def _(pe):
                pe.wait_ge(s_cpool, 6)
                pe.wait_ge(s_wdve, 2)
                nc.tensor.matmul(bank[0][:, 0:2], ones[:, :], tmp[:, 1:3], start=True, stop=True).then_inc(s_wpe, 1)

        s_step = sem("s_step")
        s_gi = [sem(f"s_gi{b}") for b in range(2)]
        s_gx = [sem(f"s_gx{b}") for b in range(2)]
        s_c = sem("s_c")
        s_sq = sem("s_sq")
        s_ss = sem("s_ss")
        s_std = sem("s_std")
        s_h = sem("s_h")
        s_tp = sem("s_tp")
        s_ht = sem("s_ht")
        s_m1 = sem("s_m1")
        s_hid = sem("s_hid")
        s_m2 = sem("s_m2")
        s_msg = sem("s_msg")
        s_hi = sem("s_hi")
        s_rest = sem("s_rest")
        s_mid = sem("s_mid")
        s_low = sem("s_low")
        s_same = sem("s_same")
        s_sidx = sem("s_sidx")
        s_m3 = sem("s_m3")
        s_tot = sem("s_tot")
        s_sc = sem("s_sc")
        HALF = GT // 2 * P
        with nc.Block() as block:
            @block.sync
            def _(sp):
                def load(u, b, g):
                    await_(sp, s_gx[b], 128 * u)
                    await_(sp, s_same, g - 1)
                    await_(sp, s_m1, g - 1)
                    sp.dma_start(gidx[:, b, :], gat[bass.ds(g, 1), :, :].rearrange("g p c -> (g p) c")).then_inc(s_gi[b], 16)
                    sp.dma_start(krow[:, b, :], key_dst[bass.ds(g * GROUP, GROUP)].partition_broadcast(P)).then_inc(s_gi[b], 16)
                    sp.dma_start(eat[0:32, b, :], ea32_t[:, bass.ds(g * GROUP, GROUP)]).then_inc(s_gi[b], 16)

                load(0, 0, 0)
                load(0, 1, 1)
                with sp.Fori(1, GROUPS // 2) as u:
                    for b in range(2):
                        load(u, b, u * 2 + b)
                load(GROUPS // 2, 0, GROUPS - 1)

            @block.gpsimd
            def _(pool):
                def gather(b, ks):
                    for k in ks:
                        pool.indirect_dma_start(gx[:, b, k, :], None, x,
                                                bass.IndirectOffsetOnAxis(gidx[:, b, k:k + 1], 0)).then_inc(s_gx[b], 16)

                def gather_start(u, b, g):
                    pool.wait_ge(s_gi[b], 48 * (u + 1))
                    await_(pool, s_c, g - 1)
                    pool.sem_inc(s_step, 1)

                def scatter(b, g, pair):
                    if pair == 0:
                        pool.wait_ge(s_tot, g + 1)
                        pool.wait_ge(s_sidx, g + 1)
                    await_(pool, s_sc, 64 * g + 32 * pair)
                    pool.sem_inc(s_step, 1)
                    for k in (2 * pair, 2 * pair + 1):
                        pool.indirect_dma_start(agg, bass.IndirectOffsetOnAxis(sidx[:, b, k:k + 1], 0),
                                                gtot[:, b, k, :], None, compute_op=ALU.add).then_inc(s_sc, 16)

                def both(u, b, g):
                    gather_start(u, b, g)
                    gather(b, range(4))
                    scatter(1 - b, g - 3, 0)
                    gather(b, range(4, 8))
                    scatter(1 - b, g - 3, 1)

                for g in range(3):
                    gather_start(g // 2, g % 2, g)
                    gather(g % 2, range(8))
                pool.wait_ge(s_zagg, ZEROED)
                both(1, 1, 3)
                with pool.Fori(2, GROUPS // 2) as u:
                    for b in range(2):
                        both(u, b, u * 2 + b)
                both(GROUPS // 2, 0, GROUPS - 1)
                for g in range(GROUPS - 3, GROUPS):
                    scatter(g % 2, g, 0)
                    scatter(g % 2, g, 1)
                pool.wait_ge(s_sc, 64 * GROUPS)

            @block.vector
            def _(dve):
                ch = sem("p1_chain")
                chm = sem("p1_msg_chain")
                PER = 8

                def msg(b, g):
                    dve.wait_ge(s_m2, g + 1)
                    nc.vector.tensor_tensor(
                        gmsg[:, :, :], bank[2][:, 0:GT * D].rearrange("p (j d) -> p j d", d=D),
                        b_msg2[:, :].rearrange("p (a d) -> p a d", a=1).to_broadcast([P, GT, D]), ALU.add).then_inc(s_msg, 1)
                    await_(dve, s_sc, 64 * (g - 1))
                    nc.vector.tensor_tensor(sidx[:, b, :], dumped[:, b, :],
                                            kcolf[:, 0, bass.ds(g * GT, GT)], ALU.max).then_inc(s_sidx, 1)
                    dve.wait_ge(s_hi, g + 1)
                    nc.vector.tensor_tensor(grest[:, :, :], gmsg[:, :, :], gparts[:, 0, :, :], ALU.subtract).then_inc(s_rest, 1)

                def low(g):
                    dve.wait_ge(s_mid, g + 1)
                    nc.vector.tensor_tensor(gparts[:, 2, :, :], grest[:, :, :], gparts[:, 1, :, :], ALU.subtract).then_inc(s_low, 1)

                def group(u, b, g):
                    k = [0]

                    def link(ins):
                        k[0] += 1
                        ins.then_inc(ch, 1)
                        dve.wait_ge(ch, g * PER + k[0])

                    rows = gx[:, b, :, :]
                    bc = lambda i: gst[:, i, :].rearrange("p (a o) -> p a o", o=1).to_broadcast([P, 2 * GT, D])
                    dve.wait_ge(s_gx[b], 128 * (u + 1))
                    await_(dve, s_h, g)
                    link(nc.vector.reduce_sum(gst[:, 0, :], rows, X))
                    link(nc.vector.tensor_scalar(gst[:, 1, :], gst[:, 0, :], 1.0 / D, None, ALU.mult))
                    nc.vector.tensor_tensor(gc[:, :, :], rows, bc(1), ALU.subtract).then_inc(s_c, 1)
                    dve.wait_ge(s_gi[b], 48 * (u + 1))
                    await_(dve, s_m3, g - 1)
                    for j in range(GT):
                        half = HALF * (j // 2)
                        ins = nc.vector.tensor_scalar(same[:, b, j, 0:HALF], krow[:, b, half:half + HALF],
                                                      kcolf[:, 0, bass.ds(g * GT + j, 1)], None, ALU.is_equal)
                    ins.then_inc(s_same, 1)
                    dve.wait_ge(s_sq, g + 1)
                    nc.vector.reduce_sum(gst[:, 2, :], gsq[:, :, :], X).then_inc(s_ss, 1)
                    dve.wait_ge(s_same, g + 1)
                    for j in range(GT):
                        n = P * (j % 2 + 1)
                        link(nc.vector.tensor_tensor_reduce(
                            out=same_out[:, 0:n], in0=same[:, b, j, 0:n], in1=before[:, GROUP - n:GROUP], scale=1.0,
                            scalar=0.0, op0=ALU.mult, op1=ALU.add, accum_out=cnt[:, 0, j:j + 1]))
                    dve.wait_ge(s_std, g + 1)
                    link(nc.vector.reciprocal(gst[:, 0, :], gst[:, 3, :]))
                    link(nc.vector.scalar_tensor_tensor(out=dumped[:, b, :], in0=cnt[:, 0, :], scalar=1.0,
                                                        in1=dump_f[:, :], op0=ALU.min, op1=ALU.mult))
                    await_(dve, s_tp, g)
                    nc.vector.scalar_tensor_tensor(out=gh[:, :, :], in0=gc[:, :, :], scalar=0.0, in1=bc(0),
                                                   op0=ALU.max, op1=ALU.mult).then_inc(s_h, 1)
                    if not known(g) or g > 0:
                        msg(1 - b, g - 1)
                        low(g - 1)
                    assert k[0] == PER

                group(0, 0, 0)
                group(0, 1, 1)
                with dve.Fori(1, GROUPS // 2) as u:
                    for b in range(2):
                        group(u, b, u * 2 + b)
                group(GROUPS // 2, 0, GROUPS - 1)
                msg(0, GROUPS - 1)
                low(GROUPS - 1)

            @block.scalar
            def _(act):
                def late(b, g):
                    act.wait_ge(s_msg, g + 1)
                    await_(act, s_m3, g)
                    nc.scalar.copy(gparts[:, 0, :, :], gmsg[:, :, :]).then_inc(s_hi, 1)
                    act.wait_ge(s_rest, g + 1)
                    nc.scalar.copy(gparts[:, 1, :, :], grest[:, :, :]).then_inc(s_mid, 1)

                def sums(b, g):
                    act.wait_ge(s_m3, g + 1)
                    await_(act, s_sc, 64 * (g - 1))
                    nc.scalar.copy(gtot[:, b, :, :], bank[3][:, 0:GT * D].rearrange("p (j d) -> p j d", d=D)).then_inc(s_tot, 1)

                def group(u, b, g):
                    act.wait_ge(s_c, g + 1)
                    await_(act, s_ss, g)
                    nc.scalar.activation(gsq[:, :, :], gc[:, :, :], ACT.Square).then_inc(s_sq, 1)
                    act.wait_ge(s_ss, g + 1)
                    nc.scalar.activation(gst[:, 3, :], gst[:, 2, :], ACT.Sqrt, bias=eps_col[:, :],
                                         scale=1.0 / D).then_inc(s_std, 1)
                    if not known(g) or g > 0:
                        late(1 - b, g - 1)
                    act.wait_ge(s_tp, g + 1)
                    nc.scalar.copy(ght[:, :], bank[0][:, :]).then_inc(s_ht, 1)
                    if not known(g) or g > 0:
                        sums(1 - b, g - 1)
                    act.wait_ge(s_m1, g + 1)
                    nc.scalar.activation(ghid[:, :], bank[1][:, :], ACT.Relu, bias=b_msg1[:, :]).then_inc(s_hid, 1)

                group(0, 0, 0)
                group(0, 1, 1)
                with act.Fori(1, GROUPS // 2) as u:
                    for b in range(2):
                        group(u, b, u * 2 + b)
                group(GROUPS // 2, 0, GROUPS - 1)
                late(0, GROUPS - 1)
                sums(0, GROUPS - 1)

            @block.tensor
            def _(pe):
                def sums(b, g):
                    pe.wait_ge(s_low, g + 1)
                    pe.wait_ge(s_same, g + 1)
                    await_(pe, s_tot, g)
                    for i in range(GT):
                        pair = i // 2 * 2
                        for j in (pair, pair + 1):
                            for part in range(3):
                                ins = nc.tensor.matmul(bank[3][:, D * i:D * i + D],
                                                       same[:, b, j, P * (i - pair):P * (i - pair) + P],
                                                       gparts[:, part, j, :], start=(j == pair and part == 0),
                                                       stop=(j == pair + 1 and part == 2))
                    ins.then_inc(s_m3, 1)

                def group(u, b, g):
                    pe.wait_ge(s_h, g + 1)
                    for j in range(GT):
                        ins = nc.tensor.transpose(bank[0][:, P * j:P * j + P],
                                                  gh[:, 2 * j:2 * j + 2, :].rearrange("p a d -> p (a d)"), ident[:, :])
                    ins.then_inc(s_tp, 1)
                    if not known(g) or g > 0:
                        sums(1 - b, g - 1)
                    pe.wait_ge(s_ht, g + 1)
                    nc.tensor.matmul(bank[1][:, :], w_msg1[:, :], ght[:, :], start=True, stop=False)
                    nc.tensor.matmul(bank[1][:, :], w_msg1e[:, :], eat[0:32, b, :], start=False, stop=True).then_inc(s_m1, 1)
                    pe.wait_ge(s_hid, g + 1)
                    for j in range(GT):
                        ins = nc.tensor.matmul(bank[2][:, D * j:D * j + D], ghid[:, P * j:P * j + P], w_msg2[:, :],
                                               start=True, stop=True)
                    ins.then_inc(s_m2, 1)

                group(0, 0, 0)
                group(0, 1, 1)
                with pe.Fori(1, GROUPS // 2) as u:
                    for b in range(2):
                        group(u, b, u * 2 + b)
                group(GROUPS // 2, 0, GROUPS - 1)
                sums(0, GROUPS - 1)

        s_nx = [sem(f"s_nx{b}") for b in range(2)]
        s_na = [sem(f"s_na{b}") for b in range(2)]
        s_nm = sem("s_nm")
        s_nc = sem("s_nc")
        s_ncb = sem("s_ncb")
        s_nsq = sem("s_nsq")
        s_nss = sem("s_nss")
        s_nstd = sem("s_nstd")
        s_nh = sem("s_nh")
        s_ntp = sem("s_ntp")
        s_nht = sem("s_nht")
        s_nm1 = sem("s_nm1")
        s_nhid = sem("s_nhid")
        s_nm2 = sem("s_nm2")
        s_nc1 = sem("s_nc1")
        s_nsq1 = sem("s_nsq1")
        s_nss1 = sem("s_nss1")
        s_nstd1 = sem("s_nstd1")
        s_nst = [sem(f"s_nst{b}") for b in range(2)]
        xin = [area(0), area(1)]
        c0 = [area(2), area(3)]
        c0b = [area(4), area(5)]
        c1 = [area(6), area(7)]
        sq0 = area(8)
        sq1 = area(9)
        ha = [area(10, (J, 2 * D)), area(12, (J, 2 * D))]
        hts = [area(14, (4, P))[:, :, :], area(15, (4, P))]
        hids = [area(16, (4, P)), area(17, (4, P))]
        nst = big[:, 18 * J * D:18 * J * D + 16 * J].rearrange("p (a j) -> p a j", j=J)
        Q = J // 4
        LAST = CHUNKS - 1

        def periods(eng, period):
            period(0, 0, 0)
            period(0, 1, 1)
            with eng.Fori(1, CHUNKS // 2 - 1) as u:
                for b in range(2):
                    period(u, b, u * 2 + b)
            for g in range(CHUNKS - 3, CHUNKS):
                period(g // 2, g % 2, g)

        def has(g):
            return not known(g) or 0 <= g <= LAST

        with nc.Block() as block:
            @block.sync
            def _(sp):
                def load_x(u, b, g):
                    await_(sp, s_nc, g - 1)
                    sp.dma_start(xin[b], chunk_rows(x, g)).then_inc(s_nx[b], 16)

                def load_a(u, b, g):
                    await_(sp, s_ntp, 4 * (g - 1))
                    sp.dma_start(ha[b][:, :, D:2 * D], chunk_rows(agg, g)).then_inc(s_na[b], 16)

                def period(u, b, g):
                    if has(g + 3):
                        load_x(None, 1 - b, g + 3)
                    if has(g + 2):
                        load_a(None, b, g + 2)
                    sp.wait_ge(s_nc1, 4 * (g + 1))
                    sp.dma_start(chunk_rows(ctab, g), c1[b]).then_inc(s_nst[b], 16)

                sp.wait_ge(s_znsum, ZEROED)
                load_x(0, 0, 0)
                load_x(0, 1, 1)
                load_a(0, 0, 0)
                load_a(0, 1, 1)
                load_x(1, 0, 2)
                periods(sp, period)
                sp.wait_ge(s_nst[0], 16 * (CHUNKS // 2 + 1))
                sp.wait_ge(s_nst[1], 16 * (CHUNKS // 2))

            bcj = lambda ap: ap.rearrange("p (a o) -> p a o", o=1).to_broadcast([P, J, D])
            bcd = lambda ap: ap.rearrange("p (a d) -> p a d", a=1).to_broadcast([P, J, D])

            @block.gpsimd
            def _(pool):
                def centre(b, g):
                    pool.wait_ge(s_nm, g + 1)
                    await_(pool, s_nh, g - 1)
                    await_(pool, s_ncb, g - 1)
                    nc.gpsimd.tensor_tensor(c0[b], xin[b], bcj(nst[:, 1 + b, :]), ALU.subtract).then_inc(s_nc, 1)

                def bias(b, g):
                    pool.wait_ge(s_nc, g + 1)
                    await_(pool, s_nc1, 4 * (g - 1))
                    nc.gpsimd.tensor_tensor(c0b[b], c0[b], bcd(b_upd2[:, 0:D]), ALU.add).then_inc(s_ncb, 1)

                def period(u, b, g):
                    if has(g + 2):
                        centre(b, g + 2)
                    if has(g + 1):
                        bias(1 - b, g + 1)

                centre(0, 0)
                bias(0, 0)
                centre(1, 1)
                periods(pool, period)

            @block.vector
            def _(dve):
                cha = sem("p2_chain_sum")
                chb = sem("p2_chain_h")

                def mean(u, b, g):
                    dve.wait_ge(s_nx[b], 16 * (u + 1))
                    await_(dve, s_nm, g)
                    nc.vector.reduce_sum(nst[:, 0, :], xin[b], X).then_inc(cha, 1)
                    dve.wait_ge(cha, g + 1)
                    await_(dve, s_nc, g - 1)
                    nc.vector.tensor_scalar(m1[:, bass.ds(g * J, J)], nst[:, 0, :], 1.0 / D, None, ALU.mult)
                    nc.vector.tensor_scalar(nst[:, 1 + b, :], nst[:, 0, :], 1.0 / D, None, ALU.mult).then_inc(s_nm, 1)

                def squares(g):
                    dve.wait_ge(s_nsq, g + 1)
                    nc.vector.reduce_sum(nst[:, 3, :], sq0, X).then_inc(s_nss, 1)

                def norm(b, g):
                    dve.wait_ge(s_nstd, g + 1)
                    nc.vector.reciprocal(nst[:, 5, :], nst[:, 4, :]).then_inc(chb, 1)
                    dve.wait_ge(chb, g + 1)
                    await_(dve, s_ntp, 4 * (g - 1))
                    nc.vector.scalar_tensor_tensor(out=ha[b][:, :, 0:D], in0=c0[b], scalar=0.0, in1=bcj(nst[:, 5, :]),
                                                   op0=ALU.max, op1=ALU.mult).then_inc(s_nh, 1)

                def update(u, b, g, q):
                    o = bank[4 + q][:, 0:Q * (D + 1)].rearrange("p (j e) -> p j e", e=D + 1)
                    dve.wait_ge(s_nm2, 4 * g + q + 1)
                    if q == 0:
                        dve.wait_ge(s_ncb, g + 1)
                        await_(dve, s_nst[b], 16 * u)
                        await_(dve, s_nsq1, g - 1)
                    means = m1[:, bass.ds(g * J + Q * q, Q)]
                    nc.vector.scalar_tensor_tensor(
                        out=means, in0=o[:, :, D:D + 1].rearrange("p j o -> p (j o)"),
                        scalar=b_upd2[:, D:D + 1], in1=means, op0=ALU.add, op1=ALU.add)
                    nc.vector.tensor_tensor(c1[b][:, Q * q:Q * q + Q, :], c0b[b][:, Q * q:Q * q + Q, :],
                                            o[:, :, 0:D], ALU.add).then_inc(s_nc1, 1)

                def variance(g):
                    dve.wait_ge(s_nsq1, g + 1)
                    nc.vector.reduce_sum(nst[:, 7, :], sq1, X).then_inc(s_nss1, 1)

                def scale(g):
                    dve.wait_ge(s_nstd1, g + 1)
                    nc.vector.reciprocal(r1[:, bass.ds(g * J, J)], nst[:, 8, :])

                def period(u, b, g):
                    if has(g + 1):
                        norm(1 - b, g + 1)
                    update(u, b, g, 0)
                    if has(g - 1):
                        variance(g - 1)
                    update(u, b, g, 1)
                    if has(g + 2):
                        squares(g + 2)
                    update(u, b, g, 2)
                    if has(g + 3):
                        mean(u + 1 + b, 1 - b, g + 3)
                    if has(g - 1):
                        scale(g - 1)
                    update(u, b, g, 3)

                mean(0, 0, 0)
                squares(0)
                norm(0, 0)
                mean(0, 1, 1)
                squares(1)
                mean(1, 0, 2)
                periods(dve, period)
                variance(LAST)
                scale(LAST)

            @block.scalar
            def _(act):
                def squares(b, g):
                    act.wait_ge(s_nc, g + 1)
                    await_(act, s_nss, g)
                    nc.scalar.activation(sq0, c0[b], ACT.Square).then_inc(s_nsq, 1)

                def deviation(g):
                    act.wait_ge(s_nss, g + 1)
                    nc.scalar.activation(nst[:, 4, :], nst[:, 3, :], ACT.Sqrt, bias=eps_col[:, :], scale=1.0 / D).then_inc(s_nstd, 1)

                def turned(g, q):
                    act.wait_ge(s_ntp, 4 * g + q + 1)
                    nc.scalar.copy(hts[q % 2], bank[q % 2][:, :].rearrange("p (a b) -> p a b", b=P)).then_inc(s_nht, 1)

                def hidden(g, q):
                    act.wait_ge(s_nm1, 4 * g + q + 1)
                    nc.scalar.activation(hids[q % 2], bank[2 + q % 2][:, :].rearrange("p (a b) -> p a b", b=P), ACT.Relu,
                                         bias=b_upd1[:, :]).then_inc(s_nhid, 1)

                def squares1(b, g):
                    act.wait_ge(s_nc1, 4 * (g + 1))
                    await_(act, s_nss1, g)
                    nc.scalar.activation(sq1, c1[b], ACT.Square).then_inc(s_nsq1, 1)

                def deviation1(g):
                    act.wait_ge(s_nss1, g + 1)
                    nc.scalar.activation(nst[:, 8, :], nst[:, 7, :], ACT.Sqrt, bias=eps_col[:, :], scale=1.0 / D).then_inc(s_nstd1, 1)

                def period(u, b, g):
                    turned(g, 2)
                    hidden(g, 1)
                    if has(g - 1):
                        squares1(1 - b, g - 1)
                    turned(g, 3)
                    hidden(g, 2)
                    if has(g + 2):
                        squares(b, g + 2)
                    if has(g + 1):
                        turned(g + 1, 0)
                    hidden(g, 3)
                    if has(g - 1):
                        deviation1(g - 1)
                    if has(g + 1):
                        turned(g + 1, 1)
                        hidden(g + 1, 0)
                    if has(g + 2):
                        deviation(g + 2)

                squares(0, 0)
                deviation(0)
                squares(1, 1)
                deviation(1)
                turned(0, 0)
                turned(0, 1)
                hidden(0, 0)
                periods(act, period)
                squares1(0, LAST)
                deviation1(LAST)

            @block.tensor
            def _(pe):
                def turn(b, g, q):
                    await_(pe, s_nht, 4 * g + q - 1)
                    for j in range(4):
                        ins = nc.tensor.transpose(bank[q % 2][:, P * j:P * j + P], ha[b][:, 4 * q + j, :], ident[:, :])
                    ins.then_inc(s_ntp, 1)

                def first(g, q):
                    pe.wait_ge(s_nht, 4 * g + q + 1)
                    await_(pe, s_nhid, 4 * g + q - 1)
                    nc.tensor.matmul(bank[2 + q % 2][:, :], w_upd1[:, :], hts[q % 2].rearrange("p a b -> p (a b)"),
                                     start=True, stop=True).then_inc(s_nm1, 1)

                def second(g, q):
                    pe.wait_ge(s_nhid, 4 * g + q + 1)
                    await_(pe, s_nc1, 4 * (g - 1) + q + 1)
                    for j in range(4):
                        ins = nc.tensor.matmul(bank[4 + q][:, (D + 1) * j:(D + 1) * (j + 1)], hids[q % 2][:, j, :],
                                               w_upd2[:, :], start=True, stop=True)
                    ins.then_inc(s_nm2, 1)

                def start(u, b, g):
                    pe.wait_ge(s_nh, g + 1)
                    pe.wait_ge(s_na[b], 16 * (u + 1))

                def period(u, b, g):
                    turn(b, g, 2)
                    first(g, 1)
                    second(g, 0)
                    turn(b, g, 3)
                    first(g, 2)
                    second(g, 1)
                    if has(g + 1):
                        start(u + b, 1 - b, g + 1)
                        turn(1 - b, g + 1, 0)
                    first(g, 3)
                    second(g, 2)
                    if has(g + 1):
                        turn(1 - b, g + 1, 1)
                        first(g + 1, 0)
                    second(g, 3)

                start(0, 0, 0)
                turn(0, 0, 0)
                turn(0, 0, 1)
                first(0, 0)
                periods(pe, period)

        s_ei = [sem(f"s_ei{b}") for b in range(2)]
        s_ew = [sem(f"s_ew{b}") for b in range(2)]
        s_ex = [sem(f"s_ex{b}") for b in range(2)]
        s_esq = sem("s_esq")
        s_ess = sem("s_ess")
        s_estd = sem("s_estd")
        s_eh = sem("s_eh")
        s_etp = sem("s_etp")
        s_eht = sem("s_eht")
        s_em = sem("s_em")
        s_et = sem("s_et")
        s_es = sem("s_es")
        s_esame = sem("s_esame")
        with nc.Block() as block:
            @block.sync
            def _(sp):
                def load(u, b, g):
                    await_(sp, s_ex[b], 128 * u)
                    await_(sp, s_em, g - 1)
                    await_(sp, s_esame, g - 1)
                    sp.dma_start(gidx[:, b, :], gat[bass.ds(g, 1), :, :].rearrange("g p c -> (g p) c")).then_inc(s_ei[b], 16)
                    sp.dma_start(eat[:, b, :], ea64_t[:, bass.ds(g * GROUP, GROUP)]).then_inc(s_ei[b], 16)
                    sp.dma_start(krow[:, b, :], key_src[bass.ds(g * GROUP, GROUP)].partition_broadcast(P)).then_inc(s_ei[b], 16)
                    await_(sp, s_es, g - 1)
                    sp.dma_start(ewr[:, b, :], edge_w[bass.ds(g * GROUP, GROUP)].partition_broadcast(P)).then_inc(s_ew[b], 16)

                load(0, 0, 0)
                load(0, 1, 1)
                with sp.Fori(1, GROUPS // 2) as u:
                    for b in range(2):
                        load(u, b, u * 2 + b)
                load(GROUPS // 2, 0, GROUPS - 1)

            @block.gpsimd
            def _(pool):
                def gather(u, b, g):
                    pool.wait_ge(s_ei[b], 48 * (u + 1))
                    await_(pool, s_eh, g - 1)
                    pool.sem_inc(s_step, 1)
                    for k in range(2 * GT):
                        pool.indirect_dma_start(gx[:, b, k, :], None, ctab,
                                                bass.IndirectOffsetOnAxis(gidx[:, b, k:k + 1], 0)).then_inc(s_ex[b], 16)

                gather(0, 0, 0)
                gather(0, 1, 1)
                with pool.Fori(1, GROUPS // 2) as u:
                    for b in range(2):
                        gather(u, b, u * 2 + b)
                gather(GROUPS // 2, 0, GROUPS - 1)

            @block.vector
            def _(dve):
                ch = sem("p3_chain")
                cht = sem("p3_sum_chain")
                PER = 6

                def sums(u, b, g):
                    dve.wait_ge(s_et, g + 1)
                    dve.wait_ge(s_ew[b], 16 * (u + 1))
                    t = tbuf[:, b, :]
                    await_(dve, cht, 2 * g)
                    nc.vector.tensor_tensor_reduce(out=same_out[:, :], in0=t, in1=ewr[:, b, :], scale=1.0,
                                                   scalar=s1[:, 1 - b:2 - b], op0=ALU.mult, op1=ALU.add,
                                                   accum_out=s1[:, b:b + 1]).then_inc(cht, 1)
                    dve.wait_ge(cht, 2 * g + 1)
                    nc.vector.tensor_tensor_reduce(out=ghid[:, :], in0=same_out[:, :], in1=t, scale=1.0,
                                                   scalar=s2[:, 1 - b:2 - b], op0=ALU.mult, op1=ALU.add,
                                                   accum_out=s2[:, b:b + 1]).then_inc(cht, 1)
                    nc.vector.tensor_copy(big[:, bass.ds(g * GROUP, GROUP)], t).then_inc(s_es, 1)

                def group(u, b, g):
                    k = [0]

                    def link(ins):
                        k[0] += 1
                        ins.then_inc(ch, 1)
                        dve.wait_ge(ch, g * PER + k[0])

                    dve.wait_ge(s_esq, g + 1)
                    nc.vector.reduce_sum(gst[:, 2, :], gsq[:, :, :], X).then_inc(s_ess, 1)
                    dve.wait_ge(s_ei[b], 48 * (u + 1))
                    for j in range(GT):
                        ins = nc.vector.tensor_scalar(same[:, 0, j, :], krow[:, b, :], kcolf[:, 1, bass.ds(g * GT + j, 1)],
                                                      None, ALU.is_equal)
                    ins.then_inc(s_esame, 1)
                    dve.wait_ge(s_estd, g + 1)
                    link(nc.vector.reciprocal(gst[:, 0, :], gst[:, 3, :]))
                    await_(dve, s_etp, g)
                    nc.vector.scalar_tensor_tensor(
                        out=gh[:, :, :], in0=gx[:, b, :, :], scalar=0.0,
                        in1=gst[:, 0, :].rearrange("p (a o) -> p a o", o=1).to_broadcast([P, 2 * GT, D]),
                        op0=ALU.max, op1=ALU.mult).then_inc(s_eh, 1)
                    if not known(g) or g > 0:
                        sums(u - 1 + b, 1 - b, g - 1)
                        dve.wait_ge(cht, 2 * g)
                    dve.wait_ge(s_esame, g + 1)
                    for j in range(GT):
                        n = P * (j + 1)
                        link(nc.vector.tensor_tensor_reduce(
                            out=same_out[:, 0:n], in0=same[:, 0, j, 0:n], in1=before[:, GROUP - n:GROUP], scale=1.0,
                            scalar=0.0, op0=ALU.mult, op1=ALU.add, accum_out=cnt[:, 0, j:j + 1]))
                    link(nc.vector.scalar_tensor_tensor(out=cnt[:, 1, :], in0=cnt[:, 0, :], scalar=1.0,
                                                        in1=dump_f[:, :], op0=ALU.min, op1=ALU.mult))
                    nc.vector.tensor_tensor(sidx_src[:, bass.ds(g * GT, GT)], cnt[:, 1, :],
                                            kcolf[:, 1, bass.ds(g * GT, GT)], ALU.max)
                    assert k[0] == PER

                group(0, 0, 0)
                group(0, 1, 1)
                with dve.Fori(1, GROUPS // 2) as u:
                    for b in range(2):
                        group(u, b, u * 2 + b)
                group(GROUPS // 2, 0, GROUPS - 1)
                sums(GROUPS // 2, 0, GROUPS - 1)

            @block.scalar
            def _(act):
                def kept(b, g):
                    act.wait_ge(s_em, g + 1)
                    await_(act, s_es, g - 1)
                    nc.scalar.activation(tbuf[:, b, :], bank[1][:, :], ACT.Identity, bias=b_gate[:, :]).then_inc(s_et, 1)

                def group(u, b, g):
                    act.wait_ge(s_ex[b], 128 * (u + 1))
                    await_(act, s_ess, g)
                    nc.scalar.activation(gsq[:, :, :], gx[:, b, :, :], ACT.Square).then_inc(s_esq, 1)
                    act.wait_ge(s_ess, g + 1)
                    nc.scalar.activation(gst[:, 3, :], gst[:, 2, :], ACT.Sqrt, bias=eps_col[:, :], scale=1.0 / D).then_inc(s_estd, 1)
                    if not known(g) or g > 0:
                        kept(1 - b, g - 1)
                    act.wait_ge(s_etp, g + 1)
                    nc.scalar.copy(ght[:, :], bank[0][:, :]).then_inc(s_eht, 1)

                group(0, 0, 0)
                group(0, 1, 1)
                with act.Fori(1, GROUPS // 2) as u:
                    for b in range(2):
                        group(u, b, u * 2 + b)
                group(GROUPS // 2, 0, GROUPS - 1)
                kept(0, GROUPS - 1)

            @block.tensor
            def _(pe):
                def group(u, b, g):
                    pe.wait_ge(s_eh, g + 1)
                    for j in range(GT):
                        ins = nc.tensor.transpose(bank[0][:, P * j:P * j + P],
                                                  gh[:, 2 * j:2 * j + 2, :].rearrange("p a d -> p (a d)"), ident[:, :])
                    ins.then_inc(s_etp, 1)
                    pe.wait_ge(s_eht, g + 1)
                    pe.wait_ge(s_ei[b], 48 * (u + 1))
                    await_(pe, s_et, g)
                    nc.tensor.matmul(bank[1][:, :], w_gate[:, :], ght[:, :], start=True, stop=False)
                    nc.tensor.matmul(bank[1][:, :], w_gatee[:, :], eat[:, b, :], start=False, stop=True).then_inc(s_em, 1)

                group(0, 0, 0)
                group(0, 1, 1)
                with pe.Fori(1, GROUPS // 2) as u:
                    for b in range(2):
                        group(u, b, u * 2 + b)
                group(GROUPS // 2, 0, GROUPS - 1)

        s_var = sem("s_var")
        s_sd = sem("s_sd")
        with nc.Block() as block:
            @block.vector
            def _(dve):
                ch = sem("p3b_chain")
                k = [0]

                def link(ins):
                    k[0] += 1
                    ins.then_inc(ch, 1)
                    dve.wait_ge(ch, k[0])

                link(nc.vector.tensor_copy(tmp[:, 0:1], s1[:, 0:1]))
                link(nc.vector.tensor_copy(tmp[:, 1:2], s2[:, 0:1]))
                link(nc.vector.tensor_scalar(tmp[:, 2:4], tmp[:, 0:2], wsum_inv[:, 0:1], None, ALU.mult))
                link(nc.vector.tensor_tensor(tmp[:, 4:5], tmp[:, 2:3], tmp[:, 2:3], ALU.mult))
                link(nc.vector.tensor_tensor(tmp[:, 5:6], tmp[:, 3:4], tmp[:, 4:5], ALU.subtract))
                nc.vector.tensor_scalar(tmp[:, 5:6], tmp[:, 5:6], 0.0, None, ALU.max).then_inc(s_var, 1)
                dve.wait_ge(s_sd, 1)
                link(nc.vector.reciprocal(tmp[:, 7:8], tmp[:, 6:7]))
                link(nc.vector.tensor_tensor(A1[:, :], g1c[:, :], tmp[:, 7:8], ALU.mult))
                link(nc.vector.tensor_tensor(tmp[:, 0:1], A1[:, :], tmp[:, 2:3], ALU.mult))
                link(nc.vector.tensor_tensor(B1[:, :], b1c[:, :], tmp[:, 0:1], ALU.subtract))

            @block.scalar
            def _(act):
                act.wait_ge(s_var, 1)
                nc.scalar.activation(tmp[:, 6:7], tmp[:, 5:6], ACT.Sqrt, bias=eps_col[:, :]).then_inc(s_sd, 1)

        s_fi = [sem(f"s_fi{b}") for b in range(2)]
        s_fg = sem("s_fg")
        s_ftp = sem("s_ftp")
        s_fe = sem("s_fe")
        s_fa = sem("s_fa")
        s_fea = sem("s_fea")
        s_fl = sem("s_fl")
        s_fmsg = sem("s_fmsg")
        s_fhi = sem("s_fhi")
        s_frest = sem("s_frest")
        s_fmid = sem("s_fmid")
        s_flow = sem("s_flow")
        s_fsame = sem("s_fsame")
        s_fsidx = sem("s_fsidx")
        s_fm = sem("s_fm")
        s_ftot = sem("s_ftot")
        s_fsc = sem("s_fsc")
        exp_f = gsq[:, 0:GT, :]
        abs_c = gsq[:, GT:2 * GT, :]
        exp_c = gx[:, 0, 0:GT, :]
        log_c = gx[:, 0, GT:2 * GT, :]
        one_f = gh[:, 0:GT, :]
        sig_f = gh[:, GT:2 * GT, :]
        soft_c = gc[:, 0:GT, :]
        halves = [bank[b][:, :].rearrange("p (j e) -> p j e", e=P) for b in range(2)]
        with nc.Block() as block:
            @block.sync
            def _(sp):
                def load(u, b, g):
                    await_(sp, s_fsame, g - 1)
                    sp.dma_start(krow[:, b, :], key_src[bass.ds(g * GROUP, GROUP)].partition_broadcast(P)).then_inc(s_fi[b], 16)

                load(0, 0, 0)
                load(0, 1, 1)
                with sp.Fori(1, GROUPS // 2) as u:
                    for b in range(2):
                        load(u, b, u * 2 + b)
                load(GROUPS // 2, 0, GROUPS - 1)

            @block.gpsimd
            def _(pool):
                def scatter(b, g):
                    pool.wait_ge(s_ftot, g + 1)
                    pool.wait_ge(s_fsidx, g + 1)
                    await_(pool, s_fsc, 64 * g)
                    pool.sem_inc(s_step, 1)
                    for k in range(GT):
                        pool.indirect_dma_start(nsum, bass.IndirectOffsetOnAxis(sidx[:, b, k:k + 1], 0),
                                                gtot[:, b, k, :], None, compute_op=ALU.add).then_inc(s_fsc, 16)

                scatter(0, 0)
                scatter(1, 1)
                with pool.Fori(1, GROUPS // 2) as u:
                    for b in range(2):
                        scatter(b, u * 2 + b)
                scatter(0, GROUPS - 1)
                pool.wait_ge(s_fsc, 64 * GROUPS)

            @block.vector
            def _(dve):
                ch = sem("p4_chain")
                PER = 3

                def group(u, b, g):
                    k = [0]

                    def link(ins):
                        k[0] += 1
                        ins.then_inc(ch, 1)
                        dve.wait_ge(ch, g * PER + k[0])

                    dve.wait_ge(s_fi[b], 16 * (u + 1))
                    await_(dve, s_fm, g - 1)
                    for j in range(GT):
                        ins = nc.vector.tensor_scalar(same[:, b, j, :], krow[:, b, :], kcolf[:, 1, bass.ds(g * GT + j, 1)],
                                                      None, ALU.is_equal)
                    ins.then_inc(s_fsame, 1)
                    await_(dve, s_fsc, 64 * (g - 1))
                    nc.vector.tensor_copy(sidx[:, b, :], sidx_src[:, bass.ds(g * GT, GT)]).then_inc(s_fsidx, 1)
                    dve.wait_ge(s_fe, g + 1)
                    link(nc.vector.tensor_scalar(one_f, exp_f, 1.0, None, ALU.add))
                    link(nc.vector.reciprocal(sig_f, one_f))
                    dve.wait_ge(s_fl, g + 1)
                    link(nc.vector.scalar_tensor_tensor(out=soft_c, in0=halves[b][:, :, D:P], scalar=0.0, in1=log_c,
                                                        op0=ALU.max, op1=ALU.add))
                    nc.vector.tensor_tensor(gmsg[:, :, :], soft_c, sig_f, ALU.mult).then_inc(s_fmsg, 1)
                    dve.wait_ge(s_fhi, g + 1)
                    nc.vector.tensor_tensor(grest[:, :, :], gmsg[:, :, :], gparts[:, 0, :, :], ALU.subtract).then_inc(s_frest, 1)
                    dve.wait_ge(s_fmid, g + 1)
                    nc.vector.tensor_tensor(gparts[:, 2, :, :], grest[:, :, :], gparts[:, 1, :, :], ALU.subtract).then_inc(s_flow, 1)
                    assert k[0] == PER

                group(0, 0, 0)
                group(0, 1, 1)
                with dve.Fori(1, GROUPS // 2) as u:
                    for b in range(2):
                        group(u, b, u * 2 + b)
                group(GROUPS // 2, 0, GROUPS - 1)

            @block.scalar
            def _(act):
                affs = [ght, ghid]

                def gate(b, g):
                    await_(act, s_ftp, g - 1)
                    nc.scalar.activation(affs[b][:, :], big[:, bass.ds(g * GROUP, GROUP)], ACT.Identity, bias=B1[:, :],
                                         scale=A1[:, :]).then_inc(s_fg, 1)

                def sums(b, g):
                    act.wait_ge(s_fm, g + 1)
                    await_(act, s_fsc, 64 * (g - 1))
                    nc.scalar.copy(gtot[:, b, :, :], bank[3][:, 0:GT * D].rearrange("p (j d) -> p j d", d=D)).then_inc(s_ftot, 1)

                def group(u, b, g):
                    if not known(g) or g + 1 < GROUPS:
                        gate(1 - b, g + 1)
                    act.wait_ge(s_ftp, g + 1)
                    await_(act, s_fmsg, g)
                    nc.scalar.activation(exp_f, halves[b][:, :, 0:D], ACT.Exp, scale=-1.0).then_inc(s_fe, 1)
                    nc.scalar.activation(abs_c, halves[b][:, :, D:P], ACT.Abs).then_inc(s_fa, 1)
                    act.wait_ge(s_fa, g + 1)
                    nc.scalar.activation(exp_c, abs_c, ACT.Exp, scale=-1.0).then_inc(s_fea, 1)
                    act.wait_ge(s_fea, g + 1)
                    nc.scalar.activation(log_c, exp_c, ACT.Ln, bias=1.0).then_inc(s_fl, 1)
                    if not known(g) or g > 0:
                        sums(1 - b, g - 1)
                    act.wait_ge(s_fmsg, g + 1)
                    nc.scalar.copy(gparts[:, 0, :, :], gmsg[:, :, :]).then_inc(s_fhi, 1)
                    act.wait_ge(s_frest, g + 1)
                    nc.scalar.copy(gparts[:, 1, :, :], grest[:, :, :]).then_inc(s_fmid, 1)

                nc.scalar.preload_act_table_set("natural_log_exp_and_others")
                gate(0, 0)
                group(0, 0, 0)
                group(0, 1, 1)
                with act.Fori(1, GROUPS // 2) as u:
                    for b in range(2):
                        group(u, b, u * 2 + b)
                group(GROUPS // 2, 0, GROUPS - 1)
                sums(0, GROUPS - 1)

            @block.tensor
            def _(pe):
                affs = [ght, ghid]

                def turn(b, g):
                    pe.wait_ge(s_fg, g + 1)
                    await_(pe, s_fmsg, g - 1)
                    for j in range(GT):
                        ins = nc.tensor.transpose(bank[b][:, P * j:P * j + P], affs[b][:, P * j:P * j + P], ident[:, :])
                    ins.then_inc(s_ftp, 1)

                def group(u, b, g):
                    if not known(g) or g + 1 < GROUPS:
                        turn(1 - b, g + 1)
                    pe.wait_ge(s_flow, g + 1)
                    pe.wait_ge(s_fsame, g + 1)
                    await_(pe, s_ftot, g)
                    for i in range(GT):
                        for j in range(GT):
                            for part in range(3):
                                ins = nc.tensor.matmul(bank[3][:, D * i:D * i + D], same[:, b, j, P * i:P * i + P],
                                                       gparts[:, part, j, :], start=(j == 0 and part == 0),
                                                       stop=(j == GT - 1 and part == 2))
                    ins.then_inc(s_fm, 1)

                turn(0, 0)
                group(0, 0, 0)
                group(0, 1, 1)
                with pe.Fori(1, GROUPS // 2) as u:
                    for b in range(2):
                        group(u, b, u * 2 + b)
                group(GROUPS // 2, 0, GROUPS - 1)

        s_vx = [sem(f"s_vx{b}") for b in range(2)]
        s_vcp = sem("s_vcp")
        s_vsq = sem("s_vsq")
        s_vm = sem("s_vm")
        s_vend = sem("s_vend")
        s_vd = sem("s_vd")
        s_vbc = sem("s_vbc")
        s_vvar = sem("s_vvar")
        s_vsd = sem("s_vsd")
        vin = [area(0), area(1)]
        vw = [nst[:, 0, :], nst[:, 1, :]]
        pair = [area(3, (J, 2 * D)), area(5, (J, 2 * D))]
        with nc.Block() as block:
            @block.sync
            def _(sp):
                def load(u, b, g):
                    if not isinstance(g, int) or g >= 2:
                        sp.wait_ge(s_vcp, g - 1)
                        sp.wait_ge(s_vsq, g - 1)
                        sp.wait_ge(s_vm, g - 1)
                    sp.dma_start(vin[b], chunk_rows(nsum, g)).then_inc(s_vx[b], 16)
                    sp.dma_start(vw[b], node_w[:, bass.ds(g * J, J)]).then_inc(s_vx[b], 16)

                load(0, 0, 0)
                load(0, 1, 1)
                with sp.Fori(1, CHUNKS // 2) as u:
                    for b in range(2):
                        load(u, b, u * 2 + b)
                load(CHUNKS // 2, 0, CHUNKS - 1)

            @block.scalar
            def _(act):
                def chunk(u, b, g):
                    act.wait_ge(s_vx[b], 32 * (u + 1))
                    if not isinstance(g, int) or g >= 2:
                        act.wait_ge(s_vm, g - 1)
                    nc.scalar.activation(pair[b][:, :, D:2 * D], vin[b], ACT.Square).then_inc(s_vsq, 1)

                chunk(0, 0, 0)
                chunk(0, 1, 1)
                with act.Fori(1, CHUNKS // 2) as u:
                    for b in range(2):
                        chunk(u, b, u * 2 + b)
                chunk(CHUNKS // 2, 0, CHUNKS - 1)
                act.wait_ge(s_vvar, 1)
                nc.scalar.activation(row_tmp[:, 2, :], row_tmp[:, 1, :], ACT.Sqrt, bias=eps_col[:, :]).then_inc(s_vsd, 1)

            @block.vector
            def _(dve):
                def chunk(u, b, g):
                    dve.wait_ge(s_vx[b], 32 * (u + 1))
                    if not isinstance(g, int) or g >= 2:
                        dve.wait_ge(s_vm, g - 1)
                    nc.vector.tensor_copy(pair[b][:, :, 0:D], vin[b]).then_inc(s_vcp, 1)

                chunk(0, 0, 0)
                chunk(0, 1, 1)
                with dve.Fori(1, CHUNKS // 2) as u:
                    for b in range(2):
                        chunk(u, b, u * 2 + b)
                chunk(CHUNKS // 2, 0, CHUNKS - 1)
                ch = sem("p5_chain")
                k = [0]

                def link(ins):
                    k[0] += 1
                    ins.then_inc(ch, 1)
                    dve.wait_ge(ch, k[0])

                dve.wait_ge(s_vend, 1)
                link(nc.vector.tensor_scalar(tmp[:, 0:1], bank[0][:, 0:1], wsum_inv[:, 1:2], None, ALU.mult))
                nc.vector.tensor_scalar(same_out[:, 0:P], ident[:, :], tmp[:, 0:1], None, ALU.mult).then_inc(s_vd, 1)
                dve.wait_ge(s_vbc, 1)
                link(nc.vector.tensor_copy(row_tmp[:, 0, :], bank[1][:, 0:D]))
                link(nc.vector.tensor_tensor(row_tmp[:, 3, :], row_tmp[:, 0, :], row_tmp[:, 0, :], ALU.mult))
                link(nc.vector.tensor_tensor(row_tmp[:, 1, :], bank[1][:, D:2 * D], row_tmp[:, 3, :], ALU.subtract))
                nc.vector.tensor_scalar(row_tmp[:, 1, :], row_tmp[:, 1, :], 0.0, None, ALU.max).then_inc(s_vvar, 1)
                dve.wait_ge(s_vsd, 1)
                link(nc.vector.reciprocal(row_tmp[:, 3, :], row_tmp[:, 2, :]))
                link(nc.vector.tensor_tensor(A2[:, :], g2r[:, :], row_tmp[:, 3, :], ALU.mult))
                link(nc.vector.tensor_tensor(row_tmp[:, 1, :], A2[:, :], row_tmp[:, 0, :], ALU.mult))
                link(nc.vector.tensor_tensor(B2[:, :], b2r[:, :], row_tmp[:, 1, :], ALU.subtract))

            @block.tensor
            def _(pe):
                def chunk(u, b, g):
                    pe.wait_ge(s_vcp, g + 1)
                    pe.wait_ge(s_vsq, g + 1)
                    pe.wait_ge(s_vx[b], 32 * (u + 1))
                    for j in range(J):
                        first = isinstance(g, int) and g == 0 and j == 0
                        last = isinstance(g, int) and g == CHUNKS - 1 and j == J - 1
                        ins = nc.tensor.matmul(bank[0][:, 0:1], pair[b][:, j, :], vw[b][:, j:j + 1], start=first,
                                               stop=last)
                    ins.then_inc(s_vm, 1)
                    return ins

                chunk(0, 0, 0)
                chunk(0, 1, 1)
                with pe.Fori(1, CHUNKS // 2) as u:
                    for b in range(2):
                        chunk(u, b, u * 2 + b)
                chunk(CHUNKS // 2, 0, CHUNKS - 1)
                pe.wait_ge(s_vm, CHUNKS)
                pe.nop().then_inc(s_vend, 1)
                pe.wait_ge(s_vd, 1)
                nc.tensor.matmul(bank[1][:, 0:P], ones[:, :], same_out[:, 0:P], start=True, stop=True).then_inc(s_vbc, 1)

        s_ox = [sem(f"s_oxin{b}") for b in range(2)]
        s_oh = sem("s_oh")
        s_ou = sem("s_ou")
        s_oub = sem("s_oub")
        s_oz = sem("s_oz")
        s_osp = sem("s_osp")
        s_oabs = sem("s_oabs")
        s_oexp = sem("s_oexp")
        s_ol = sem("s_ol")
        s_ox1 = sem("s_ox1")
        s_oo = sem("s_oo")
        s_ost = [sem(f"s_ost{b}") for b in range(2)]
        cin = [area(0), area(1)]
        sin = [area(2), area(3)]
        oh = area(4)
        ou = area(5)
        oub = [area(6), area(7)]
        oz = [area(8), area(9)]
        oabs = area(10)
        oexp = area(11)
        ol = [area(12), area(13)]
        ox1 = [area(14), area(15)]
        osp = area(16)
        oo = [area(18), area(19)]
        with nc.Block() as block:
            bcj = lambda ap: ap.rearrange("p (a o) -> p a o", o=1).to_broadcast([P, J, D])
            bcd = lambda ap: ap.rearrange("p (a d) -> p a d", a=1).to_broadcast([P, J, D])

            @block.sync
            def _(sp):
                def load(u, b, g):
                    if not isinstance(g, int) or g >= 2:
                        sp.wait_ge(s_ox1, g - 1)
                        sp.wait_ge(s_ou, g - 1)
                        sp.wait_ge(s_oh, g - 1)
                    sp.dma_start(cin[b], chunk_rows(ctab, g)).then_inc(s_ox[b], 16)
                    sp.dma_start(sin[b], chunk_rows(nsum, g)).then_inc(s_ox[b], 16)

                def store(b, g):
                    sp.wait_ge(s_oo, g + 1)
                    sp.dma_start(chunk_rows(out, g), oo[b]).then_inc(s_ost[b], 16)

                load(0, 0, 0)
                load(0, 1, 1)
                with sp.Fori(0, CHUNKS // 2 - 1) as u:
                    for b in range(2):
                        load(u + 1, b, u * 2 + b + 2)
                        store(b, u * 2 + b)
                load(CHUNKS // 2, 0, CHUNKS - 1)
                for b in range(3):
                    store(b % 2, CHUNKS - 3 + b)
                sp.wait_ge(s_ost[0], 16 * (CHUNKS // 2 + 1))
                sp.wait_ge(s_ost[1], 16 * (CHUNKS // 2))

            @block.gpsimd
            def _(pool):
                def chunk(u, b, g):
                    pool.wait_ge(s_ox[b], 32 * (u + 1))
                    nc.gpsimd.tensor_tensor(ou, sin[b], bcd(A2[:, :]), ALU.mult).then_inc(s_ou, 1)
                    pool.wait_ge(s_ou, g + 1)
                    if not isinstance(g, int) or g >= 2:
                        pool.wait_ge(s_oz, g - 1)
                    nc.gpsimd.tensor_tensor(oub[b], ou, bcd(B2[:, :]), ALU.add).then_inc(s_oub, 1)
                    pool.wait_ge(s_oub, g + 1)

                chunk(0, 0, 0)
                chunk(0, 1, 1)
                with pool.Fori(1, CHUNKS // 2) as u:
                    for b in range(2):
                        chunk(u, b, u * 2 + b)
                chunk(CHUNKS // 2, 0, CHUNKS - 1)

            @block.vector
            def _(dve):
                def front(u, b, g):
                    dve.wait_ge(s_ox[b], 32 * (u + 1))
                    dve.wait_ge(s_oz, g)
                    nc.vector.scalar_tensor_tensor(out=oh, in0=cin[b], scalar=0.0, in1=bcj(r1[:, bass.ds(g * J, J)]),
                                                   op0=ALU.max, op1=ALU.mult).then_inc(s_oh, 1)
                    if not isinstance(g, int) or g >= 2:
                        dve.wait_ge(s_oo, g - 1)
                    nc.vector.tensor_tensor(ox1[b], cin[b], bcj(m1[:, bass.ds(g * J, J)]), ALU.add).then_inc(s_ox1, 1)
                    dve.wait_ge(s_oub, g + 1)
                    dve.wait_ge(s_oh, g + 1)
                    if not isinstance(g, int) or g >= 2:
                        dve.wait_ge(s_oabs, g - 1)
                        dve.wait_ge(s_osp, g - 1)
                    nc.vector.tensor_tensor(oz[b], oub[b], oh, ALU.add).then_inc(s_oz, 1)

                def back(u, b, g):
                    dve.wait_ge(s_ol, g + 1)
                    dve.wait_ge(s_oo, g)
                    nc.vector.scalar_tensor_tensor(out=osp, in0=oz[b], scalar=0.0, in1=ol[b], op0=ALU.max,
                                                   op1=ALU.add).then_inc(s_osp, 1)
                    dve.wait_ge(s_osp, g + 1)
                    if not isinstance(g, int) or g >= 2:
                        dve.wait_ge(s_ost[b], 16 * u)
                    nc.vector.tensor_tensor(oo[b], osp, ox1[b], ALU.add).then_inc(s_oo, 1)

                front(0, 0, 0)
                front(0, 1, 1)
                back(0, 0, 0)
                front(1, 0, 2)
                back(0, 1, 1)
                with dve.Fori(1, CHUNKS // 2) as u:
                    front(u, 1, u * 2 + 1)
                    back(u, 0, u * 2)
                    front(u + 1, 0, u * 2 + 2)
                    back(u, 1, u * 2 + 1)
                back(CHUNKS // 2, 0, CHUNKS - 1)

            @block.scalar
            def _(act):
                def chunk(u, b, g):
                    act.wait_ge(s_oz, g + 1)
                    act.wait_ge(s_oexp, g)
                    nc.scalar.activation(oabs, oz[b], ACT.Abs).then_inc(s_oabs, 1)
                    act.wait_ge(s_oabs, g + 1)
                    act.wait_ge(s_ol, g)
                    nc.scalar.activation(oexp, oabs, ACT.Exp, scale=-1.0).then_inc(s_oexp, 1)
                    act.wait_ge(s_oexp, g + 1)
                    if not isinstance(g, int) or g >= 2:
                        act.wait_ge(s_osp, g - 1)
                    nc.scalar.activation(ol[b], oexp, ACT.Ln, bias=1.0).then_inc(s_ol, 1)

                nc.scalar.preload_act_table_set("natural_log_exp_and_others")
                chunk(0, 0, 0)
                chunk(0, 1, 1)
                with act.Fori(1, CHUNKS // 2) as u:
                    for b in range(2):
                        chunk(u, b, u * 2 + b)
                chunk(CHUNKS // 2, 0, CHUNKS - 1)


_WEIGHTS = {"mW1": "L0_gnn_mW1", "mb1": "L0_gnn_mb1", "mW2": "L0_gnn_mW2", "mb2": "L0_gnn_mb2",
            "uW1": "L0_gnn_uW1", "ub1": "L0_gnn_ub1", "uW2": "L0_gnn_uW2", "ub2": "L0_gnn_ub2",
            "W": "L1_gnn_W", "b": "L1_gnn_b", "g1": "L1_gnn_g1", "b1": "L1_gnn_b1", "g2": "L1_gnn_g2",
            "b2": "L1_gnn_b2"}


def kernel(**inputs):
    import numpy as np
    import concourse.bacc as bacc
    from concourse.bass_utils import run_bass_kernel_spmd

    a = {k: np.asarray(v) for k, v in inputs.items()}

    def padded(v, rows, fill=None):
        more = np.zeros((rows - v.shape[0],) + v.shape[1:], v.dtype)
        if fill is not None:
            more[:] = fill
        return np.concatenate([v, more])

    x = padded(a["x"], NP)
    pad_rows = np.arange(NP + GROUP, ROWS)
    key_src, key_dst = padded(a["src"], EP, pad_rows), padded(a["dst"], EP, pad_rows)
    cols = lambda v: np.ascontiguousarray(v.reshape(TILES, P).T)
    ends = [padded(a[k], EP).reshape(GROUPS, GT, P) for k in ("src", "dst")]
    arrays = {
        "x": x,
        "gat": np.ascontiguousarray(np.stack(ends, axis=-1).transpose(0, 2, 1, 3).reshape(GROUPS, P, 2 * GT)),
        "key_cols": np.ascontiguousarray(np.stack([cols(key_dst), cols(key_src)], axis=1)),
        "key_src": key_src,
        "key_dst": key_dst,
        "ea32_t": np.ascontiguousarray(padded(a["edge_attr_32"], EP).T),
        "ea64_t": np.ascontiguousarray(padded(a["edge_attr_64"], EP).T),
        "edge_w": padded(a["edge_weight"], EP),
        "edge_w_cols": cols(padded(a["edge_weight"], EP)),
        "node_w": np.ascontiguousarray(
            padded(a["node_vec"], NP).reshape(CHUNKS, P, J).transpose(1, 0, 2).reshape(P, CHUNKS * J)),
    }
    nc = bacc.Bacc("TRN2", target_bir_lowering=False, num_devices=1)

    def given(name, v):
        return nc.dram_tensor(name, v.shape, mybir.dt.from_np(v.dtype), kind="ExternalInput").ap()

    aps = {k: given(k, v) for k, v in arrays.items()}
    weights = {}
    for short, name in _WEIGHTS.items():
        arrays[f"w_{short}"] = np.ascontiguousarray(a[name])
        weights[short] = given(f"w_{short}", arrays[f"w_{short}"])
    out = nc.dram_tensor("out", [NP, D], F32, kind="ExternalOutput").ap()
    build(nc, **aps, weights=weights, out=out)
    r = run_bass_kernel_spmd(nc, [arrays], core_ids=[0])
    return r.results[0]["out"][:N]
```

```python
from contextlib import ExitStack

import concourse.bass as bass
from concourse import mybir

F32 = mybir.dt.float32
I32 = mybir.dt.int32
BF16 = mybir.dt.bfloat16
ALU = mybir.AluOpType
ACT = mybir.ActivationFunctionType
X = mybir.AxisListType.X

P = 128
D = 64
H = 128
N = 100000
E = 25000
J = 16
CHUNK = P * J
CHUNKS = -(-N // CHUNK)
NP = CHUNKS * CHUNK
GT = 4
GROUP = GT * P
GROUPS = -(-E // GROUP)
EP = GROUPS * GROUP
TILES = GROUPS * GT
DUMP = NP
ROWS = NP + GROUP + (EP - E)
EPS = 1e-5
assert GROUPS % 2 == 1 and CHUNKS % 2 == 1


def known(n):
    return isinstance(n, int)


def await_(eng, s, n):
    if not known(n) or n > 0:
        eng.wait_ge(s, n)


def build(nc, x, gat, key_cols, key_src, key_dst, ea32_t, ea64_t, edge_w, edge_w_cols, node_w, weights, out):
    agg = nc.dram_tensor("agg_table", [ROWS, D], F32, kind="Internal").ap()
    ctab = nc.dram_tensor("centred_table", [NP, D], F32, kind="Internal").ap()
    nsum = nc.dram_tensor("nsum_table", [ROWS, D], F32, kind="Internal").ap()
    chunk_rows = lambda t, g: t[bass.ds(g * CHUNK, CHUNK), :].rearrange("(p j) d -> p j d", j=J)

    ctx = ExitStack()
    with ctx:
        def sb(name, shape, dt=F32):
            return ctx.enter_context(nc.sbuf_tensor(name, shape, dt))

        def sem(name):
            return ctx.enter_context(nc.semaphore(name))

        bank = [ctx.enter_context(nc.psum_tensor(f"bank{i}", [P, 512], F32)) for i in range(8)]

        ident = sb("ident", [P, P])
        ones = sb("ones", [P, P])
        before = sb("before", [P, GROUP])
        dump_rows = sb("dump_rows", [P, GT], I32)
        dump_f = sb("dump_f", [P, GT])
        eps_col = sb("eps_col", [P, 1])
        w_msg1 = sb("w_msg1", [P, H])
        w_msg1e = sb("w_msg1e", [32, H])
        b_msg1 = sb("b_msg1", [P, 1])
        w_msg2 = sb("w_msg2", [P, D])
        b_msg2 = sb("b_msg2", [P, D])
        w_upd1 = sb("w_upd1", [P, H])
        b_upd1 = sb("b_upd1", [P, 1])
        w_upd2 = sb("w_upd2", [P, D + 1])
        b_upd2 = sb("b_upd2", [P, D + 1])
        w_gate = sb("w_gate", [P, H])
        w_gatee = sb("w_gatee", [D, H])
        b_gate = sb("b_gate", [P, 1])
        g1c = sb("g1c", [P, 1])
        b1c = sb("b1c", [P, 1])
        g2r = sb("g2r", [P, D])
        b2r = sb("b2r", [P, D])
        ew = sb("ew", [P, TILES])
        nw = sb("nw", [P, CHUNKS * J])
        wsum = sb("wsum", [P, 2])
        wsum_inv = sb("wsum_inv", [P, 2])
        m1 = sb("m1", [P, CHUNKS * J])
        r1 = sb("r1", [P, CHUNKS * J])
        s1 = sb("s1", [P, 2])
        s2 = sb("s2", [P, 2])
        tbuf = sb("tbuf", [P, 2, GROUP])
        tmp = sb("tmp", [P, 8])
        A1 = sb("A1", [P, 1])
        B1 = sb("B1", [P, 1])
        A2 = sb("A2", [P, 2, D])
        B2 = sb("B2", [P, 2, D])
        coef = sb("coef", [P, 2])
        row_tmp = sb("row_tmp", [P, 4, D])
        kcols = sb("kcols", [P, 2, TILES], I32)
        kcolf = sb("kcolf", [P, 2, TILES])
        gidx = sb("gidx", [P, 2, 2 * GT], I32)
        krow = sb("krow", [P, 2, GROUP], I32)
        eat = sb("eat", [D, 2, GROUP])
        ewr = sb("ewr", [P, 2, GROUP])
        gx = sb("gx", [P, 2, 2 * GT, D])
        gc = sb("gc", [P, 2 * GT, D])
        gsq = sb("gsq", [P, 2 * GT, D])
        gh = sb("gh", [P, 2 * GT, D])
        gst = sb("gst", [P, 4, 2 * GT])
        ght = sb("ght", [P, GROUP])
        ghid = sb("ghid", [P, GROUP])
        gmsg = sb("gmsg", [P, GT, D])
        gtot = sb("gtot", [P, 2, GT, D])
        same = sb("same", [P, 2, GT, GROUP], BF16)
        same_out = sb("same_out", [P, GROUP])
        gparts = sb("gparts", [P, 2, 3, GT, D], BF16)
        grest = sb("grest", [P, GT, D])
        sidx_dst = sb("sidx_dst", [P, TILES], I32)
        sidx_src = sb("sidx_src", [P, TILES], I32)
        cnt = sb("cnt", [P, 2, GT])
        dumped = sb("dumped", [P, 2, GT])
        sidx = sb("sidx", [P, 2, GT], I32)
        big = sb("big", [P, EP])

        def area(i, shape=(J, D)):
            n = shape[0] * shape[1]
            return big[:, i * J * D:i * J * D + n].rearrange("p (a b) -> p a b", b=shape[1])

        zeros = area(20)

        bcj = lambda ap: ap.rearrange("p (a o) -> p a o", o=1).to_broadcast([P, ap.shape[1], D])
        bcd = lambda ap: ap.rearrange("p (a d) -> p a d", a=1).to_broadcast([P, J, D])


        s_const = sem("s_const")
        s_cpool = sem("s_cpool")
        s_zero = sem("s_zero")
        s_wdve = sem("s_wdve")
        s_wpe = sem("s_wpe")
        s_cdve = sem("s_cdve")
        NLOADS = 18

        def setup_sync(sp):
            W = weights
            loads = [
                (w_msg1[:, :], W["mW1"][0:P, :]), (w_msg1e[:, :], W["mW1"][P:P + 32, :]),
                (b_msg1[:, :], W["mb1"].rearrange("(p a) -> p a", a=1)), (w_msg2[:, :], W["mW2"]),
                (b_msg2[:, :], W["mb2"].partition_broadcast(P)), (w_upd1[:, :], W["uW1"]),
                (b_upd1[:, :], W["ub1"].rearrange("(p a) -> p a", a=1)), (w_upd2[:, 0:D], W["uW2"]),
                (b_upd2[:, 0:D], W["ub2"].partition_broadcast(P)), (w_gate[:, :], W["W"][0:P, :]),
                (w_gatee[:, :], W["W"][P:P + D, :]), (b_gate[:, :], W["b"].rearrange("(p a) -> p a", a=1)),
                (g1c[:, :], W["g1"].rearrange("(p a) -> p a", a=1)),
                (b1c[:, :], W["b1"].rearrange("(p a) -> p a", a=1)),
                (g2r[:, :], W["g2"].partition_broadcast(P)), (b2r[:, :], W["b2"].partition_broadcast(P)),
                (ew[:, :], edge_w_cols), (nw[:, :], node_w),
            ]
            assert len(loads) == NLOADS
            for dst, src in loads:
                sp.dma_start(dst, src).then_inc(s_const, 16)
            sp.dma_start(kcols[:, :, :], key_cols).then_inc(s_const, 16)

        def setup_gpsimd(pool):
            nc.gpsimd.memset(ident[:, :], 0.0).then_inc(s_cpool, 1)
            nc.gpsimd.memset(before[:, :], 1.0).then_inc(s_cpool, 1)
            nc.gpsimd.memset(ones[:, :], 1.0).then_inc(s_cpool, 1)
            pool.wait_ge(s_cpool, 3)
            nc.gpsimd.affine_select(out=ident[:, :], in_=ident[:, :], compare_op=ALU.not_equal, fill=1.0,
                                    base=0, pattern=[[-1, P]], channel_multiplier=1).then_inc(s_cpool, 1)
            nc.gpsimd.affine_select(out=before[:, :], in_=before[:, :], compare_op=ALU.is_gt, fill=0.0,
                                    base=GROUP - P, pattern=[[-1, GROUP]],
                                    channel_multiplier=1).then_inc(s_cpool, 1)
            nc.gpsimd.iota(dump_rows[:, :], pattern=[[P, GT]], base=DUMP,
                           channel_multiplier=1).then_inc(s_cpool, 1)

        def setup_vector(dve):
            ch = sem("s_setup_links")
            k = [0]

            def link(ins):
                k[0] += 1
                ins.then_inc(ch, 1)
                dve.wait_ge(ch, k[0])

            nc.vector.memset(zeros, 0.0).then_inc(s_zero, 1)
            nc.vector.memset(eps_col[:, :], EPS)
            nc.vector.memset(s1[:, :], 0.0)
            nc.vector.memset(s2[:, :], 0.0).then_inc(s_cdve, 1)
            dve.wait_ge(s_cpool, 6)
            nc.vector.tensor_copy(dump_f[:, :], dump_rows[:, :])
            dve.wait_ge(s_const, 16 * (NLOADS + 1))
            nc.vector.tensor_copy(kcolf[:, :, :], kcols[:, :, :])
            for w in (w_upd2, b_upd2):
                link(nc.vector.reduce_sum(tmp[:, 0:1], w[:, 0:D], X))
                link(nc.vector.tensor_scalar(w[:, D:D + 1], tmp[:, 0:1], 1.0 / D, None, ALU.mult))
                link(nc.vector.tensor_scalar(w[:, 0:D], w[:, 0:D], w[:, D:D + 1], None, ALU.subtract))
            nc.vector.reduce_sum(tmp[:, 1:2], ew[:, :], X).then_inc(s_wdve, 1)
            nc.vector.reduce_sum(tmp[:, 2:3], nw[:, :], X).then_inc(s_wdve, 1)
            dve.wait_ge(s_wpe, 1)
            link(nc.vector.tensor_copy(wsum[:, :], bank[0][:, 0:2]))
            link(nc.vector.reciprocal(wsum_inv[:, :], wsum[:, :]))

        def setup_scalar(act):
            act.wait_ge(s_const, 16 * (NLOADS + 1))
            act.wait_ge(s_cdve, 1)

        def setup_tensor(pe):
            pe.wait_ge(s_const, 16 * (NLOADS + 1))
            pe.wait_ge(s_cpool, 6)
            pe.wait_ge(s_wdve, 2)
            nc.tensor.matmul(bank[0][:, 0:2], ones[:, :], tmp[:, 1:3], start=True, stop=True).then_inc(s_wpe, 1)

        s_step = sem("s_step")
        s_gi = [sem(f"s_gi{b}") for b in range(2)]
        s_ga = [sem(f"s_ga{b}") for b in range(2)]
        s_gx = [sem(f"s_gx{b}") for b in range(2)]
        s_c = sem("s_c")
        s_sq = sem("s_sq")
        s_ss = sem("s_ss")
        s_std = sem("s_std")
        s_h = sem("s_h")
        s_tp = sem("s_tp")
        s_ht = sem("s_ht")
        s_m1 = sem("s_m1")
        s_hid = sem("s_hid")
        s_m2 = sem("s_m2")
        s_msg = sem("s_msg")
        s_hi = sem("s_hi")
        s_rest = sem("s_rest")
        s_mid = sem("s_mid")
        s_low = sem("s_low")
        s_same = sem("s_same")
        s_sidx = sem("s_sidx")
        s_m3 = sem("s_m3")
        s_tot = sem("s_tot")
        s_sc = sem("s_sc")
        ZRING = 3
        s_zagg = [sem(f"s_zagg{r}") for r in range(ZRING)]
        s_ztail = sem("s_ztail")
        s_znsum = sem("s_znsum")
        HALF = GT // 2 * P
        LEAD = 9
        CATCH = 6
        LAG = LEAD - CATCH
        STEADY = LEAD + CATCH
        ZPART = CHUNKS // (LEAD - 2)
        assert CHUNKS % (LEAD - 2) == 0 and CHUNKS == GROUPS and LEAD % 2 == 1 and CATCH % 2 == 0
        s_astep = sem("s_astep")
        s_stage = sem("s_stage")
        tots = big[:, 0:GROUPS * GT * D].rearrange("p (j d) -> p j d", d=D)

        def edges0_indices(sp, u, b, g):
            await_(sp, s_gx[b], 128 * u)
            sp.dma_start(gidx[:, b, :], gat[bass.ds(g, 1), :, :].rearrange("g p c -> (g p) c")).then_inc(s_gi[b], 16)

        def edges0_first(sp):
            edges0_indices(sp, 0, 0, 0)
            edges0_indices(sp, 0, 1, 1)

        def edges0_sync(sp):
            def load(b, g):
                await_(sp, s_same, g - 1)
                await_(sp, s_m1, g - 1)
                sp.dma_start(krow[:, b, :], key_dst[bass.ds(g * GROUP, GROUP)].partition_broadcast(P)).then_inc(s_ga[b], 16)
                sp.dma_start(eat[0:32, b, :], ea32_t[:, bass.ds(g * GROUP, GROUP)]).then_inc(s_ga[b], 16)

            def zero_agg(part):
                def zero(r, u):
                    await_(sp, s_zagg[r], 16 * u)
                    sp.dma_start(chunk_rows(agg, u * ZRING + r), zeros).then_inc(s_zagg[r], 16)

                first, end = (round(k * ZPART / ZRING) for k in (part, part + 1))
                if part == 0:
                    for r in range(ZRING):
                        zero(r, 0)
                with sp.Fori(max(first, 1), end) as u:
                    for r in range(ZRING):
                        zero(r, u)
                if part == LEAD - 3:
                    for r in range(CHUNKS % ZRING):
                        zero(r, end)

            def zero_tail(table, s):
                n = (ROWS - NP) * D // P
                sp.dma_start(table[NP:ROWS, :].rearrange("r d -> (r d)").rearrange("(p f) -> p f", f=n),
                             zeros.rearrange("p j d -> p (j d)")[:, 0:n]).then_inc(s, 16)

            def zero_nsum(g):
                sp.dma_start(chunk_rows(nsum, g), zeros).then_inc(s_znsum, 16)

            load(0, 0)
            sp.wait_ge(s_zero, 1)
            zero_tail(agg, s_ztail)
            for g in range(2, STEADY):
                if g < LEAD:
                    zero_agg(g - 2)
                edges0_indices(sp, g // 2, g % 2, g)
                load((g - 1) % 2, g - 1)
                if g >= LEAD:
                    each = -(-(STEADY - 1) // CATCH)
                    for c in range(each * (g - LEAD), min(each * (g - LEAD + 1), STEADY - 1)):
                        zero_nsum(c)
            with sp.Fori(STEADY // 2, GROUPS // 2) as u:
                edges0_indices(sp, u, 1, u * 2 + 1)
                load(0, u * 2)
                zero_nsum(u * 2)
                edges0_indices(sp, u + 1, 0, u * 2 + 2)
                load(1, u * 2 + 1)
                zero_nsum(u * 2 + 1)
            load(0, GROUPS - 1)
            zero_nsum(CHUNKS - 1)
            zero_tail(nsum, s_znsum)

        def edges0_gpsimd(pool):
            def gather(b, ks):
                for k in ks:
                    pool.indirect_dma_start(gx[:, b, k, :], None, x,
                                            bass.IndirectOffsetOnAxis(gidx[:, b, k:k + 1], 0)).then_inc(s_gx[b], 16)

            def gather_start(u, b, g):
                pool.wait_ge(s_gi[b], 16 * (u + 1))
                await_(pool, s_c, g - 1)
                pool.sem_inc(s_step, 1)

            def scatter(b, g, pair):
                if pair == 0:
                    pool.wait_ge(s_stage, g + 1)
                await_(pool, s_sc, 64 * g + 32 * pair)
                pool.sem_inc(s_step, 1)
                for k in (2 * pair, 2 * pair + 1):
                    pool.indirect_dma_start(agg, bass.IndirectOffsetOnAxis(sidx[:, b, k:k + 1], 0),
                                            gtot[:, b, k, :], None, compute_op=ALU.add).then_inc(s_sc, 16)

            def lead(u, b, g):
                gather_start(u, b, g)
                gather(b, range(8))

            def catch_up(u, b, g):
                gather_start(u, b, g)
                for k in range(4):
                    gather(b, (2 * k, 2 * k + 1))
                    scatter(k // 2, 2 * (g - LEAD) + k // 2, k % 2)

            def both(u, b, g):
                gather_start(u, b, g)
                gather(b, range(4))
                scatter(1 - b, g - LAG, 0)
                gather(b, range(4, 8))
                scatter(1 - b, g - LAG, 1)

            lead(0, 0, 0)
            lead(0, 1, 1)
            with pool.Fori(1, LEAD // 2) as u:
                for b in range(2):
                    lead(u, b, u * 2 + b)
            lead(LEAD // 2, 0, LEAD - 1)
            pool.wait_ge(s_ztail, 16)
            for r in range(ZRING):
                pool.wait_ge(s_zagg[r], 16 * -(-(CHUNKS - r) // ZRING))
            for g in range(LEAD, STEADY):
                catch_up(g // 2, g % 2, g)
            both(STEADY // 2, 1, STEADY)
            with pool.Fori(STEADY // 2 + 1, GROUPS // 2) as u:
                for b in range(2):
                    both(u, b, u * 2 + b)
            both(GROUPS // 2, 0, GROUPS - 1)
            for g in range(GROUPS - LAG, GROUPS):
                scatter(g % 2, g, 0)
                scatter(g % 2, g, 1)

        def edges0_vector(dve):
            ch = sem("s_edges0_links")
            PER = 8

            def msg(b, g):
                dve.wait_ge(s_m2, g + 1)
                nc.vector.tensor_tensor(
                    gmsg[:, :, :], bank[2][:, 0:GT * D].rearrange("p (j d) -> p j d", d=D),
                    b_msg2[:, :].rearrange("p (a d) -> p a d", a=1).to_broadcast([P, GT, D]), ALU.add).then_inc(s_msg, 1)
                nc.vector.tensor_tensor(sidx_dst[:, bass.ds(g * GT, GT)], dumped[:, b, :],
                                        kcolf[:, 0, bass.ds(g * GT, GT)], ALU.max).then_inc(s_sidx, 1)
                dve.wait_ge(s_hi, g + 1)
                nc.vector.tensor_tensor(grest[:, :, :], gmsg[:, :, :], gparts[:, 0, 0, :, :], ALU.subtract).then_inc(s_rest, 1)

            def low(g):
                dve.wait_ge(s_mid, g + 1)
                nc.vector.tensor_tensor(gparts[:, 0, 2, :, :], grest[:, :, :], gparts[:, 0, 1, :, :],
                                        ALU.subtract).then_inc(s_low, 1)

            def group(u, b, g):
                k = [0]

                def link(ins):
                    k[0] += 1
                    ins.then_inc(ch, 1)
                    dve.wait_ge(ch, g * PER + k[0])

                rows = gx[:, b, :, :]
                bc = lambda i: gst[:, i, :].rearrange("p (a o) -> p a o", o=1).to_broadcast([P, 2 * GT, D])
                dve.wait_ge(s_gx[b], 128 * (u + 1))
                await_(dve, s_h, g)
                link(nc.vector.reduce_sum(gst[:, 0, :], rows, X))
                link(nc.vector.tensor_scalar(gst[:, 1, :], gst[:, 0, :], 1.0 / D, None, ALU.mult))
                nc.vector.tensor_tensor(gc[:, :, :], rows, bc(1), ALU.subtract).then_inc(s_c, 1)
                dve.wait_ge(s_ga[b], 32 * (u + 1))
                await_(dve, s_m3, g - 1)
                for j in range(GT):
                    half = HALF * (j // 2)
                    ins = nc.vector.tensor_scalar(same[:, b, j, 0:HALF], krow[:, b, half:half + HALF],
                                                  kcolf[:, 0, bass.ds(g * GT + j, 1)], None, ALU.is_equal)
                ins.then_inc(s_same, 1)
                dve.wait_ge(s_sq, g + 1)
                nc.vector.reduce_sum(gst[:, 2, :], gsq[:, :, :], X).then_inc(s_ss, 1)
                dve.wait_ge(s_same, g + 1)
                for j in range(GT):
                    n = P * (j % 2 + 1)
                    link(nc.vector.tensor_tensor_reduce(
                        out=same_out[:, 0:n], in0=same[:, b, j, 0:n], in1=before[:, GROUP - n:GROUP], scale=1.0,
                        scalar=0.0, op0=ALU.mult, op1=ALU.add, accum_out=cnt[:, 0, j:j + 1]))
                dve.wait_ge(s_std, g + 1)
                link(nc.vector.reciprocal(gst[:, 0, :], gst[:, 3, :]))
                link(nc.vector.scalar_tensor_tensor(out=dumped[:, b, :], in0=cnt[:, 0, :], scalar=1.0,
                                                    in1=dump_f[:, :], op0=ALU.min, op1=ALU.mult))
                await_(dve, s_tp, g)
                nc.vector.scalar_tensor_tensor(out=gh[:, :, :], in0=gc[:, :, :], scalar=0.0, in1=bc(0),
                                               op0=ALU.max, op1=ALU.mult).then_inc(s_h, 1)
                if not known(g) or g > 0:
                    msg(1 - b, g - 1)
                    low(g - 1)
                assert k[0] == PER

            group(0, 0, 0)
            group(0, 1, 1)
            with dve.Fori(1, GROUPS // 2) as u:
                for b in range(2):
                    group(u, b, u * 2 + b)
            group(GROUPS // 2, 0, GROUPS - 1)
            msg(0, GROUPS - 1)
            low(GROUPS - 1)

        def edges0_scalar(act):
            def late(b, g):
                act.wait_ge(s_msg, g + 1)
                await_(act, s_m3, g)
                nc.scalar.copy(gparts[:, 0, 0, :, :], gmsg[:, :, :]).then_inc(s_hi, 1)
                act.wait_ge(s_rest, g + 1)
                nc.scalar.copy(gparts[:, 0, 1, :, :], grest[:, :, :]).then_inc(s_mid, 1)

            def sums(g):
                act.wait_ge(s_m3, g + 1)
                nc.scalar.copy(tots[:, bass.ds(g * GT, GT), :],
                               bank[3][:, 0:GT * D].rearrange("p (j d) -> p j d", d=D)).then_inc(s_tot, 1)

            def stage(b, g):
                act.wait_ge(s_tot, g + 1)
                act.wait_ge(s_sidx, g + 1)
                await_(act, s_sc, 64 * (g - 1))
                act.sem_inc(s_astep, 1)
                nc.scalar.copy(gtot[:, b, :, :], tots[:, bass.ds(g * GT, GT), :])
                nc.scalar.copy(sidx[:, b, :], sidx_dst[:, bass.ds(g * GT, GT)]).then_inc(s_stage, 1)

            def group(u, b, g):
                if known(g) and LEAD - 1 <= g < STEADY - 1:
                    stage(0, 2 * (g - LEAD + 1))
                    stage(1, 2 * (g - LEAD + 1) + 1)
                if in_steady:
                    stage(b, g - LAG + 1)
                act.wait_ge(s_c, g + 1)
                await_(act, s_ss, g)
                nc.scalar.activation(gsq[:, :, :], gc[:, :, :], ACT.Square).then_inc(s_sq, 1)
                act.wait_ge(s_ss, g + 1)
                nc.scalar.activation(gst[:, 3, :], gst[:, 2, :], ACT.Sqrt, bias=eps_col[:, :],
                                     scale=1.0 / D).then_inc(s_std, 1)
                if not known(g) or g > 0:
                    late(1 - b, g - 1)
                act.wait_ge(s_tp, g + 1)
                nc.scalar.copy(ght[:, :], bank[0][:, :]).then_inc(s_ht, 1)
                if not known(g) or g > 0:
                    sums(g - 1)
                act.wait_ge(s_m1, g + 1)
                nc.scalar.activation(ghid[:, :], bank[1][:, :], ACT.Relu, bias=b_msg1[:, :]).then_inc(s_hid, 1)

            in_steady = False
            group(0, 0, 0)
            group(0, 1, 1)
            with act.Fori(1, (LEAD - 1) // 2) as u:
                for b in range(2):
                    group(u, b, u * 2 + b)
            for g in range(LEAD - 1, STEADY - 1):
                group(g // 2, g % 2, g)
            in_steady = True
            with act.Fori((STEADY - 1) // 2, GROUPS // 2) as u:
                for b in range(2):
                    group(u, b, u * 2 + b)
            group(GROUPS // 2, 0, GROUPS - 1)
            stage(1, GROUPS - 2)
            late(0, GROUPS - 1)
            sums(GROUPS - 1)
            stage(0, GROUPS - 1)

        def edges0_tensor(pe):
            def sums(b, g):
                pe.wait_ge(s_low, g + 1)
                pe.wait_ge(s_same, g + 1)
                await_(pe, s_tot, g)
                for i in range(GT):
                    pair = i // 2 * 2
                    for j in (pair, pair + 1):
                        for part in range(3):
                            ins = nc.tensor.matmul(bank[3][:, D * i:D * i + D],
                                                   same[:, b, j, P * (i - pair):P * (i - pair) + P],
                                                   gparts[:, 0, part, j, :], start=(j == pair and part == 0),
                                                   stop=(j == pair + 1 and part == 2))
                ins.then_inc(s_m3, 1)

            def group(u, b, g):
                pe.wait_ge(s_h, g + 1)
                for j in range(GT):
                    ins = nc.tensor.transpose(bank[0][:, P * j:P * j + P],
                                              gh[:, 2 * j:2 * j + 2, :].rearrange("p a d -> p (a d)"), ident[:, :])
                ins.then_inc(s_tp, 1)
                if not known(g) or g > 0:
                    sums(1 - b, g - 1)
                pe.wait_ge(s_ht, g + 1)
                pe.wait_ge(s_ga[b], 32 * (u + 1))
                nc.tensor.matmul(bank[1][:, :], w_msg1[:, :], ght[:, :], start=True, stop=False)
                nc.tensor.matmul(bank[1][:, :], w_msg1e[:, :], eat[0:32, b, :], start=False, stop=True).then_inc(s_m1, 1)
                pe.wait_ge(s_hid, g + 1)
                for j in range(GT):
                    ins = nc.tensor.matmul(bank[2][:, D * j:D * j + D], ghid[:, P * j:P * j + P], w_msg2[:, :],
                                           start=True, stop=True)
                ins.then_inc(s_m2, 1)

            group(0, 0, 0)
            group(0, 1, 1)
            with pe.Fori(1, GROUPS // 2) as u:
                for b in range(2):
                    group(u, b, u * 2 + b)
            group(GROUPS // 2, 0, GROUPS - 1)
            sums(0, GROUPS - 1)

        s_nx = [sem(f"s_nx{b}") for b in range(2)]
        s_na = [sem(f"s_na{b}") for b in range(2)]
        s_nm = sem("s_nm")
        s_nc = sem("s_nc")
        s_ncb = sem("s_ncb")
        s_nsq = sem("s_nsq")
        s_nss = sem("s_nss")
        s_nstd = sem("s_nstd")
        s_nh = sem("s_nh")
        s_ntp = sem("s_ntp")
        s_nht = sem("s_nht")
        s_nm1 = sem("s_nm1")
        s_nhid = sem("s_nhid")
        s_nm2 = sem("s_nm2")
        s_nc1 = sem("s_nc1")
        s_nsq1 = sem("s_nsq1")
        s_nss1 = sem("s_nss1")
        s_nstd1 = sem("s_nstd1")
        s_nst = [sem(f"s_nst{b}") for b in range(2)]
        xin = [area(0), area(1)]
        c0 = [area(2), area(3)]
        c0b = [area(4), area(5)]
        c1 = [area(6), area(7)]
        sq0 = area(8)
        sq1 = area(9)
        ha = [area(10, (J, 2 * D)), area(12, (J, 2 * D))]
        hts = [area(14, (4, P)), area(15, (4, P))]
        hids = [area(16, (4, P)), area(17, (4, P))]
        nst = big[:, 18 * J * D:18 * J * D + 16 * J].rearrange("p (a j) -> p a j", j=J)
        Q = J // 4
        LAST = CHUNKS - 1

        def periods(eng, period):
            period(0, 0, 0)
            period(0, 1, 1)
            with eng.Fori(1, CHUNKS // 2 - 1) as u:
                for b in range(2):
                    period(u, b, u * 2 + b)
            for g in range(CHUNKS - 3, CHUNKS):
                period(g // 2, g % 2, g)

        def has(g):
            return not known(g) or 0 <= g <= LAST

        def nodes0_sync(sp):
            def load_x(u, b, g):
                await_(sp, s_nc, g - 1)
                sp.dma_start(xin[b], chunk_rows(x, g)).then_inc(s_nx[b], 16)

            def load_a(u, b, g):
                await_(sp, s_ntp, 4 * (g - 1))
                sp.dma_start(ha[b][:, :, D:2 * D], chunk_rows(agg, g)).then_inc(s_na[b], 16)

            def period(u, b, g):
                if has(g + 3):
                    load_x(None, 1 - b, g + 3)
                if has(g + 2):
                    load_a(None, b, g + 2)
                sp.wait_ge(s_nc1, 4 * (g + 1))
                sp.dma_start(chunk_rows(ctab, g), c1[b]).then_inc(s_nst[b], 16)

            load_x(0, 0, 0)
            load_x(0, 1, 1)
            sp.wait_ge(s_sc, 64 * GROUPS)
            load_a(0, 0, 0)
            load_a(0, 1, 1)
            load_x(1, 0, 2)
            periods(sp, period)

        def nodes0_gpsimd(pool):
            def centre(b, g):
                pool.wait_ge(s_nm, g + 1)
                await_(pool, s_nh, g - 1)
                await_(pool, s_ncb, g - 1)
                nc.gpsimd.tensor_tensor(c0[b], xin[b], bcj(nst[:, 1 + b, :]), ALU.subtract).then_inc(s_nc, 1)

            def bias(b, g):
                pool.wait_ge(s_nc, g + 1)
                await_(pool, s_nc1, 4 * (g - 1))
                nc.gpsimd.tensor_tensor(c0b[b], c0[b], bcd(b_upd2[:, 0:D]), ALU.add).then_inc(s_ncb, 1)

            def period(u, b, g):
                if has(g + 2):
                    centre(b, g + 2)
                if has(g + 1):
                    bias(1 - b, g + 1)

            centre(0, 0)
            bias(0, 0)
            centre(1, 1)
            periods(pool, period)

        def nodes0_vector(dve):
            cha = sem("s_nsum_links")
            chb = sem("s_nrec_links")

            def mean(u, b, g):
                dve.wait_ge(s_nx[b], 16 * (u + 1))
                await_(dve, s_nm, g)
                nc.vector.reduce_sum(nst[:, 0, :], xin[b], X).then_inc(cha, 1)
                dve.wait_ge(cha, g + 1)
                await_(dve, s_nc, g - 1)
                nc.vector.tensor_scalar(m1[:, bass.ds(g * J, J)], nst[:, 0, :], 1.0 / D, None, ALU.mult)
                nc.vector.tensor_scalar(nst[:, 1 + b, :], nst[:, 0, :], 1.0 / D, None, ALU.mult).then_inc(s_nm, 1)

            def squares(g):
                dve.wait_ge(s_nsq, g + 1)
                nc.vector.reduce_sum(nst[:, 3, :], sq0, X).then_inc(s_nss, 1)

            def norm(b, g):
                dve.wait_ge(s_nstd, g + 1)
                nc.vector.reciprocal(nst[:, 5, :], nst[:, 4, :]).then_inc(chb, 1)
                dve.wait_ge(chb, g + 1)
                await_(dve, s_ntp, 4 * (g - 1))
                nc.vector.scalar_tensor_tensor(out=ha[b][:, :, 0:D], in0=c0[b], scalar=0.0, in1=bcj(nst[:, 5, :]),
                                               op0=ALU.max, op1=ALU.mult).then_inc(s_nh, 1)

            def update(u, b, g, q):
                o = bank[4 + q][:, 0:Q * (D + 1)].rearrange("p (j e) -> p j e", e=D + 1)
                dve.wait_ge(s_nm2, 4 * g + q + 1)
                if q == 0:
                    dve.wait_ge(s_ncb, g + 1)
                    await_(dve, s_nst[b], 16 * u)
                    await_(dve, s_nsq1, g - 1)
                means = m1[:, bass.ds(g * J + Q * q, Q)]
                nc.vector.scalar_tensor_tensor(
                    out=means, in0=o[:, :, D:D + 1].rearrange("p j o -> p (j o)"),
                    scalar=b_upd2[:, D:D + 1], in1=means, op0=ALU.add, op1=ALU.add)
                nc.vector.tensor_tensor(c1[b][:, Q * q:Q * q + Q, :], c0b[b][:, Q * q:Q * q + Q, :],
                                        o[:, :, 0:D], ALU.add).then_inc(s_nc1, 1)

            def variance(g):
                dve.wait_ge(s_nsq1, g + 1)
                nc.vector.reduce_sum(nst[:, 7, :], sq1, X).then_inc(s_nss1, 1)

            def scale(g):
                dve.wait_ge(s_nstd1, g + 1)
                nc.vector.reciprocal(r1[:, bass.ds(g * J, J)], nst[:, 8, :])

            def period(u, b, g):
                if has(g + 1):
                    norm(1 - b, g + 1)
                update(u, b, g, 0)
                if has(g - 1):
                    variance(g - 1)
                update(u, b, g, 1)
                if has(g + 2):
                    squares(g + 2)
                update(u, b, g, 2)
                if has(g + 3):
                    mean(u + 1 + b, 1 - b, g + 3)
                if has(g - 1):
                    scale(g - 1)
                update(u, b, g, 3)

            mean(0, 0, 0)
            squares(0)
            norm(0, 0)
            mean(0, 1, 1)
            squares(1)
            mean(1, 0, 2)
            periods(dve, period)
            variance(LAST)
            scale(LAST)

        def nodes0_scalar(act):
            def squares(b, g):
                act.wait_ge(s_nc, g + 1)
                await_(act, s_nss, g)
                nc.scalar.activation(sq0, c0[b], ACT.Square).then_inc(s_nsq, 1)

            def deviation(g):
                act.wait_ge(s_nss, g + 1)
                nc.scalar.activation(nst[:, 4, :], nst[:, 3, :], ACT.Sqrt, bias=eps_col[:, :], scale=1.0 / D).then_inc(s_nstd, 1)

            def turned(g, q):
                act.wait_ge(s_ntp, 4 * g + q + 1)
                nc.scalar.copy(hts[q % 2], bank[q % 2][:, :].rearrange("p (a b) -> p a b", b=P)).then_inc(s_nht, 1)

            def hidden(g, q):
                act.wait_ge(s_nm1, 4 * g + q + 1)
                nc.scalar.activation(hids[q % 2], bank[2 + q % 2][:, :].rearrange("p (a b) -> p a b", b=P), ACT.Relu,
                                     bias=b_upd1[:, :]).then_inc(s_nhid, 1)

            def squares1(b, g):
                act.wait_ge(s_nc1, 4 * (g + 1))
                await_(act, s_nss1, g)
                nc.scalar.activation(sq1, c1[b], ACT.Square).then_inc(s_nsq1, 1)

            def deviation1(g):
                act.wait_ge(s_nss1, g + 1)
                nc.scalar.activation(nst[:, 8, :], nst[:, 7, :], ACT.Sqrt, bias=eps_col[:, :], scale=1.0 / D).then_inc(s_nstd1, 1)

            def period(u, b, g):
                turned(g, 2)
                hidden(g, 1)
                if has(g - 1):
                    squares1(1 - b, g - 1)
                turned(g, 3)
                hidden(g, 2)
                if has(g + 2):
                    squares(b, g + 2)
                if has(g + 1):
                    turned(g + 1, 0)
                hidden(g, 3)
                if has(g - 1):
                    deviation1(g - 1)
                if has(g + 1):
                    turned(g + 1, 1)
                    hidden(g + 1, 0)
                if has(g + 2):
                    deviation(g + 2)

            squares(0, 0)
            deviation(0)
            squares(1, 1)
            deviation(1)
            turned(0, 0)
            turned(0, 1)
            hidden(0, 0)
            periods(act, period)
            squares1(0, LAST)
            deviation1(LAST)

        def nodes0_tensor(pe):
            def turn(b, g, q):
                await_(pe, s_nht, 4 * g + q - 1)
                for j in range(4):
                    ins = nc.tensor.transpose(bank[q % 2][:, P * j:P * j + P], ha[b][:, 4 * q + j, :], ident[:, :])
                ins.then_inc(s_ntp, 1)

            def first(g, q):
                pe.wait_ge(s_nht, 4 * g + q + 1)
                await_(pe, s_nhid, 4 * g + q - 1)
                nc.tensor.matmul(bank[2 + q % 2][:, :], w_upd1[:, :], hts[q % 2].rearrange("p a b -> p (a b)"),
                                 start=True, stop=True).then_inc(s_nm1, 1)

            def second(g, q):
                pe.wait_ge(s_nhid, 4 * g + q + 1)
                await_(pe, s_nc1, 4 * (g - 1) + q + 1)
                for j in range(4):
                    ins = nc.tensor.matmul(bank[4 + q][:, (D + 1) * j:(D + 1) * (j + 1)], hids[q % 2][:, j, :],
                                           w_upd2[:, :], start=True, stop=True)
                ins.then_inc(s_nm2, 1)

            def start(u, b, g):
                pe.wait_ge(s_nh, g + 1)
                pe.wait_ge(s_na[b], 16 * (u + 1))

            def period(u, b, g):
                turn(b, g, 2)
                first(g, 1)
                second(g, 0)
                turn(b, g, 3)
                first(g, 2)
                second(g, 1)
                if has(g + 1):
                    start(u + b, 1 - b, g + 1)
                    turn(1 - b, g + 1, 0)
                first(g, 3)
                second(g, 2)
                if has(g + 1):
                    turn(1 - b, g + 1, 1)
                    first(g + 1, 0)
                second(g, 3)

            pe.wait_ge(s_tot, GROUPS)
            pe.wait_ge(s_hid, GROUPS)
            start(0, 0, 0)
            turn(0, 0, 0)
            turn(0, 0, 1)
            first(0, 0)
            periods(pe, period)

        s_ei = [sem(f"s_ei{b}") for b in range(2)]
        s_ea = [sem(f"s_ea{b}") for b in range(2)]
        s_ew = [sem(f"s_ew{b}") for b in range(2)]
        s_ex = [sem(f"s_ex{b}") for b in range(2)]
        s_esq = sem("s_esq")
        s_ess = sem("s_ess")
        s_estd = sem("s_estd")
        s_eh = sem("s_eh")
        s_etp = sem("s_etp")
        s_eht = sem("s_eht")
        s_em = sem("s_em")
        s_et = sem("s_et")
        s_es = sem("s_es")
        s_esame = sem("s_esame")

        def edges1_sync(sp):
            def indices(u, b, g):
                await_(sp, s_ex[b], 128 * u)
                sp.dma_start(gidx[:, b, :], gat[bass.ds(g, 1), :, :].rearrange("g p c -> (g p) c")).then_inc(s_ei[b], 16)

            def load(b, g):
                await_(sp, s_em, g - 1)
                await_(sp, s_esame, g - 1)
                sp.dma_start(eat[:, b, :], ea64_t[:, bass.ds(g * GROUP, GROUP)]).then_inc(s_ea[b], 16)
                sp.dma_start(krow[:, b, :], key_src[bass.ds(g * GROUP, GROUP)].partition_broadcast(P)).then_inc(s_ea[b], 16)
                await_(sp, s_es, g - 1)
                sp.dma_start(ewr[:, b, :], edge_w[bass.ds(g * GROUP, GROUP)].partition_broadcast(P)).then_inc(s_ew[b], 16)

            indices(0, 0, 0)
            indices(0, 1, 1)
            load(0, 0)
            indices(1, 0, 2)
            load(1, 1)
            with sp.Fori(1, GROUPS // 2) as u:
                indices(u, 1, u * 2 + 1)
                load(0, u * 2)
                indices(u + 1, 0, u * 2 + 2)
                load(1, u * 2 + 1)
            load(0, GROUPS - 1)

        def edges1_gpsimd(pool):
            def gather(u, b, g):
                pool.wait_ge(s_ei[b], 16 * (u + 1))
                await_(pool, s_eh, g - 1)
                pool.sem_inc(s_step, 1)
                for k in range(2 * GT):
                    pool.indirect_dma_start(gx[:, b, k, :], None, ctab,
                                            bass.IndirectOffsetOnAxis(gidx[:, b, k:k + 1], 0)).then_inc(s_ex[b], 16)

            pool.wait_ge(s_nst[0], 16 * (CHUNKS // 2 + 1))
            pool.wait_ge(s_nst[1], 16 * (CHUNKS // 2))
            gather(0, 0, 0)
            gather(0, 1, 1)
            with pool.Fori(1, GROUPS // 2) as u:
                for b in range(2):
                    gather(u, b, u * 2 + b)
            gather(GROUPS // 2, 0, GROUPS - 1)

        def edges1_vector(dve):
            ch = sem("s_edges1_links")
            cht = sem("s_edges1_sums")
            PER = 6

            def sums(u, b, g):
                dve.wait_ge(s_et, g + 1)
                dve.wait_ge(s_ew[b], 16 * (u + 1))
                t = tbuf[:, b, :]
                await_(dve, cht, 2 * g)
                nc.vector.tensor_tensor_reduce(out=same_out[:, :], in0=t, in1=ewr[:, b, :], scale=1.0,
                                               scalar=s1[:, 1 - b:2 - b], op0=ALU.mult, op1=ALU.add,
                                               accum_out=s1[:, b:b + 1]).then_inc(cht, 1)
                dve.wait_ge(cht, 2 * g + 1)
                nc.vector.tensor_tensor_reduce(out=ghid[:, :], in0=same_out[:, :], in1=t, scale=1.0,
                                               scalar=s2[:, 1 - b:2 - b], op0=ALU.mult, op1=ALU.add,
                                               accum_out=s2[:, b:b + 1]).then_inc(cht, 1)
                nc.vector.tensor_copy(big[:, bass.ds(g * GROUP, GROUP)], t).then_inc(s_es, 1)

            def group(u, b, g):
                k = [0]

                def link(ins):
                    k[0] += 1
                    ins.then_inc(ch, 1)
                    dve.wait_ge(ch, g * PER + k[0])

                dve.wait_ge(s_esq, g + 1)
                nc.vector.reduce_sum(gst[:, 2, :], gsq[:, :, :], X).then_inc(s_ess, 1)
                dve.wait_ge(s_ea[b], 32 * (u + 1))
                for j in range(GT):
                    ins = nc.vector.tensor_scalar(same[:, 0, j, :], krow[:, b, :], kcolf[:, 1, bass.ds(g * GT + j, 1)],
                                                  None, ALU.is_equal)
                ins.then_inc(s_esame, 1)
                dve.wait_ge(s_estd, g + 1)
                link(nc.vector.reciprocal(gst[:, 0, :], gst[:, 3, :]))
                await_(dve, s_etp, g)
                nc.vector.scalar_tensor_tensor(
                    out=gh[:, :, :], in0=gx[:, b, :, :], scalar=0.0,
                    in1=gst[:, 0, :].rearrange("p (a o) -> p a o", o=1).to_broadcast([P, 2 * GT, D]),
                    op0=ALU.max, op1=ALU.mult).then_inc(s_eh, 1)
                if not known(g) or g > 0:
                    sums(u - 1 + b, 1 - b, g - 1)
                    dve.wait_ge(cht, 2 * g)
                dve.wait_ge(s_esame, g + 1)
                for j in range(GT):
                    n = P * (j + 1)
                    link(nc.vector.tensor_tensor_reduce(
                        out=same_out[:, 0:n], in0=same[:, 0, j, 0:n], in1=before[:, GROUP - n:GROUP], scale=1.0,
                        scalar=0.0, op0=ALU.mult, op1=ALU.add, accum_out=cnt[:, 0, j:j + 1]))
                link(nc.vector.scalar_tensor_tensor(out=cnt[:, 1, :], in0=cnt[:, 0, :], scalar=1.0,
                                                    in1=dump_f[:, :], op0=ALU.min, op1=ALU.mult))
                nc.vector.tensor_tensor(sidx_src[:, bass.ds(g * GT, GT)], cnt[:, 1, :],
                                        kcolf[:, 1, bass.ds(g * GT, GT)], ALU.max)
                assert k[0] == PER

            dve.wait_ge(s_znsum, 16 * (CHUNKS + 1))
            group(0, 0, 0)
            group(0, 1, 1)
            with dve.Fori(1, GROUPS // 2) as u:
                for b in range(2):
                    group(u, b, u * 2 + b)
            group(GROUPS // 2, 0, GROUPS - 1)
            sums(GROUPS // 2, 0, GROUPS - 1)

        def edges1_scalar(act):
            def kept(b, g):
                act.wait_ge(s_em, g + 1)
                await_(act, s_es, g - 1)
                nc.scalar.activation(tbuf[:, b, :], bank[1][:, :], ACT.Identity, bias=b_gate[:, :]).then_inc(s_et, 1)

            def group(u, b, g):
                act.wait_ge(s_ex[b], 128 * (u + 1))
                await_(act, s_ess, g)
                nc.scalar.activation(gsq[:, :, :], gx[:, b, :, :], ACT.Square).then_inc(s_esq, 1)
                act.wait_ge(s_ess, g + 1)
                nc.scalar.activation(gst[:, 3, :], gst[:, 2, :], ACT.Sqrt, bias=eps_col[:, :], scale=1.0 / D).then_inc(s_estd, 1)
                if not known(g) or g > 0:
                    kept(1 - b, g - 1)
                act.wait_ge(s_etp, g + 1)
                nc.scalar.copy(ght[:, :], bank[0][:, :]).then_inc(s_eht, 1)

            group(0, 0, 0)
            group(0, 1, 1)
            with act.Fori(1, GROUPS // 2) as u:
                for b in range(2):
                    group(u, b, u * 2 + b)
            group(GROUPS // 2, 0, GROUPS - 1)
            kept(0, GROUPS - 1)

        def edges1_tensor(pe):
            def group(u, b, g):
                pe.wait_ge(s_eh, g + 1)
                for j in range(GT):
                    ins = nc.tensor.transpose(bank[0][:, P * j:P * j + P],
                                              gh[:, 2 * j:2 * j + 2, :].rearrange("p a d -> p (a d)"), ident[:, :])
                ins.then_inc(s_etp, 1)
                pe.wait_ge(s_eht, g + 1)
                pe.wait_ge(s_ea[b], 32 * (u + 1))
                await_(pe, s_et, g)
                nc.tensor.matmul(bank[1][:, :], w_gate[:, :], ght[:, :], start=True, stop=False)
                nc.tensor.matmul(bank[1][:, :], w_gatee[:, :], eat[:, b, :], start=False, stop=True).then_inc(s_em, 1)

            pe.wait_ge(s_nhid, 4 * CHUNKS)
            group(0, 0, 0)
            group(0, 1, 1)
            with pe.Fori(1, GROUPS // 2) as u:
                for b in range(2):
                    group(u, b, u * 2 + b)
            group(GROUPS // 2, 0, GROUPS - 1)

        s_var = sem("s_var")
        s_sd = sem("s_sd")
        s_norm = sem("s_norm")

        def norm1_vector(dve):
            ch = sem("s_norm_links")
            k = [0]

            def link(ins):
                k[0] += 1
                ins.then_inc(ch, 1)
                dve.wait_ge(ch, k[0])

            link(nc.vector.tensor_copy(tmp[:, 0:1], s1[:, 0:1]))
            link(nc.vector.tensor_copy(tmp[:, 1:2], s2[:, 0:1]))
            link(nc.vector.tensor_scalar(tmp[:, 2:4], tmp[:, 0:2], wsum_inv[:, 0:1], None, ALU.mult))
            link(nc.vector.tensor_tensor(tmp[:, 4:5], tmp[:, 2:3], tmp[:, 2:3], ALU.mult))
            link(nc.vector.tensor_tensor(tmp[:, 5:6], tmp[:, 3:4], tmp[:, 4:5], ALU.subtract))
            nc.vector.tensor_scalar(tmp[:, 5:6], tmp[:, 5:6], 0.0, None, ALU.max).then_inc(s_var, 1)
            dve.wait_ge(s_sd, 1)
            link(nc.vector.reciprocal(tmp[:, 7:8], tmp[:, 6:7]))
            link(nc.vector.tensor_tensor(A1[:, :], g1c[:, :], tmp[:, 7:8], ALU.mult))
            link(nc.vector.tensor_tensor(tmp[:, 0:1], A1[:, :], tmp[:, 2:3], ALU.mult))
            nc.vector.tensor_tensor(B1[:, :], b1c[:, :], tmp[:, 0:1], ALU.subtract).then_inc(s_norm, 1)

        def norm1_scalar(act):
            act.wait_ge(s_var, 1)
            nc.scalar.activation(tmp[:, 6:7], tmp[:, 5:6], ACT.Sqrt, bias=eps_col[:, :]).then_inc(s_sd, 1)

        s_fi = [sem(f"s_fi{b}") for b in range(2)]
        s_fg = sem("s_fg")
        s_ftp = sem("s_ftp")
        s_fe = sem("s_fe")
        s_fa = sem("s_fa")
        s_fea = sem("s_fea")
        s_fl = sem("s_fl")
        s_fmsg = sem("s_fmsg")
        s_fhi = sem("s_fhi")
        s_frest = sem("s_frest")
        s_fmid = sem("s_fmid")
        s_flow = sem("s_flow")
        s_fsame = sem("s_fsame")
        s_fsidx = sem("s_fsidx")
        s_fm = sem("s_fm")
        s_ftot = sem("s_ftot")
        s_fsc = sem("s_fsc")
        exp_f = gsq[:, 0:GT, :]
        abs_c = gsq[:, GT:2 * GT, :]
        exp_c = gx[:, 0, 0:GT, :]
        log_c = gx[:, 0, GT:2 * GT, :]
        one_f = gh[:, 0:GT, :]
        sig_f = gh[:, GT:2 * GT, :]
        soft_c = gc[:, 0:GT, :]
        halves = [bank[b][:, :].rearrange("p (j e) -> p j e", e=P) for b in range(2)]

        def gates_sync(sp):
            def load(u, b, g):
                await_(sp, s_fsame, g - 1)
                sp.dma_start(krow[:, b, :], key_src[bass.ds(g * GROUP, GROUP)].partition_broadcast(P)).then_inc(s_fi[b], 16)

            sp.wait_ge(s_esame, GROUPS)
            load(0, 0, 0)
            load(0, 1, 1)
            with sp.Fori(1, GROUPS // 2) as u:
                for b in range(2):
                    load(u, b, u * 2 + b)
            load(GROUPS // 2, 0, GROUPS - 1)

        def gates_gpsimd(pool):
            def scatter(b, g):
                pool.wait_ge(s_ftot, g + 1)
                pool.wait_ge(s_fsidx, g + 1)
                await_(pool, s_fsc, 64 * g)
                pool.sem_inc(s_step, 1)
                for k in range(GT):
                    pool.indirect_dma_start(nsum, bass.IndirectOffsetOnAxis(sidx[:, b, k:k + 1], 0),
                                            gtot[:, b, k, :], None, compute_op=ALU.add).then_inc(s_fsc, 16)

            pool.wait_ge(s_znsum, 16 * (CHUNKS + 1))
            scatter(0, 0)
            scatter(1, 1)
            with pool.Fori(1, GROUPS // 2) as u:
                for b in range(2):
                    scatter(b, u * 2 + b)
            scatter(0, GROUPS - 1)

        def gates_vector(dve):
            ch = sem("s_gates_links")
            PER = 3

            def group(u, b, g):
                k = [0]

                def link(ins):
                    k[0] += 1
                    ins.then_inc(ch, 1)
                    dve.wait_ge(ch, g * PER + k[0])

                dve.wait_ge(s_fe, g + 1)
                link(nc.vector.tensor_scalar(one_f, exp_f, 1.0, None, ALU.add))
                link(nc.vector.reciprocal(sig_f, one_f))
                dve.wait_ge(s_fl, g + 1)
                link(nc.vector.scalar_tensor_tensor(out=soft_c, in0=halves[b][:, :, D:P], scalar=0.0, in1=log_c,
                                                    op0=ALU.max, op1=ALU.add))
                nc.vector.tensor_tensor(gmsg[:, :, :], soft_c, sig_f, ALU.mult).then_inc(s_fmsg, 1)
                dve.wait_ge(s_fi[b], 16 * (u + 1))
                await_(dve, s_fm, g - 1)
                for j in range(GT):
                    ins = nc.vector.tensor_scalar(same[:, b, j, :], krow[:, b, :], kcolf[:, 1, bass.ds(g * GT + j, 1)],
                                                  None, ALU.is_equal)
                ins.then_inc(s_fsame, 1)
                dve.wait_ge(s_fhi, g + 1)
                nc.vector.tensor_tensor(grest[:, :, :], gmsg[:, :, :], gparts[:, b, 0, :, :], ALU.subtract).then_inc(s_frest, 1)
                await_(dve, s_fsc, 64 * (g - 1))
                nc.vector.tensor_copy(sidx[:, b, :], sidx_src[:, bass.ds(g * GT, GT)]).then_inc(s_fsidx, 1)
                dve.wait_ge(s_fmid, g + 1)
                nc.vector.tensor_tensor(gparts[:, b, 2, :, :], grest[:, :, :], gparts[:, b, 1, :, :],
                                        ALU.subtract).then_inc(s_flow, 1)
                assert k[0] == PER

            group(0, 0, 0)
            group(0, 1, 1)
            with dve.Fori(1, GROUPS // 2) as u:
                for b in range(2):
                    group(u, b, u * 2 + b)
            group(GROUPS // 2, 0, GROUPS - 1)

        def gates_scalar(act):
            affs = [ght, ghid]

            def gate(b, g):
                await_(act, s_ftp, g - 1)
                nc.scalar.activation(affs[b][:, :], big[:, bass.ds(g * GROUP, GROUP)], ACT.Identity, bias=B1[:, :],
                                     scale=A1[:, :]).then_inc(s_fg, 1)

            def exps(b, g):
                act.wait_ge(s_ftp, g + 1)
                await_(act, s_fmsg, g)
                nc.scalar.activation(exp_f, halves[b][:, :, 0:D], ACT.Exp, scale=-1.0).then_inc(s_fe, 1)
                nc.scalar.activation(abs_c, halves[b][:, :, D:P], ACT.Abs).then_inc(s_fa, 1)

            def logs(g):
                act.wait_ge(s_fa, g + 1)
                nc.scalar.activation(exp_c, abs_c, ACT.Exp, scale=-1.0).then_inc(s_fea, 1)
                act.wait_ge(s_fea, g + 1)
                nc.scalar.activation(log_c, exp_c, ACT.Ln, bias=1.0).then_inc(s_fl, 1)

            def sums(b, g):
                act.wait_ge(s_fm, g + 1)
                await_(act, s_fsc, 64 * (g - 1))
                nc.scalar.copy(gtot[:, b, :, :], bank[3][:, 0:GT * D].rearrange("p (j d) -> p j d", d=D)).then_inc(s_ftot, 1)

            def group(u, b, g):
                if not known(g) or g + 2 < GROUPS:
                    gate(b, g + 2)
                act.wait_ge(s_fmsg, g + 1)
                await_(act, s_fm, g - 1)
                nc.scalar.copy(gparts[:, b, 0, :, :], gmsg[:, :, :]).then_inc(s_fhi, 1)
                if not known(g) or g + 1 < GROUPS:
                    exps(1 - b, g + 1)
                act.wait_ge(s_frest, g + 1)
                nc.scalar.copy(gparts[:, b, 1, :, :], grest[:, :, :]).then_inc(s_fmid, 1)
                if not known(g) or g + 1 < GROUPS:
                    logs(g + 1)
                if not known(g) or g > 0:
                    sums(1 - b, g - 1)

            nc.scalar.preload_act_table_set("natural_log_exp_and_others")
            act.wait_ge(s_es, GROUPS)
            act.wait_ge(s_norm, 1)
            gate(0, 0)
            gate(1, 1)
            exps(0, 0)
            logs(0)
            group(0, 0, 0)
            group(0, 1, 1)
            with act.Fori(1, GROUPS // 2 - 1) as u:
                for b in range(2):
                    group(u, b, u * 2 + b)
            for g in range(GROUPS - 3, GROUPS):
                group(g // 2, g % 2, g)
            sums(0, GROUPS - 1)

        def gates_tensor(pe):
            affs = [ght, ghid]

            def turn(b, g):
                pe.wait_ge(s_fg, g + 1)
                await_(pe, s_fmsg, g - 1)
                for j in range(GT):
                    ins = nc.tensor.transpose(bank[b][:, P * j:P * j + P], affs[b][:, P * j:P * j + P], ident[:, :])
                ins.then_inc(s_ftp, 1)

            def group(u, b, g):
                if not known(g) or g + 2 < GROUPS:
                    turn(b, g + 2)
                pe.wait_ge(s_flow, g + 1)
                pe.wait_ge(s_fsame, g + 1)
                await_(pe, s_ftot, g)
                for i in range(GT):
                    for j in range(GT):
                        for part in range(3):
                            ins = nc.tensor.matmul(bank[3][:, D * i:D * i + D], same[:, b, j, P * i:P * i + P],
                                                   gparts[:, b, part, j, :], start=(j == 0 and part == 0),
                                                   stop=(j == GT - 1 and part == 2))
                ins.then_inc(s_fm, 1)

            turn(0, 0)
            turn(1, 1)
            group(0, 0, 0)
            group(0, 1, 1)
            with pe.Fori(1, GROUPS // 2 - 1) as u:
                for b in range(2):
                    group(u, b, u * 2 + b)
            for g in range(GROUPS - 3, GROUPS):
                group(g // 2, g % 2, g)

        RING = 4
        s_vx = [sem(f"s_vx{r}") for r in range(RING)]
        s_vprod = sem("s_vprod")
        s_vprod2 = sem("s_vprod2")
        s_vacc = sem("s_vacc")
        s_vsq = sem("s_vsq")
        s_vm = sem("s_vm")
        s_vdiag = sem("s_vdiag")
        s_vrow = sem("s_vrow")
        s_vvar = sem("s_vvar")
        s_vsd = sem("s_vsd")
        s_vcoef = sem("s_vcoef")
        s_vcolp = sem("s_vcolp")
        s_vcols = sem("s_vcols")
        vin = [area(r) for r in range(RING)]
        vsq = [area(8), area(9)]
        vprod = [area(10), area(11)]
        vacc = area(12)
        vdiag = area(13)
        vw = [nst[:, 0, :], nst[:, 1, :]]
        POOL_J = 12
        HJ = J // 2
        assert CHUNKS % RING == 1

        def ring_chunks(eng, chunk):
            for g in range(RING):
                chunk(0, g, g)
            with eng.Fori(1, CHUNKS // RING) as u:
                for r in range(RING):
                    chunk(u, r, u * RING + r)
            chunk(CHUNKS // RING, 0, LAST)

        def moments_sync(sp):
            def load(u, r, g):
                await_(sp, s_vsq, g - RING + 1)
                await_(sp, s_vprod, g - RING + 1)
                await_(sp, s_vprod2, g - RING + 1)
                sp.dma_start(vin[r], chunk_rows(nsum, g)).then_inc(s_vx[r], 16)

            sp.wait_ge(s_fg, GROUPS)
            sp.wait_ge(s_fsc, 64 * GROUPS)
            ring_chunks(sp, load)

        def moments_gpsimd(pool):
            def product(u, r, g):
                pool.wait_ge(s_vx[r], 16 * (u + 1))
                await_(pool, s_vacc, g - 1)
                pool.sem_inc(s_step, 1)
                nc.gpsimd.tensor_tensor(vprod[r % 2][:, 0:POOL_J, :], vin[r][:, 0:POOL_J, :],
                                        bcj(nw[:, bass.ds(g * J, POOL_J)]), ALU.mult).then_inc(s_vprod, 1)

            ring_chunks(pool, product)

        def moments_scalar(act):
            def square(u, r, g):
                act.wait_ge(s_vx[r], 16 * (u + 1))
                await_(act, s_vm, g - 1)
                nc.scalar.activation(vsq[r % 2], vin[r], ACT.Square)
                nc.scalar.copy(vw[r % 2], nw[:, bass.ds(g * J, J)]).then_inc(s_vsq, 1)

            ring_chunks(act, square)
            act.wait_ge(s_vvar, 1)
            nc.scalar.activation(row_tmp[:, 2, :], row_tmp[:, 1, :], ACT.Sqrt, bias=eps_col[:, :]).then_inc(s_vsd, 1)

        def moments_vector(dve):
            def product(u, r, g):
                dve.wait_ge(s_vx[r], 16 * (u + 1))
                await_(dve, s_vacc, g - 1)
                nc.vector.tensor_tensor(vprod[r % 2][:, POOL_J:J, :], vin[r][:, POOL_J:J, :],
                                        bcj(nw[:, bass.ds(g * J + POOL_J, J - POOL_J)]), ALU.mult).then_inc(s_vprod2, 1)

            def add(b, g):
                dve.wait_ge(s_vprod, g + 1)
                dve.wait_ge(s_vprod2, g + 1)
                await_(dve, s_vacc, g)
                nc.vector.tensor_tensor(vacc, vacc, vprod[b], ALU.add).then_inc(s_vacc, 1)

            def chunk(u, r, g):
                product(u, r, g)
                if not known(g) or g > 0:
                    add((r + 1) % 2, g - 1)

            ch = sem("s_moments_links")
            k = [0]

            def link(ins):
                k[0] += 1
                ins.then_inc(ch, 1)
                dve.wait_ge(ch, k[0])

            link(nc.vector.memset(vacc, 0.0))
            ring_chunks(dve, chunk)
            add(0, LAST)

            dve.wait_ge(s_vm, CHUNKS)
            for h in range(2):
                ins = nc.vector.tensor_tensor(
                    vdiag[0:J, h * HJ:h * HJ + HJ, :], bank[h][0:J, :].rearrange("p (j d) -> p j d", d=D),
                    ident[0:J, h * HJ:h * HJ + HJ].rearrange("p (j o) -> p j o", o=1).to_broadcast([J, HJ, D]), ALU.mult)
            ins.then_inc(s_vdiag, 1)
            dve.wait_ge(s_vrow, 2)
            for i in range(2):
                link(nc.vector.reduce_sum(row_tmp[:, 2 + i, :], bank[2 + i][:, :].rearrange("p (j d) -> p d j", d=D), X))
                link(nc.vector.tensor_scalar(row_tmp[:, i, :], row_tmp[:, 2 + i, :], wsum_inv[:, 1:2], None, ALU.mult))
            link(nc.vector.tensor_tensor(row_tmp[:, 3, :], row_tmp[:, 0, :], row_tmp[:, 0, :], ALU.mult))
            link(nc.vector.tensor_tensor(row_tmp[:, 1, :], row_tmp[:, 1, :], row_tmp[:, 3, :], ALU.subtract))
            nc.vector.tensor_scalar(row_tmp[:, 1, :], row_tmp[:, 1, :], 0.0, None, ALU.max).then_inc(s_vvar, 1)
            dve.wait_ge(s_vsd, 1)
            link(nc.vector.reciprocal(row_tmp[:, 3, :], row_tmp[:, 2, :]))
            link(nc.vector.tensor_tensor(A2[:, 0, :], g2r[:, :], row_tmp[:, 3, :], ALU.mult))
            link(nc.vector.tensor_tensor(row_tmp[:, 1, :], A2[:, 0, :], row_tmp[:, 0, :], ALU.mult))
            link(nc.vector.tensor_tensor(B2[:, 0, :], b2r[:, :], row_tmp[:, 1, :], ALU.subtract))
            nc.vector.tensor_copy(A2[:, 1, :], A2[:, 0, :])
            nc.vector.tensor_copy(B2[:, 1, :], B2[:, 0, :]).then_inc(s_vcoef, 1)
            dve.wait_ge(s_vcolp, 1)
            for i in range(2):
                nc.vector.tensor_copy(coef[:, i:i + 1], bank[4 + i][:, 0:1]).then_inc(s_vcols, 1)

        def moments_tensor(pe):
            def weigh(u, r, g):
                pe.wait_ge(s_vsq, g + 1)
                for h in range(2):
                    ins = nc.tensor.matmul(bank[h][0:J, :], vw[r % 2],
                                           vsq[r % 2][:, h * HJ:h * HJ + HJ, :].rearrange("p j d -> p (j d)"),
                                           start=known(g) and g == 0, stop=known(g) and g == LAST)
                ins.then_inc(s_vm, 1)

            ring_chunks(pe, weigh)
            pe.wait_ge(s_ftot, GROUPS)
            pe.wait_ge(s_vacc, CHUNKS)
            for h in range(2):
                ins = nc.tensor.matmul(bank[2][:, :], ones[:, :],
                                       vacc[:, h * HJ:h * HJ + HJ, :].rearrange("p j d -> p (j d)"),
                                       start=h == 0, stop=h == 1)
            ins.then_inc(s_vrow, 1)
            pe.wait_ge(s_vdiag, 1)
            for h in range(2):
                ins = nc.tensor.matmul(bank[3][:, :], ones[0:J, :],
                                       vdiag[0:J, h * HJ:h * HJ + HJ, :].rearrange("p j d -> p (j d)"),
                                       start=h == 0, stop=h == 1)
            ins.then_inc(s_vrow, 1)
            pe.wait_ge(s_vcoef, 1)
            for i, c in enumerate((A2, B2)):
                ins = nc.tensor.transpose(bank[4 + i][:, 0:P], c[:, :, :].rearrange("p a d -> p (a d)"), ident[:, :])
            ins.then_inc(s_vcolp, 1)

        s_oc = [sem(f"s_oc{b}") for b in range(2)]
        s_on = [sem(f"s_on{b}") for b in range(2)]
        s_oturn = sem("s_oturn")
        s_oaff = sem("s_oaff")
        s_oback = sem("s_oback")
        s_oh = sem("s_oh")
        s_oz = sem("s_oz")
        s_oabs = sem("s_oabs")
        s_oexp = sem("s_oexp")
        s_olog = sem("s_olog")
        s_osp = sem("s_osp")
        s_ox1 = sem("s_ox1")
        s_oo = sem("s_oo")
        s_ost = [sem(f"s_ost{b}") for b in range(2)]
        cin = [area(0), area(1)]
        sin = [area(2), area(3)]
        aff = [area(4, (HJ, D)), area(5, (HJ, D))]
        oh = [area(6), area(7)]
        oz = [area(8), area(9)]
        oabs = area(10)
        oexp = area(11)
        ol = [area(12), area(13)]
        ox1 = [area(14), area(15)]
        osp = [area(16), area(17)]
        oo = [area(18), area(19)]
        half = lambda ap, q: ap[:, q * HJ:q * HJ + HJ, :]
        OUT_DVE = 3
        s_oov = sem("s_oov")
        pairs = HJ // 2

        def output_sync(sp):
            def load_c(b, g):
                await_(sp, s_ox1, g - 1)
                await_(sp, s_oh, g - 1)
                sp.dma_start(cin[b], chunk_rows(ctab, g)).then_inc(s_oc[b], 16)

            def load_n(b, g):
                await_(sp, s_oturn, 2 * (g - 1))
                sp.dma_start(sin[b], chunk_rows(nsum, g)).then_inc(s_on[b], 16)

            def store(b, g):
                sp.wait_ge(s_oo, g + 1)
                sp.wait_ge(s_oov, g + 1)
                sp.dma_start(chunk_rows(out, g), oo[b]).then_inc(s_ost[b], 16)

            def period(u, b, g):
                if has(g + 2):
                    load_c(b, g + 2)
                if has(g + 3):
                    load_n(1 - b, g + 3)
                if has(g - 1):
                    store(1 - b, g - 1)

            sp.wait_ge(s_vprod, CHUNKS)
            sp.wait_ge(s_vprod2, CHUNKS)
            sp.wait_ge(s_vm, CHUNKS)
            load_n(0, 0)
            load_n(1, 1)
            load_c(0, 0)
            load_c(1, 1)
            load_n(0, 2)
            periods(sp, period)
            store(0, LAST)
            sp.wait_ge(s_ost[0], 16 * (CHUNKS // 2 + 1))
            sp.wait_ge(s_ost[1], 16 * (CHUNKS // 2))

        def output_gpsimd(pool):
            def x1(u, b, g):
                pool.wait_ge(s_oc[b], 16 * (u + 1))
                await_(pool, s_oo, g - 1)
                await_(pool, s_oov, g - 1)
                pool.sem_inc(s_step, 1)
                nc.gpsimd.tensor_tensor(ox1[b], cin[b], bcj(m1[:, bass.ds(g * J, J)]), ALU.add).then_inc(s_ox1, 1)

            def total(u, b, g):
                pool.wait_ge(s_osp, g + 1)
                pool.wait_ge(s_ox1, g + 1)
                await_(pool, s_ost[b], 16 * u)
                nc.gpsimd.tensor_tensor(oo[b][:, OUT_DVE:J, :], osp[b][:, OUT_DVE:J, :], ox1[b][:, OUT_DVE:J, :],
                                        ALU.add).then_inc(s_oo, 1)

            def period(u, b, g):
                x1(u, b, g)
                if has(g - 1):
                    total(u - 1 + b, 1 - b, g - 1)

            periods(pool, period)
            total(CHUNKS // 2, 0, LAST)

        def output_vector(dve):
            def h(u, b, g):
                dve.wait_ge(s_oc[b], 16 * (u + 1))
                await_(dve, s_oz, 2 * (g - 1))
                nc.vector.scalar_tensor_tensor(out=oh[b], in0=cin[b], scalar=0.0, in1=bcj(r1[:, bass.ds(g * J, J)]),
                                               op0=ALU.max, op1=ALU.mult).then_inc(s_oh, 1)

            def argument(b, g):
                for q in range(2):
                    dve.wait_ge(s_oback, 2 * g + q + 1)
                    if q == 0:
                        dve.wait_ge(s_oh, g + 1)
                        await_(dve, s_oabs, g - 1)
                        await_(dve, s_osp, g - 1)
                    nc.vector.tensor_tensor(half(oz[b], q), bank[2 + 2 * b + q][:, :].rearrange("p (j d) -> p j d", d=D),
                                            half(oh[b], q), ALU.add).then_inc(s_oz, 1)

            def softplus(b, g):
                dve.wait_ge(s_olog, g + 1)
                await_(dve, s_oo, g - 1)
                await_(dve, s_oov, g - 1)
                nc.vector.scalar_tensor_tensor(out=osp[b], in0=oz[b], scalar=0.0, in1=ol[b], op0=ALU.max,
                                               op1=ALU.add).then_inc(s_osp, 1)

            def total(u, b, g):
                dve.wait_ge(s_osp, g + 1)
                dve.wait_ge(s_ox1, g + 1)
                await_(dve, s_ost[b], 16 * u)
                nc.vector.tensor_tensor(oo[b][:, 0:OUT_DVE, :], osp[b][:, 0:OUT_DVE, :], ox1[b][:, 0:OUT_DVE, :],
                                        ALU.add).then_inc(s_oov, 1)

            def period(u, b, g):
                if has(g - 1):
                    softplus(1 - b, g - 1)
                if has(g + 1):
                    h(u + b, 1 - b, g + 1)
                    argument(1 - b, g + 1)
                if has(g - 1):
                    total(u - 1 + b, 1 - b, g - 1)

            h(0, 0, 0)
            argument(0, 0)
            periods(dve, period)
            softplus(0, LAST)
            total(CHUNKS // 2, 0, LAST)

        def output_scalar(act):
            def affine(g, q):
                act.wait_ge(s_oturn, 2 * g + q + 1)
                await_(act, s_oback, 2 * (g - 1) + q + 1)
                nc.scalar.activation(aff[q].rearrange("p j d -> p (j d)"), bank[q][:, :], ACT.Identity,
                                     bias=coef[:, 1:2], scale=coef[:, 0:1]).then_inc(s_oaff, 1)

            def period(u, b, g):
                if has(g + 1):
                    affine(g + 1, 0)
                act.wait_ge(s_oz, 2 * (g + 1))
                await_(act, s_oexp, g)
                nc.scalar.activation(oabs, oz[b], ACT.Abs).then_inc(s_oabs, 1)
                if has(g + 1):
                    affine(g + 1, 1)
                act.wait_ge(s_oabs, g + 1)
                await_(act, s_olog, g)
                nc.scalar.activation(oexp, oabs, ACT.Exp, scale=-1.0).then_inc(s_oexp, 1)
                act.wait_ge(s_oexp, g + 1)
                await_(act, s_osp, g - 1)
                nc.scalar.activation(ol[b], oexp, ACT.Ln, bias=1.0).then_inc(s_olog, 1)

            nc.scalar.preload_act_table_set("natural_log_exp_and_others")
            act.wait_ge(s_vcols, 2)
            affine(0, 0)
            affine(0, 1)
            periods(act, period)

        def output_tensor(pe):
            def turn(u, b, g):
                pe.wait_ge(s_on[b], 16 * (u + 1))
                for q in range(2):
                    await_(pe, s_oaff, 2 * (g - 1) + q + 1)
                    for i in range(pairs):
                        j = q * HJ + 2 * i
                        ins = nc.tensor.transpose(bank[q][:, P * i:P * i + P],
                                                  sin[b][:, j:j + 2, :].rearrange("p a d -> p (a d)"), ident[:, :])
                    ins.then_inc(s_oturn, 1)

            def back(b, g, q):
                pe.wait_ge(s_oaff, 2 * g + q + 1)
                await_(pe, s_oz, 2 * (g - 2) + q + 1)
                for i in range(pairs):
                    ins = nc.tensor.transpose(bank[2 + 2 * b + q][:, P * i:P * i + P],
                                              aff[q][:, 2 * i:2 * i + 2, :].rearrange("p a d -> p (a d)"), ident[:, :])
                ins.then_inc(s_oback, 1)

            def period(u, b, g):
                if has(g + 1):
                    back(1 - b, g + 1, 0)
                    back(1 - b, g + 1, 1)
                if has(g + 2):
                    turn(u + 1, b, g + 2)

            turn(0, 0, 0)
            back(0, 0, 0)
            back(0, 0, 1)
            turn(0, 1, 1)
            periods(pe, period)

        with nc.Block() as block:
            @block.sync
            def _(sp):
                edges0_first(sp)
                setup_sync(sp)
                edges0_sync(sp)
                nodes0_sync(sp)
                edges1_sync(sp)
                gates_sync(sp)
                moments_sync(sp)
                output_sync(sp)

            @block.gpsimd
            def _(pool):
                setup_gpsimd(pool)
                edges0_gpsimd(pool)
                nodes0_gpsimd(pool)
                edges1_gpsimd(pool)
                gates_gpsimd(pool)
                moments_gpsimd(pool)
                output_gpsimd(pool)

            @block.vector
            def _(dve):
                setup_vector(dve)
                edges0_vector(dve)
                nodes0_vector(dve)
                edges1_vector(dve)
                norm1_vector(dve)
                gates_vector(dve)
                moments_vector(dve)
                output_vector(dve)

            @block.scalar
            def _(act):
                setup_scalar(act)
                edges0_scalar(act)
                nodes0_scalar(act)
                edges1_scalar(act)
                norm1_scalar(act)
                gates_scalar(act)
                moments_scalar(act)
                output_scalar(act)

            @block.tensor
            def _(pe):
                setup_tensor(pe)
                edges0_tensor(pe)
                nodes0_tensor(pe)
                edges1_tensor(pe)
                gates_tensor(pe)
                moments_tensor(pe)
                output_tensor(pe)


_WEIGHTS = {"mW1": "L0_gnn_mW1", "mb1": "L0_gnn_mb1", "mW2": "L0_gnn_mW2", "mb2": "L0_gnn_mb2",
            "uW1": "L0_gnn_uW1", "ub1": "L0_gnn_ub1", "uW2": "L0_gnn_uW2", "ub2": "L0_gnn_ub2",
            "W": "L1_gnn_W", "b": "L1_gnn_b", "g1": "L1_gnn_g1", "b1": "L1_gnn_b1", "g2": "L1_gnn_g2",
            "b2": "L1_gnn_b2"}


def kernel(**inputs):
    import numpy as np
    import concourse.bacc as bacc
    from concourse.bass_utils import run_bass_kernel_spmd

    a = {k: np.asarray(v) for k, v in inputs.items()}

    def padded(v, rows, fill=None):
        more = np.zeros((rows - v.shape[0],) + v.shape[1:], v.dtype)
        if fill is not None:
            more[:] = fill
        return np.concatenate([v, more])

    x = padded(a["x"], NP)
    pad_rows = np.arange(NP + GROUP, ROWS)
    key_src, key_dst = padded(a["src"], EP, pad_rows), padded(a["dst"], EP, pad_rows)
    cols = lambda v: np.ascontiguousarray(v.reshape(TILES, P).T)
    ends = [padded(a[k], EP).reshape(GROUPS, GT, P) for k in ("src", "dst")]
    arrays = {
        "x": x,
        "gat": np.ascontiguousarray(np.stack(ends, axis=-1).transpose(0, 2, 1, 3).reshape(GROUPS, P, 2 * GT)),
        "key_cols": np.ascontiguousarray(np.stack([cols(key_dst), cols(key_src)], axis=1)),
        "key_src": key_src,
        "key_dst": key_dst,
        "ea32_t": np.ascontiguousarray(padded(a["edge_attr_32"], EP).T),
        "ea64_t": np.ascontiguousarray(padded(a["edge_attr_64"], EP).T),
        "edge_w": padded(a["edge_weight"], EP),
        "edge_w_cols": cols(padded(a["edge_weight"], EP)),
        "node_w": np.ascontiguousarray(
            padded(a["node_vec"], NP).reshape(CHUNKS, P, J).transpose(1, 0, 2).reshape(P, CHUNKS * J)),
    }
    nc = bacc.Bacc("TRN2", target_bir_lowering=False, num_devices=1)

    def given(name, v):
        return nc.dram_tensor(name, v.shape, mybir.dt.from_np(v.dtype), kind="ExternalInput").ap()

    aps = {k: given(k, v) for k, v in arrays.items()}
    weights = {}
    for short, name in _WEIGHTS.items():
        arrays[f"w_{short}"] = np.ascontiguousarray(a[name])
        weights[short] = given(f"w_{short}", arrays[f"w_{short}"])
    out = nc.dram_tensor("out", [NP, D], F32, kind="ExternalOutput").ap()
    build(nc, **aps, weights=weights, out=out)
    r = run_bass_kernel_spmd(nc, [arrays], core_ids=[0])
    return r.results[0]["out"][:N]
```
